# Optimizing a Trainium2 kernel written in Bass

```python
import numpy as np
import jax
import jax.numpy as jnp

def _softmax(x, axis=-1):
    return jax.nn.softmax(x, axis=axis)

def _gelu(x):
    return jax.nn.gelu(x, approximate=True)

def _silu(x):
    return jax.nn.silu(x)

def _sigmoid(x):
    return jax.nn.sigmoid(x)

def _layernorm(x, axis=-1, eps=1e-05):
    m = jnp.mean(x, axis=axis, keepdims=True)
    v = jnp.var(x, axis=axis, keepdims=True)
    return (x - m) / jnp.sqrt(v + eps)

def _scatter_add(tgt, idx, src, axis=0):
    return tgt.at[idx].add(src)

def _segment_sum(src, seg, n):
    return jax.ops.segment_sum(src, seg, n)
kernel_name = 'mk_seq_postln_d2_jaxref_r8_69c835'

def setup_inputs(seed: int=0):
    np.random.seed(seed)
    _w = jnp.asarray

    def _L0_attn_setup():
        import jax, jax.numpy as jnp
        import numpy as np
        import math
        D_MODEL = 256
        N_HEADS = 16
        D_HEAD = 128
        BATCH = 2
        SEQ = 256
        key = jax.random.key(seed)
        ks = jax.random.split(key, 5)
        std = 0.02
        x = jax.random.normal(ks[0], (BATCH, SEQ, D_MODEL), dtype=jnp.float32)
        W_Q = std * jax.random.normal(ks[1], (N_HEADS, D_HEAD, D_MODEL), dtype=jnp.float32)
        W_K = std * jax.random.normal(ks[2], (N_HEADS, D_HEAD, D_MODEL), dtype=jnp.float32)
        W_V = std * jax.random.normal(ks[3], (N_HEADS, D_HEAD, D_MODEL), dtype=jnp.float32)
        W_O = std * jax.random.normal(ks[4], (N_HEADS, D_MODEL, D_HEAD), dtype=jnp.float32)
        return {'x': x, 'W_Q': W_Q, 'W_K': W_K, 'W_V': W_V, 'W_O': W_O}
    _L0_attn_in = _L0_attn_setup()

    def _L0_ffn_setup():
        import jax, jax.numpy as jnp
        import numpy as np
        HID = 256
        N_EXP = 32
        F_EXP = 96
        TOP_K = 6
        F_SH = 192
        B, S = (1, 128)
        key = jax.random.key(seed)
        ks = jax.random.split(key, 8)
        s = 0.02
        return {'hidden_states': jax.random.normal(ks[0], (B, S, HID), dtype=jnp.float32), 'gate_w': jax.random.normal(ks[1], (HID, N_EXP), dtype=jnp.float32) * s, 'wg': jax.random.normal(ks[2], (N_EXP, HID, F_EXP), dtype=jnp.float32) * s, 'wu': jax.random.normal(ks[3], (N_EXP, HID, F_EXP), dtype=jnp.float32) * s, 'wd': jax.random.normal(ks[4], (N_EXP, F_EXP, HID), dtype=jnp.float32) * s, 'sg': jax.random.normal(ks[5], (HID, F_SH), dtype=jnp.float32) * s, 'su': jax.random.normal(ks[6], (HID, F_SH), dtype=jnp.float32) * s, 'sd': jax.random.normal(ks[7], (F_SH, HID), dtype=jnp.float32) * s}
    _L0_ffn_in = _L0_ffn_setup()

    def _L1_attn_setup():
        import jax, jax.numpy as jnp
        import numpy as np
        B_, S, H = (2, 256, 256)
        E = 2 * H
        P = 64
        NH = E // P
        N = 64
        G = 1
        K = 4
        CS = 32
        CONV_DIM = E + 2 * G * N
        PROJ = E + CONV_DIM + NH
        EPS = 1e-06

        def segment_sum(a):
            l = a.shape[-1]
            a_exp = jnp.broadcast_to(a[..., None], (*a.shape, l))
            a_exp = jnp.where(jnp.tril(jnp.ones((l, l), bool), -1), a_exp, 0.0)
            s = jnp.cumsum(a_exp, axis=-2)
            return jnp.where(jnp.tril(jnp.ones((l, l), bool), 0), s, -jnp.inf)
        key = jax.random.key(seed)
        ks = jax.random.split(key, 8)
        s = 0.02
        return {'x': jax.random.normal(ks[0], (B_, S, H), jnp.float32), 'in_proj_w': jax.random.normal(ks[1], (PROJ, H), jnp.float32) * s, 'conv_w': jax.random.normal(ks[2], (CONV_DIM, K), jnp.float32) * s, 'conv_b': jnp.zeros((CONV_DIM,), jnp.float32), 'dt_bias': jax.random.uniform(ks[3], (NH,), jnp.float32, 0.0, 1.0), 'A_log': jnp.log(jax.random.uniform(ks[4], (NH,), jnp.float32, 1.0, 16.0)), 'D': jnp.ones((NH,), jnp.float32), 'norm_w': jnp.ones((E,), jnp.float32), 'out_proj_w': jax.random.normal(ks[5], (H, E), jnp.float32) * s}
    _L1_attn_in = _L1_attn_setup()

    def _L1_ffn_setup():
        import jax, jax.numpy as jnp
        import numpy as np
        H = 256
        I = 176
        E = 16
        G = 4
        TOPK_GROUP = 2
        K = 4
        SI = 2 * I
        SCALE = 1.0
        NORM = True
        B, S = (4, 64)

        def _swiglu(h):
            g, u = jnp.split(h, 2, axis=-1)
            return jax.nn.silu(g) * u

        def _combine_weights(xt, gate_w):
            T = xt.shape[0]
            scores = jax.nn.softmax(xt @ gate_w.T, axis=-1)
            group_scores = scores.reshape(T, G, E // G).max(axis=-1)
            _, gidx = jax.lax.top_k(group_scores, TOPK_GROUP)
            gmask = jnp.zeros((T, G), bool).at[jnp.arange(T)[:, None], gidx].set(True)
            emask = jnp.repeat(gmask, E // G, axis=1)
            masked = jnp.where(emask, scores, 0.0)
            w, eidx = jax.lax.top_k(masked, K)
            if NORM:
                w = w / (w.sum(-1, keepdims=True) + 1e-20)
            w = w * SCALE
            return jnp.zeros((T, E), xt.dtype).at[jnp.arange(T)[:, None], eidx].add(w)
        key = jax.random.key(seed)
        ks = jax.random.split(key, 6)
        sc = lambda fan_in: 1.0 / np.sqrt(fan_in)
        return {'x': jax.random.normal(ks[0], (B, S, H), jnp.float32), 'gate_w': jax.random.normal(ks[1], (E, H), jnp.float32) * sc(H), 'expert_up_w': jax.random.normal(ks[2], (E, 2 * I, H), jnp.float32) * sc(H), 'expert_down_w': jax.random.normal(ks[3], (E, H, I), jnp.float32) * sc(I), 'shared_up_w': jax.random.normal(ks[4], (2 * SI, H), jnp.float32) * sc(H), 'shared_down_w': jax.random.normal(ks[5], (H, SI), jnp.float32) * sc(SI)}
    _L1_ffn_in = _L1_ffn_setup()
    _d = {'L0_attn_x': _L0_attn_in['x'], 'L0_attn_W_Q': _L0_attn_in['W_Q'], 'L0_attn_W_K': _L0_attn_in['W_K'], 'L0_attn_W_V': _L0_attn_in['W_V'], 'L0_attn_W_O': _L0_attn_in['W_O'], 'L0_ffn_gate_w': _L0_ffn_in['gate_w'], 'L0_ffn_wg': _L0_ffn_in['wg'], 'L0_ffn_wu': _L0_ffn_in['wu'], 'L0_ffn_wd': _L0_ffn_in['wd'], 'L0_ffn_sg': _L0_ffn_in['sg'], 'L0_ffn_su': _L0_ffn_in['su'], 'L0_ffn_sd': _L0_ffn_in['sd'], 'L1_attn_in_proj_w': _L1_attn_in['in_proj_w'], 'L1_attn_conv_w': _L1_attn_in['conv_w'], 'L1_attn_conv_b': _L1_attn_in['conv_b'], 'L1_attn_dt_bias': _L1_attn_in['dt_bias'], 'L1_attn_A_log': _L1_attn_in['A_log'], 'L1_attn_D': _L1_attn_in['D'], 'L1_attn_norm_w': _L1_attn_in['norm_w'], 'L1_attn_out_proj_w': _L1_attn_in['out_proj_w'], 'L1_ffn_gate_w': _L1_ffn_in['gate_w'], 'L1_ffn_expert_up_w': _L1_ffn_in['expert_up_w'], 'L1_ffn_expert_down_w': _L1_ffn_in['expert_down_w'], 'L1_ffn_shared_up_w': _L1_ffn_in['shared_up_w'], 'L1_ffn_shared_down_w': _L1_ffn_in['shared_down_w']}
    _x0 = _d['L0_attn_x']
    _d['L0_attn_x'] = jax.random.normal(jax.random.fold_in(jax.random.key(seed), 1), (8, 256, 256), dtype=_x0.dtype)
    del _x0
    return _d

def reference(L0_attn_x, L0_attn_W_Q, L0_attn_W_K, L0_attn_W_V, L0_attn_W_O, L0_ffn_gate_w, L0_ffn_wg, L0_ffn_wu, L0_ffn_wd, L0_ffn_sg, L0_ffn_su, L0_ffn_sd, L1_attn_in_proj_w, L1_attn_conv_w, L1_attn_conv_b, L1_attn_dt_bias, L1_attn_A_log, L1_attn_D, L1_attn_norm_w, L1_attn_out_proj_w, L1_ffn_gate_w, L1_ffn_expert_up_w, L1_ffn_expert_down_w, L1_ffn_shared_up_w, L1_ffn_shared_down_w):

    def _L0_attn_ref(x, W_Q, W_K, W_V, W_O):
        import jax, jax.numpy as jnp
        import numpy as np
        import math
        D_MODEL = 256
        N_HEADS = 16
        D_HEAD = 128
        BATCH = 2
        SEQ = 256
        d_head = W_Q.shape[1]
        seq_len = x.shape[1]
        scale = 1.0 / math.sqrt(d_head)
        q = jnp.einsum('bsd,hed->bhse', x, W_Q)
        k = jnp.einsum('bsd,hed->bhse', x, W_K)
        v = jnp.einsum('bsd,hed->bhse', x, W_V)
        scores = jnp.einsum('bhse,bhme->bhsm', q, k) * scale
        causal = jnp.triu(jnp.ones((seq_len, seq_len), dtype=bool), k=1)
        scores = jnp.where(causal, jnp.float32(-1000000000.0), scores)
        pattern = jax.nn.softmax(scores, axis=-1)
        z = jnp.einsum('bhsm,bhme->bhse', pattern, v)
        out = jnp.einsum('bhse,hde->bsd', z, W_O)
        return out

    def _L0_ffn_ref(hidden_states, gate_w, wg, wu, wd, sg, su, sd):
        import jax, jax.numpy as jnp
        import numpy as np
        HID = 256
        N_EXP = 32
        F_EXP = 96
        TOP_K = 6
        F_SH = 192
        B, S = (1, 128)
        orig_shape = hidden_states.shape
        x = hidden_states.reshape(-1, HID)
        scores = jax.nn.sigmoid(x @ gate_w)
        topk_w, topk_i = jax.lax.top_k(scores, TOP_K)
        topk_w = topk_w / (jnp.sum(topk_w, axis=-1, keepdims=True) + 1e-20)
        combine = jnp.sum(jax.nn.one_hot(topk_i, N_EXP, dtype=topk_w.dtype) * topk_w[..., None], axis=1)
        g = jnp.einsum('td,edf->tef', x, wg)
        u = jnp.einsum('td,edf->tef', x, wu)
        act = jax.nn.silu(g) * u
        routed = jnp.einsum('tef,efd,te->td', act, wd, combine)
        routed = routed.reshape(orig_shape)
        shared = jax.nn.silu(hidden_states @ sg) * (hidden_states @ su) @ sd
        return routed + shared

    def _L1_attn_ref(x, in_proj_w, conv_w, conv_b, dt_bias, A_log, D, norm_w, out_proj_w):
        import jax, jax.numpy as jnp
        import numpy as np
        B_, S, H = (2, 256, 256)
        E = 2 * H
        P = 64
        NH = E // P
        N = 64
        G = 1
        K = 4
        CS = 32
        CONV_DIM = E + 2 * G * N
        PROJ = E + CONV_DIM + NH
        EPS = 1e-06

        def segment_sum(a):
            l = a.shape[-1]
            a_exp = jnp.broadcast_to(a[..., None], (*a.shape, l))
            a_exp = jnp.where(jnp.tril(jnp.ones((l, l), bool), -1), a_exp, 0.0)
            s = jnp.cumsum(a_exp, axis=-2)
            return jnp.where(jnp.tril(jnp.ones((l, l), bool), 0), s, -jnp.inf)
        b, s, _ = x.shape
        proj = x @ in_proj_w.T
        gate, hBC, dt = jnp.split(proj, [E, E + CONV_DIM], axis=-1)
        xp = jnp.pad(hBC, ((0, 0), (K - 1, 0), (0, 0)))
        conv = sum((xp[:, k:k + s, :] * conv_w[:, k] for k in range(K))) + conv_b
        hBC = jax.nn.silu(conv)
        h, Bm, Cm = jnp.split(hBC, [E, E + G * N], axis=-1)
        dt = jax.nn.softplus(dt + dt_bias)
        A = -jnp.exp(A_log)
        h = h.reshape(b, s, NH, P)
        Bm = jnp.tile(Bm.reshape(b, s, G, N), (1, 1, NH // G, 1))
        Cm = jnp.tile(Cm.reshape(b, s, G, N), (1, 1, NH // G, 1))
        pad = -s % CS
        D_res = D[:, None] * jnp.pad(h, ((0, 0), (0, pad), (0, 0), (0, 0)))
        h = h * dt[..., None]
        A_d = A * dt

        def chunk(t):
            t = jnp.pad(t, ((0, 0), (0, pad)) + ((0, 0),) * (t.ndim - 2))
            return t.reshape(b, -1, CS, *t.shape[2:])
        hc, Ac, Bc, Cc = (chunk(h), chunk(A_d), chunk(Bm), chunk(Cm))
        Ac = jnp.transpose(Ac, (0, 3, 1, 2))
        A_cs = jnp.cumsum(Ac, axis=-1)
        L = jnp.exp(segment_sum(Ac))
        Gm = jnp.einsum('bclhn,bcshn->bclsh', Cc, Bc)
        M = Gm * jnp.transpose(L, (0, 2, 3, 4, 1))
        Y_diag = jnp.einsum('bclsh,bcshp->bclhp', M, hc)
        decay = jnp.exp(A_cs[..., -1:] - A_cs)
        Bdec = Bc * jnp.transpose(decay, (0, 2, 3, 1))[..., None]
        states = jnp.einsum('bclhn,bclhp->bchpn', Bdec, hc)
        states = jnp.concatenate([jnp.zeros_like(states[:, :1]), states], axis=1)
        A_last = jnp.pad(A_cs[..., -1], ((0, 0), (0, 0), (1, 0)))
        dchunk = jnp.transpose(jnp.exp(segment_sum(A_last)), (0, 3, 2, 1))
        new_states = jnp.einsum('bzjh,bzhpn->bjhpn', dchunk, states)
        states = new_states[:, :-1]
        sdo = jnp.exp(A_cs)
        Y_off = jnp.einsum('bclhn,bchpn->bclhp', Cc, states) * jnp.transpose(sdo, (0, 2, 3, 1))[..., None]
        y = (Y_diag + Y_off).reshape(b, -1, NH, P) + D_res
        y = y[:, :s].reshape(b, s, E)
        yf = y * jax.nn.silu(gate)
        var = jnp.mean(yf * yf, axis=-1, keepdims=True)
        yn = norm_w * (yf * jax.lax.rsqrt(var + EPS))
        return yn @ out_proj_w.T

    def _L1_ffn_ref(x, gate_w, expert_up_w, expert_down_w, shared_up_w, shared_down_w):
        import jax, jax.numpy as jnp
        import numpy as np
        H = 256
        I = 176
        E = 16
        G = 4
        TOPK_GROUP = 2
        K = 4
        SI = 2 * I
        SCALE = 1.0
        NORM = True
        B, S = (4, 64)

        def _swiglu(h):
            g, u = jnp.split(h, 2, axis=-1)
            return jax.nn.silu(g) * u

        def _combine_weights(xt, gate_w):
            T = xt.shape[0]
            scores = jax.nn.softmax(xt @ gate_w.T, axis=-1)
            group_scores = scores.reshape(T, G, E // G).max(axis=-1)
            _, gidx = jax.lax.top_k(group_scores, TOPK_GROUP)
            gmask = jnp.zeros((T, G), bool).at[jnp.arange(T)[:, None], gidx].set(True)
            emask = jnp.repeat(gmask, E // G, axis=1)
            masked = jnp.where(emask, scores, 0.0)
            w, eidx = jax.lax.top_k(masked, K)
            if NORM:
                w = w / (w.sum(-1, keepdims=True) + 1e-20)
            w = w * SCALE
            return jnp.zeros((T, E), xt.dtype).at[jnp.arange(T)[:, None], eidx].add(w)
        Bq, Sq, _ = x.shape
        xt = x.reshape(-1, H)
        cw = _combine_weights(xt, gate_w)
        out = jnp.zeros_like(xt)
        for e in range(E):
            a = _swiglu(xt @ expert_up_w[e].T)
            out = out + cw[:, e:e + 1] * (a @ expert_down_w[e].T)
        out = out + _swiglu(xt @ shared_up_w.T) @ shared_down_w.T
        return out.reshape(Bq, Sq, H)
    x = L0_attn_x
    x = _layernorm(x + _L0_attn_ref(x, L0_attn_W_Q, L0_attn_W_K, L0_attn_W_V, L0_attn_W_O), axis=-1)
    x = _layernorm(x + _L0_ffn_ref(x, L0_ffn_gate_w, L0_ffn_wg, L0_ffn_wu, L0_ffn_wd, L0_ffn_sg, L0_ffn_su, L0_ffn_sd), axis=-1)
    x = _layernorm(x + _L1_attn_ref(x, L1_attn_in_proj_w, L1_attn_conv_w, L1_attn_conv_b, L1_attn_dt_bias, L1_attn_A_log, L1_attn_D, L1_attn_norm_w, L1_attn_out_proj_w), axis=-1)
    x = _layernorm(x + _L1_ffn_ref(x, L1_ffn_gate_w, L1_ffn_expert_up_w, L1_ffn_expert_down_w, L1_ffn_shared_up_w, L1_ffn_shared_down_w), axis=-1)
    return x

_drawn_inputs = setup_inputs


def setup_inputs(seed=0):
    import zlib

    import numpy as np

    out = dict(_drawn_inputs(seed))
    spreads = {'L1_attn_conv_b': (0.0, 0.1), 'L1_attn_D': (1.0, 0.2), 'L1_attn_norm_w': (1.0, 0.2)}
    factors = {'L0_attn_W_Q': 4.271,
     'L0_attn_W_K': 4.769,
     'L0_ffn_gate_w': 4.82,
     'L0_ffn_wg': 3.934,
     'L0_ffn_wu': 4.467,
     'L0_ffn_wd': 4.152,
     'L1_attn_dt_bias': 5.722,
     'L1_attn_A_log': 8.0}
    for name, (base, spread) in spreads.items():
        noise = np.random.default_rng([zlib.crc32(name.encode()), seed]).standard_normal(out[name].shape)
        drawn = base * np.exp(spread * noise) if base else spread * noise
        out[name] = jnp.asarray(drawn.astype(out[name].dtype))
    for name, factor in factors.items():
        out[name] = (out[name] * factor).astype(out[name].dtype)
    return out
```

```python
from contextlib import ExitStack

import concourse.bass as bass
from concourse import mybir

F32 = mybir.dt.float32
F32R = mybir.dt.float32r
ALU = mybir.AluOpType
ACT = mybir.ActivationFunctionType
AX = mybir.AxisListType

P = 128
BATCH, SEQ, D = 8, 256, 256
T = BATCH * SEQ
TILES = T // P
DC = D // P
BANK = 512
LN_EPS = 1e-5

HEADS, DH = 16, 128
HG = 2
GROUPS = HEADS // HG
PAIRS = BATCH // 2
UNITS = PAIRS * HG * 2
JOBS = 2 * HG + 2
WQ, WK, WV, WO = 0, HG * DC * DH, 2 * HG * DC * DH, 3 * HG * DC * DH
WA = 3 * HG * DC * DH + HG * D
MASKED = -1e9 * DH ** 0.5
SCALE = DH ** -0.5

HALF = T // 2
CHUNKS = HALF // BANK
WG, WU, WD, WF = 0, DC * P, 2 * DC * P, 2 * DC * P + D
SEL = 40
OUT = -1e30
SENTINEL = -2e30
TAKEN = -3e30
L0 = dict(name="l0", experts=32, width=96, shared=192, top=6)
L1 = dict(name="l1", experts=16, width=176, shared=352, top=4, groups=4, top_groups=2)
for _l in (L0, L1):
    _l["hidden"] = _l["shared"] + _l["experts"] * _l["width"]
    _l["tiles"] = -(-_l["hidden"] // P)

E, NH, HP, NS, TAPS = 512, 8, 64, 64, 4
EJ = E // P
MJ = 2 * EJ + 3
CJ = EJ + 2
PT = 2 * SEQ
SSM_EPS = 1e-6


def program(nc, x_rows, x_cols, attn_w, l0_gate, l0_w, l1_gate, l1_w, in_w, ssm_cols, out_w, out):
    with ExitStack() as ctx:
        def sem(name):
            return ctx.enter_context(nc.semaphore(name))

        def dram(name, shape):
            return nc.dram_tensor(name, shape, F32, kind="Internal").ap()

        def hold(eng, semaphore, count):
            if not isinstance(count, int) or count > 0:
                eng.wait_ge(semaphore, count)
                eng.sem_inc(held, 1)

        held = sem("held")

        def wait(eng, semaphore, count):
            if not isinstance(count, int) or count > 0:
                eng.wait_ge(semaphore, count)

        class Region:

            def __init__(self, at):
                self.at = at

            def __call__(self, name, shape, dt=F32):
                size = 4
                for n in shape[1:]:
                    size *= n
                t = nc.alloc_sbuf_tensor_at(name, shape, dt, offset=self.at)
                self.at += -(-size // 64) * 64
                assert self.at <= 212000, (name, self.at)
                return t

        keep = Region(nc.sbuf_base + 64 - nc.sbuf_base % 64)
        ident = keep("ident", [P, P])
        causal = keep("causal", [P, 2 * P])
        x = keep("x", [P, TILES, D])
        xT_hi = keep("xT_hi", [P, DC, T], F32R)
        xT_lo = keep("xT_lo", [P, DC, T], F32R)
        stats = keep("stats", [P, TILES, 6])
        mv = keep("mv", [P, TILES, 2])
        var, rstd, rtmp = (keep(n, [P, TILES]) for n in ("var", "rstd", "rtmp"))
        psum = ctx.enter_context(nc.psum_tensor("psum", [P, 8, BANK], F32))

        x_loaded = sem("x_loaded")
        const_ready = sem("const_ready")

        r = Region(keep.at)
        xT_raw = r("xT_raw", [P, DC, T])
        aw_raw = r("aw_raw", [P, WA])
        aw_hi = r("aw_hi", [P, WA], F32R)
        aw_lo = r("aw_lo", [P, WA], F32R)
        qT_hi, qT_lo, kT_hi, kT_lo = (r(n, [P, 2, HG, 2 * SEQ], F32R) for n in ("qT_hi", "qT_lo", "kT_hi", "kT_lo"))
        v_hi, v_lo = (r(n, [P, 2, 2, 2 * HG * DH], F32R) for n in ("v_hi", "v_lo"))
        s_sb = r("s_sb", [P, 2, 3 * P])
        p_sb = r("p_sb", [P, 3, 3 * P])
        pT_hi, pT_lo = (r(n, [P, 2, 3 * P], F32R) for n in ("pT_hi", "pT_lo"))
        zT_hi, zT_lo = (r(n, [P, 2, SEQ], F32R) for n in ("zT_hi", "zT_lo"))
        neg_max, row_sum, row_inv = (r(n, [P, 3, 2]) for n in ("neg_max", "row_sum", "row_inv"))

        xT_loaded = [sem(f"xT_loaded{i}") for i in range(PAIRS)]
        xT_hi_ready, xT_lo_ready = sem("xT_hi_ready"), sem("xT_lo_ready")
        aw_loaded, aw_split, awo_split = sem("aw_loaded"), sem("aw_split"), sem("awo_split")
        aw_hi_done = sem("aw_hi_done")
        qkv_ready, qkv_hi, qkv_lo = sem("qkv_ready"), sem("qkv_hi"), sem("qkv_lo")
        s_ready, s_masked = sem("s_ready"), sem("s_masked")
        p_ready, r_ready, p_scaled = sem("p_ready"), sem("r_ready"), sem("p_scaled")
        pT_ready, pT_hi_ready, pT_lo_ready = sem("pT_ready"), sem("pT_hi_ready"), sem("pT_lo_ready")
        z_ready, z_hi_ready, z_lo_ready = sem("z_ready"), sem("z_hi_ready"), sem("z_lo_ready")
        o_ready, o_added = sem("o_ready"), sem("o_added")

        QKV_BANK, S_BANK, PT_BANK, Z_BANK, O_BANK = 0, 2, 4, 5, 6

        def passes(a_hi, a_lo, b_hi, b_lo):
            return ((a_hi, b_hi), (a_hi, b_lo), (a_lo, b_hi))

        def attn_schedule(next_group):
            lag_t, lag_v, lag_o = 2, 3, 4
            for i in range(UNITS + lag_o):
                jobs = []
                bp = i // (2 * HG)
                if i < UNITS - 2 * HG:
                    jobs = [(bp + 1, j) for j in ((0, 1), (2,), (3, 4), (5,))[i % 4]]
                elif i >= UNITS and next_group:
                    jobs = [(PAIRS, j) for j in ((0, 1), (2, 3), (4, 5), ())[i - UNITS]]
                yield i, jobs, i if i < UNITS else None, *(i - g if 0 <= i - g < UNITS else None for g in (lag_t, lag_v, lag_o))

        def unit(u):
            return u // (2 * HG), u % (2 * HG) // 2, u % 2

        ln_stat, ln_aggr, ln_var, ln_sqrt, ln_done = (sem(n) for n in ("ln_stat", "ln_aggr", "ln_var", "ln_sqrt", "ln_done"))
        ln_root = sem("ln_root")
        lnT_ready, lnT_hi, lnT_lo = sem("lnT_ready"), sem("lnT_hi"), sem("lnT_lo")
        stored = sem("stored")
        NORMS = 4
        LNT = DC * TILES // 4

        def inverse_root(root, value, tmp, done, base):
            dve = nc.vector
            dve.reciprocal(root, root).then_inc(done, 1)
            dve.wait_ge(done, base + 1)
            dve.tensor_tensor(tmp, root, root, ALU.mult).then_inc(done, 1)
            dve.wait_ge(done, base + 2)
            dve.tensor_tensor(tmp, tmp, value, ALU.mult).then_inc(done, 1)
            dve.wait_ge(done, base + 3)
            dve.tensor_scalar(tmp, tmp, -0.5, 1.5, ALU.mult, ALU.add).then_inc(done, 1)
            dve.wait_ge(done, base + 4)
            dve.tensor_tensor(root, root, tmp, ALU.mult).then_inc(done, 1)
            dve.wait_ge(done, base + ROOT_STEPS)

        ROOT_STEPS = 5

        def ln_vector(n, ready, count):
            dve = nc.vector
            dve.wait_ge(ready, count)
            for i in range(TILES):
                dve.bn_stats(stats[:, i, :], x[:, i, :]).then_inc(ln_stat, 1)
            for i in range(TILES):
                dve.wait_ge(ln_stat, n * TILES + i + 1)
                dve.bn_aggr(mv[:, i, :], stats[:, i, :]).then_inc(ln_aggr, 1)
            dve.wait_ge(ln_aggr, (n + 1) * TILES)
            dve.tensor_scalar(var[:], mv[:, :, 1], LN_EPS, None, ALU.add).then_inc(ln_var, 1)
            dve.wait_ge(ln_sqrt, n + 1)
            inverse_root(rstd[:], var[:], rtmp[:], ln_root, n * ROOT_STEPS)
            for i in range(TILES):
                dve.tensor_scalar(x[:, i, :], x[:, i, :], mv[:, i, 0:1], rstd[:, i:i + 1],
                                  ALU.subtract, ALU.mult).then_inc(ln_done, 1)

        def ln_lows(n):
            dve = nc.vector
            for b in range(LNT):
                c, q = b % DC, b // DC
                dve.wait_ge(lnT_hi, n * LNT + b + 1)
                dve.tensor_tensor(xT_lo[:, c, q * BANK:(q + 1) * BANK], psum[:, b, :],
                                  xT_hi[:, c, q * BANK:(q + 1) * BANK].bitcast(F32), ALU.subtract).then_inc(lnT_lo, 1)

        def ln_tensor(n):
            pe = nc.tensor
            if n == 0:
                pe.wait_ge(const_ready, 4)
            for b in range(LNT):
                c, q = b % DC, b // DC
                pe.wait_ge(ln_done, n * TILES + 4 * q + 4)
                for i in range(4):
                    last = pe.transpose(psum[:, b, i * P:(i + 1) * P], x[:, 4 * q + i, c * P:(c + 1) * P], ident[:])
                last.then_inc(lnT_ready, 1)

        def ln_scalar(n, transposed=True):
            act = nc.scalar
            act.wait_ge(ln_var, n + 1)
            act.activation(rstd[:], var[:], ACT.Sqrt).then_inc(ln_sqrt, 1)
            if not transposed:
                return
            for b in range(LNT):
                c, q = b % DC, b // DC
                act.wait_ge(lnT_ready, n * LNT + b + 1)
                act.activation(xT_hi[:, c, q * BANK:(q + 1) * BANK], psum[:, b, :], ACT.Copy).then_inc(lnT_hi, 1)

        def chain(out_ap, pairs, start=True, stop=True, **kw):
            for n, (w, m) in enumerate(pairs):
                last = nc.tensor.matmul(out_ap, w, m, start=start and n == 0, stop=stop and n == len(pairs) - 1, **kw)
            return last

        r = Region(keep.at)
        fw_raw = r("fw_raw", [P, 2, WF])
        fw_hi, fw_lo = r("fw_hi", [P, 2, WF], F32R), r("fw_lo", [P, 2, WF], F32R)
        comb = r("comb", [P, 2, HALF])
        gated, gated_comb, act_sb = r("gated", [P, 2, BANK]), r("gated_comb", [P, 2, BANK]), r("act_sb", [P, 2, BANK])
        act_hi, act_lo = r("act_hi", [P, 2, BANK], F32R), r("act_lo", [P, 2, BANK], F32R)
        yT = r("yT", [P, DC, HALF])
        gate_raw = r("gate_raw", [P, DC * 32])
        gate_hi, gate_lo = r("gate_hi", [P, DC * 32], F32R), r("gate_lo", [P, DC * 32], F32R)
        ones_row = r("ones_row", [1, T])
        logit, score, weight, comb_tok = (r(n, [P, TILES, 32]) for n in ("logit", "score", "weight", "comb_tok"))
        choice, chosen = r("choice", [P, TILES, SEL]), r("chosen", [P, TILES, SEL])
        top8, group_top8 = r("top8", [P, TILES, 8]), r("group_top8", [P, TILES, 8])
        row_stat = r("row_stat", [P, TILES])
        group_choice, group_chosen = r("group_choice", [P, TILES, 16]), r("group_chosen", [P, TILES, 16])
        combT = r("combT", [32, T])

        def signals(layer):
            names = ("gate_loaded gate_hi_done gate_split ones_ready ones_stored sentinels logits_ready score_ready shifted gate_step "
                     "comb_ready combT_ready combT_copied comb_stored w_hi_done gu_split d_split g_ready u_ready gated_ready "
                     "gated_comb_ready act_ready act_hi_ready act_lo_ready down_done y_copied yT_ready y_added").split()
            return dict({n: sem(f"{layer}_{n}") for n in names},
                        w_loaded=[sem(f"{layer}_w_loaded{i}") for i in range(2)],
                        comb_loaded=[sem(f"{layer}_comb_loaded{i}") for i in range(2)])

        expert_layers = [
            dict(**layer, norm=2 * i, w_dram=w, gate_dram=g, comb_dram=dram(f"comb_dram{i}", [layer["experts"] + 1, T]), **signals(f"l{i}"))
            for i, (layer, g, w) in enumerate(((L0, l0_gate, l0_w), (L1, l1_gate, l1_w)))]
        G_BANK, U_BANK, Y_BANK = 0, 2, 4

        def segments(f, j):
            cuts, row = [], lambda n: f["experts"] if n < f["shared"] or n >= f["hidden"] else (n - f["shared"]) // f["width"]
            for p in range(P):
                n = row(j * P + p)
                if cuts and cuts[-1][0] == n:
                    cuts[-1][2] = p + 1
                else:
                    cuts.append([n, p, p + 1])
            if len(cuts) == 1:
                cuts = [[cuts[0][0], 0, P // 2], [cuts[0][0], P // 2, P]]
            assert len(cuts) == 2
            return cuts

        def hidden_tiles(eng, f, body, tail):
            n = f["tiles"]
            pairs = (n - 1) // 2
            for h in range(2):
                for j in range(2):
                    body(h, j, h * n + j, (h * n + j) % 2, j == 0, False)
                with eng.Fori(1, pairs) as m:
                    for j in range(2):
                        body(h, 2 * m + j, 2 * m + j + h * n, (h * n + j) % 2, False, False)
                for j in range(2 * pairs, n):
                    body(h, j, h * n + j, (h * n + j) % 2, False, j == n - 1)
                tail(h)

        def experts_sync(f, free, count):
            sp = nc.sync
            sp.wait_ge(free, count)
            sp.dma_start(gate_raw[:, 0:DC * f["experts"]], f["gate_dram"].rearrange("p c e -> p (c e)")).then_inc(f["gate_loaded"], 16)
            sp.wait_ge(f["ones_ready"], 1)
            sp.dma_start(f["comb_dram"][f["experts"]:f["experts"] + 1, :], ones_row[:]).then_inc(f["ones_stored"], 16)
            stored_seen = False
            for n in range(2 * f["tiles"]):
                h, j = divmod(n, f["tiles"])
                if n >= 2:
                    sp.wait_ge(f["d_split"], n - 1)
                sp.dma_start(fw_raw[:, n % 2, :], f["w_dram"][j]).then_inc(f["w_loaded"][n % 2], 16)
                if n >= 2:
                    sp.wait_ge(f["gated_comb_ready"], CHUNKS * (n - 1))
                cuts = segments(f, j)
                if n == 0:
                    sp.wait_ge(f["ones_stored"], 16)
                if not stored_seen and any(row < f["experts"] for row, _, _ in cuts):
                    sp.wait_ge(f["combT_copied"], TILES // 4)
                    sp.dma_start(f["comb_dram"][0:f["experts"], :], combT[0:f["experts"], :]).then_inc(f["comb_stored"], 16)
                    sp.wait_ge(f["comb_stored"], 16)
                    stored_seen = True
                for row, p0, p1 in cuts:
                    sp.dma_start(comb[p0:p1, n % 2, :], f["comb_dram"][row, h * HALF:(h + 1) * HALF].partition_broadcast(p1 - p0)) \
                        .then_inc(f["comb_loaded"][n % 2], 16)

        def experts_pool(f, free, count):
            pool = nc.gpsimd
            pool.wait_ge(free, count)
            pool.memset(ones_row[:], 1.0).then_inc(f["ones_ready"], 1)
            pool.memset(choice[:], SENTINEL).then_inc(f["sentinels"], 1)
            pool.memset(group_choice[:], SENTINEL).then_inc(f["sentinels"], 1)
            pool.wait_ge(f["gate_loaded"], 16)
            cols = slice(0, DC * f["experts"])
            pool.tensor_copy(gate_hi[:, cols], gate_raw[:, cols]).then_inc(f["gate_hi_done"], 1)
            pool.wait_ge(f["gate_hi_done"], 1)
            pool.tensor_tensor(gate_lo[:, cols], gate_raw[:, cols], gate_hi[:, cols].bitcast(F32), ALU.subtract).then_inc(f["gate_split"], 1)

            def split(n, buf, part, done, steps):
                pool.tensor_copy(fw_hi[:, buf, part], fw_raw[:, buf, part]).then_inc(f["w_hi_done"], 1)
                pool.wait_ge(f["w_hi_done"], steps)
                pool.tensor_tensor(fw_lo[:, buf, part], fw_raw[:, buf, part], fw_hi[:, buf, part].bitcast(F32), ALU.subtract).then_inc(done, 1)

            def loads(n, buf):
                return (n - buf) * 8 + 16

            def tile(h, j, n, buf, first, last):
                for c in range(CHUNKS):
                    s = n * CHUNKS + c
                    if c == 0:
                        pool.wait_ge(f["comb_loaded"][buf], 2 * loads(n, buf))
                    if h or not first or c > 1:
                        pool.wait_ge(f["act_ready"], s - 1)
                    pool.wait_ge(f["gated_ready"], s + 1)
                    pool.tensor_tensor(gated_comb[:, c, :], gated[:, c, :], comb[:, buf, c * BANK:(c + 1) * BANK],
                                       ALU.mult).then_inc(f["gated_comb_ready"], 1)
                    if last and h == 1:
                        continue
                    if c == 0:
                        hold(pool, f["w_loaded"][1 - buf], loads(n + 1, 1 - buf))
                        split(n + 1, 1 - buf, slice(0, WD), f["gu_split"], 2 * n + 3)
                    elif c == 1:
                        split(n + 1, 1 - buf, slice(WD, WF), f["d_split"], 2 * n + 4)

            pool.wait_ge(f["w_loaded"][0], 16)
            split(0, 0, slice(0, WD), f["gu_split"], 1)
            split(0, 0, slice(WD, WF), f["d_split"], 2)
            hidden_tiles(pool, f, tile, lambda h: None)

        def experts_scalar(f):
            act = nc.scalar
            act.wait_ge(f["logits_ready"], 1)
            logits = psum[:, Y_BANK, 0:TILES * f["experts"]].rearrange("p (i e) -> p i e", e=f["experts"])
            if f["top"] == 6:
                act.activation(score[:, :, 0:f["experts"]], logits, ACT.Sigmoid).then_inc(f["score_ready"], 1)
            else:
                act.wait_ge(f["shifted"], 1)
                act.activation(score[:, :, 0:f["experts"]], weight[:, :, 0:f["experts"]], ACT.Exp).then_inc(f["score_ready"], 1)
            for b in range(TILES // 4):
                act.wait_ge(f["combT_ready"], b + 1)
                act.activation(combT[0:f["experts"], b * BANK:(b + 1) * BANK], psum[0:f["experts"], b, :], ACT.Copy).then_inc(f["combT_copied"], 1)

            def tile(h, j, n, buf, first, last):
                for c in range(CHUNKS):
                    s = n * CHUNKS + c
                    if h or not first:
                        act.wait_ge(f["gated_comb_ready"], s - 1)
                    act.wait_ge(f["g_ready"], s + 1)
                    act.activation(gated[:, c, :], psum[:, G_BANK + c, :], ACT.Silu).then_inc(f["gated_ready"], 1)
                    act.wait_ge(f["act_ready"], s + 1)
                    act.activation(act_hi[:, c, :], act_sb[:, c, :], ACT.Copy).then_inc(f["act_hi_ready"], 1)

            def tail(h):
                act.wait_ge(f["down_done"], (h + 1) * f["tiles"] * CHUNKS)
                for b in range(DC * CHUNKS):
                    d, c = divmod(b, CHUNKS)
                    if h:
                        act.wait_ge(f["yT_ready"], DC * CHUNKS)
                    act.activation(yT[:, d, c * BANK:(c + 1) * BANK], psum[:, Y_BANK + b, :], ACT.Copy).then_inc(f["y_copied"], 1)

            hidden_tiles(act, f, tile, tail)

        def experts_vector(f):
            dve = nc.vector
            steps = [0]

            def step(ins):
                steps[0] += 1
                ins.then_inc(f["gate_step"], 1)
                dve.wait_ge(f["gate_step"], steps[0])

            def per_row(t):
                return t.rearrange("p (i a) -> p i a", a=1)

            e = f["experts"]
            logits = psum[:, Y_BANK, 0:TILES * e].rearrange("p (i e) -> p i e", e=e)
            dve.wait_ge(f["logits_ready"], 1)
            dve.wait_ge(f["sentinels"], 2)
            if f["top"] == 6:
                dve.wait_ge(f["score_ready"], 1)
                step(dve.tensor_scalar(choice[:, :, 0:e], logits, 16.636, -88.0, ALU.min, ALU.max))
                wide = SEL
            else:
                step(dve.tensor_copy(logit[:, :, 0:e], logits))
                step(dve.tensor_reduce(row_stat[:], logit[:, :, 0:e], AX.X, ALU.max))
                dve.tensor_tensor(weight[:, :, 0:e], logit[:, :, 0:e], per_row(row_stat[:]).to_broadcast([P, TILES, e]),
                                  ALU.subtract).then_inc(f["shifted"], 1)
                groups = group_choice[:, :, 0:f["groups"]]
                step(dve.tensor_reduce(groups, logit[:, :, 0:e].rearrange("p i (g m) -> p i g m", g=f["groups"]), AX.X, ALU.max))
                for i in range(TILES):
                    last = dve.max(group_top8[:, i, :], group_choice[:, i, :])
                step(last)
                step(dve.memset(group_top8[:, :, f["top_groups"]:8], SENTINEL))
                for i in range(TILES):
                    last = dve.match_replace(group_chosen[:, i, :], group_top8[:, i, :], group_choice[:, i, :], TAKEN)
                step(last)
                step(dve.tensor_scalar(groups, group_chosen[:, :, 0:f["groups"]], TAKEN, None, ALU.is_equal))
                step(dve.tensor_scalar(group_chosen[:, :, 0:f["groups"]], groups, -OUT, OUT, ALU.mult, ALU.add))
                size = e // f["groups"]
                step(dve.tensor_tensor(choice[:, :, 0:e].rearrange("p i (g m) -> p i g m", g=f["groups"]),
                                       logit[:, :, 0:e].rearrange("p i (g m) -> p i g m", g=f["groups"]),
                                       group_chosen[:, :, 0:f["groups"]].rearrange("p i (g a) -> p i g a", a=1).to_broadcast([P, TILES, f["groups"], size]),
                                       ALU.add))
                dve.wait_ge(f["score_ready"], 1)
                step(dve.tensor_reduce(row_stat[:], score[:, :, 0:e], AX.X, ALU.add))
                step(dve.reciprocal(row_stat[:], row_stat[:]))
                step(dve.tensor_tensor(score[:, :, 0:e], score[:, :, 0:e], per_row(row_stat[:]).to_broadcast([P, TILES, e]), ALU.mult))
                wide = e + 8
            for i in range(TILES):
                last = dve.max(top8[:, i, :], choice[:, i, 0:wide])
            step(last)
            step(dve.memset(top8[:, :, f["top"]:8], SENTINEL))
            for i in range(TILES):
                last = dve.match_replace(chosen[:, i, 0:wide], top8[:, i, :], choice[:, i, 0:wide], TAKEN)
            step(last)
            step(dve.tensor_scalar(weight[:, :, 0:e], chosen[:, :, 0:e], TAKEN, None, ALU.is_equal))
            step(dve.tensor_tensor(weight[:, :, 0:e], weight[:, :, 0:e], score[:, :, 0:e], ALU.mult))
            step(dve.tensor_reduce(row_stat[:], weight[:, :, 0:e], AX.X, ALU.add))
            step(dve.tensor_scalar(row_stat[:], row_stat[:], 1e-20, None, ALU.add))
            step(dve.reciprocal(row_stat[:], row_stat[:]))
            dve.tensor_tensor(comb_tok[:, :, 0:e], weight[:, :, 0:e], per_row(row_stat[:]).to_broadcast([P, TILES, e]),
                              ALU.mult).then_inc(f["comb_ready"], 1)

            def tile(h, j, n, buf, first, last):
                for c in range(CHUNKS):
                    s = n * CHUNKS + c
                    dve.wait_ge(f["u_ready"], s + 1)
                    if h or not first:
                        dve.wait_ge(f["act_hi_ready"], s - 1)
                    dve.wait_ge(f["gated_comb_ready"], s + 1)
                    dve.tensor_tensor(act_sb[:, c, :], psum[:, U_BANK + c, :], gated_comb[:, c, :], ALU.mult).then_inc(f["act_ready"], 1)
                    dve.wait_ge(f["act_hi_ready"], s + 1)
                    dve.tensor_tensor(act_lo[:, c, :], act_sb[:, c, :], act_hi[:, c, :].bitcast(F32), ALU.subtract).then_inc(f["act_lo_ready"], 1)

            def tail(h):
                for b in range(4):
                    dve.wait_ge(f["yT_ready"], 4 * h + b + 1)
                    rows = x[:, h * TILES // 2 + 2 * b:h * TILES // 2 + 2 * b + 2, :]
                    dve.tensor_tensor(rows, psum[:, b, :].rearrange("p (i d) -> p i d", i=2), rows, ALU.add).then_inc(f["y_added"], 1)

            hidden_tiles(dve, f, tile, tail)

        def experts_tensor(f):
            pe = nc.tensor
            pe.wait_ge(f["gate_split"], 1)
            pe.wait_ge(lnT_lo, (f["norm"] + 1) * LNT)
            e = f["experts"]
            for i in range(TILES):
                pairs = []
                for c in range(DC):
                    t, w = slice(i * P, (i + 1) * P), slice(c * e, (c + 1) * e)
                    pairs += passes(xT_hi[:, c, t], xT_lo[:, c, t], gate_hi[:, w], gate_lo[:, w])
                last = chain(psum[:, Y_BANK, i * e:(i + 1) * e], pairs)
            last.then_inc(f["logits_ready"], 1)
            pe.wait_ge(f["comb_ready"], 1)
            for i in range(TILES):
                last = pe.transpose(psum[0:e, i // 4, i % 4 * P:(i % 4 + 1) * P], comb_tok[:, i, 0:e], ident[:])
                if i % 4 == 3:
                    last.then_inc(f["combT_ready"], 1)

            def down(n, c, buf, first, last_tile):
                s = n * CHUNKS + c
                if c == 0:
                    pe.wait_ge(f["d_split"], n + 1)
                for lows in range(2):
                    pe.wait_ge((f["act_lo_ready"] if lows else f["act_hi_ready"]), s + 1)
                    for d in range(DC):
                        w = slice(WD + d * P, WD + (d + 1) * P)
                        pairs = passes(fw_hi[:, buf, w], fw_lo[:, buf, w], act_hi[:, c, :], act_lo[:, c, :])
                        pairs = (pairs[0], pairs[2]) if not lows else pairs[1:2]
                        last = chain(psum[:, Y_BANK + d * CHUNKS + c, :], pairs, start=first and lows == 0, stop=last_tile and lows == 1,
                                     skip_group_check=True)
                last.then_inc(f["down_done"], 1)

            def tile(h, j, n, buf, first, last):
                for c in range(CHUNKS):
                    s = n * CHUNKS + c
                    if c == 0:
                        pe.wait_ge(f["gu_split"], n + 1)
                    if first and h == 0 and c == 0:
                        pe.wait_ge(f["combT_copied"], TILES // 4)
                    if first and h == 1 and c == 0:
                        pe.wait_ge(f["y_added"], 4)
                        pe.wait_ge(f["y_copied"], DC * CHUNKS)
                    if h or not first:
                        pe.wait_ge(f["gated_ready"], s - 1)
                    for w0, bank, ready in ((WG, G_BANK, f["g_ready"]), (WU, U_BANK, f["u_ready"])):
                        if w0 == WU and (h or not first):
                            pe.wait_ge(f["act_ready"], s - 1)
                        pairs = []
                        for k in range(DC):
                            w = slice(w0 + k * P, w0 + (k + 1) * P)
                            t = bass.ds(h * HALF + c * BANK, BANK)
                            pairs += passes(fw_hi[:, buf, w], fw_lo[:, buf, w], xT_hi[:, k, t], xT_lo[:, k, t])
                        chain(psum[:, bank + c, :], pairs).then_inc(ready, 1)
                    if c > 0:
                        down(n, c - 1, buf, first, last)
                    elif not first:
                        down(n - 1, CHUNKS - 1, 1 - buf, isinstance(j, int) and j == 1, False)

            def tail(h):
                down((h + 1) * f["tiles"] - 1, CHUNKS - 1, ((h + 1) * f["tiles"] - 1) % 2, False, True)
                pe.wait_ge(f["y_copied"], (h + 1) * DC * CHUNKS)
                for b in range(4):
                    for i in range(2):
                        for d in range(DC):
                            t = 2 * b + i
                            last = pe.transpose(psum[:, b, (i * DC + d) * P:(i * DC + d + 1) * P], yT[:, d, t * P:(t + 1) * P], ident[:])
                    last.then_inc(f["yT_ready"], 1)

            hidden_tiles(pe, f, tile, tail)

        r = Region(keep.at)
        y_hi = Region(r.at)("y_hi", [P, EJ, PT], F32R)
        in_raw = r("in_raw", [P, DC, MJ * P])
        in_hi, in_lo = r("in_hi", [P, DC, MJ * P], F32R), r("in_lo", [P, DC, MJ * P], F32R)
        ow_raw = r("ow_raw", [P, EJ, D])
        ow_hi, ow_lo = r("ow_hi", [P, EJ, D], F32R), r("ow_lo", [P, EJ, D], F32R)
        cols = r("cols", [P, CJ * (TAPS + 1) + 2 * EJ + 2])
        start_row = r("start_row", [P, SEQ])
        ones_col = r("ones_col", [P, 1])
        a_col = r("a_col", [P, 1])
        silu_gate = r("silu_gate", [P, EJ, PT])
        conv = r("conv", [P, CJ, PT])
        z, neg_abs, dt, decay = (r(n, [NH, PT]) for n in ("z", "neg_abs", "dt", "decay"))
        dt_tok = r("dt_tok", [P, 4, NH])
        decay_all = r("decay_all", [P, NH, PT])
        h_hi, h_lo = r("h_hi", [P, 4, E], F32R), r("h_lo", [P, 4, E], F32R)
        gram = r("gram", [P, 2, 3 * P])
        since = r("since", [P, 2, 3 * P])
        mix = r("mix", [P, 2, 3 * P])
        mix_hi, mix_lo = r("mix_hi", [P, 2, 3 * P], F32R), r("mix_lo", [P, 2, 3 * P], F32R)
        y = r("y", [P, EJ, PT])
        square = silu_gate
        y_lo = r("y_lo", [P, EJ, PT], F32R)
        mean_sq, rms, rms_tmp = (r(n, [P, 4]) for n in ("mean_sq", "rms", "rms_tmp"))
        decay_dram = dram("decay_dram", [NH, T])

        tap = lambda j, k: cols[:, j * (TAPS + 1) + k:j * (TAPS + 1) + k + 1]
        at = CJ * (TAPS + 1)
        skip_col = lambda j: cols[:, at + j:at + j + 1]
        norm_col = lambda j: cols[:, at + EJ + j:at + EJ + j + 1]
        dt_bias, a_log = cols[0:NH, at + 2 * EJ:at + 2 * EJ + 1], cols[0:NH, at + 2 * EJ + 1:at + 2 * EJ + 2]

        names = ("in_loaded ow_loaded cols_loaded in_hi_done in_split ow_split start_ready a_exp a_ready proj_ready proj_read "
                 "z_ready exp_ready log_ready dt_ready decay_ready decay_stored decay_loaded dtT_ready dt_tok_ready tap_ready taps_done "
                 "conv_ready gram_ready gram_copied hT_ready h_hi_ready h_lo_ready gate_ready since_ready mix_ready mix_hi_ready "
                 "mix_lo_ready yT_ready y_ready gated_ready square_ready y_hi_ready y_lo_ready sum_ready out_ready mean_ready rms_root "
                 "out_added dve_step root_step").split()
        m = {n: sem(f"ssm_{n}") for n in names}
        ORDER = (10, 8, 9, 4, 5, 6, 7, 0, 1, 2, 3)
        CONVS = ORDER[1:7]
        SSM_UNITS = [(j, b, a) for j in range(EJ) for b in range(2) for a in range(2)]
        NU = len(SSM_UNITS)
        PROJ_BANK, DT_BANK, GRAM_BANK, HT_BANK, YT_BANK, OUT_BANK, SUM_BANK = 0, 2, 3, 4, 6, 2, 4

        def ssm_sync(free, count):
            sp = nc.sync
            sp.wait_ge(free, count)
            sp.dma_start(in_raw[:], in_w).then_inc(m["in_loaded"], 16)
            sp.dma_start(cols[:], ssm_cols).then_inc(m["cols_loaded"], 16)
            sp.dma_start(ow_raw[:], out_w).then_inc(m["ow_loaded"], 16)
            def pair(p):
                t = bass.ds(p * PT, PT)
                sp.wait_ge(m["decay_ready"], p + 1)
                sp.dma_start(decay_dram[:, t], decay[:]).then_inc(m["decay_stored"], 16)
                sp.wait_ge(m["decay_stored"], 16 * p + 16)
                wait(sp, m["since_ready"], NU * p)
                sp.dma_start(decay_all[:], decay_dram[:, t].partition_broadcast(P)).then_inc(m["decay_loaded"], 16)

            pair(0)
            with sp.Fori(1, PAIRS) as p:
                pair(p)

        def ssm_pool(free, count):
            pool = nc.gpsimd
            pool.wait_ge(free, count)
            pool.memset(start_row[:, P:SEQ], 0.0)
            pool.tensor_copy(start_row[:, 0:P], ident[:])
            pool.memset(ones_col[:], 1.0).then_inc(m["start_ready"], 1)
            pool.wait_ge(m["in_loaded"], 16)
            pool.tensor_copy(in_hi[:], in_raw[:]).then_inc(m["in_hi_done"], 1)
            pool.wait_ge(m["in_hi_done"], 1)
            pool.tensor_tensor(in_lo[:], in_raw[:], in_hi[:].bitcast(F32), ALU.subtract).then_inc(m["in_split"], 1)
            pool.wait_ge(m["ow_loaded"], 16)
            pool.tensor_copy(ow_hi[:], ow_raw[:]).then_inc(m["in_hi_done"], 1)
            pool.wait_ge(m["in_hi_done"], 2)
            pool.tensor_tensor(ow_lo[:], ow_raw[:], ow_hi[:].bitcast(F32), ALU.subtract).then_inc(m["ow_split"], 1)
            def pair(p):
                for u, (j, b, a) in enumerate(SSM_UNITS):
                    pool.wait_ge(m["mix_hi_ready"], NU * p + u + 1)
                    pool.tensor_tensor(mix_lo[:, u % 2, :], mix[:, u % 2, :], mix_hi[:, u % 2, :].bitcast(F32),
                                       ALU.subtract).then_inc(m["mix_lo_ready"], 1)
                    if a == 1 and b == 1:
                        pool.wait_ge(m["gate_ready"], EJ * p + j + 1)
                        pool.wait_ge(m["y_ready"], 2 * EJ * p + 2 * j + 2)
                        pool.tensor_tensor(y[:, j, :], y[:, j, :], silu_gate[:, j, :], ALU.mult).then_inc(m["gated_ready"], 1)

            pair(0)
            with pool.Fori(1, PAIRS) as p:
                pair(p)

        def ssm_scalar():
            act = nc.scalar
            act.wait_ge(m["cols_loaded"], 16)
            act.activation(a_col[0:NH, :], a_log, ACT.Exp).then_inc(m["a_exp"], 1)
            act.wait_ge(m["a_ready"], 1)
            def pair(p):
                act.wait_ge(m["z_ready"], p + 1)
                act.activation(neg_abs[:], neg_abs[:], ACT.Exp).then_inc(m["exp_ready"], 1)
                act.wait_ge(m["exp_ready"], p + 1)
                act.activation(neg_abs[:], neg_abs[:], ACT.Ln, bias=1.0).then_inc(m["log_ready"], 1)
                wait(act, m["decay_stored"], 16 * p)
                act.wait_ge(m["dt_ready"], p + 1)
                act.activation(decay[:], dt[:], ACT.Exp, scale=a_col[0:NH, :]).then_inc(m["decay_ready"], 1)
                for n, i in enumerate(ORDER):
                    if i in CONVS:
                        j = i - EJ
                        act.wait_ge(m["proj_ready"], MJ * p + n + 1)
                        act.activation(conv[:, j, :], psum[:, PROJ_BANK + n % 2, :], ACT.Identity, bias=tap(j, TAPS),
                                       scale=tap(j, TAPS - 1)).then_inc(m["tap_ready"], 1)
                        wait(act, m["taps_done"], CJ * p + n)
                        act.activation(conv[:, j, :], conv[:, j, :], ACT.Silu).then_inc(m["conv_ready"], 1)
                wait(act, m["sum_ready"], p)
                for n, i in enumerate(ORDER):
                    if i < EJ:
                        act.wait_ge(m["proj_ready"], MJ * p + n + 1)
                        act.activation(silu_gate[:, i, :], psum[:, PROJ_BANK + n % 2, :], ACT.Silu).then_inc(m["gate_ready"], 1)
                for t in range(4):
                    act.wait_ge(m["hT_ready"], 4 * p + t + 1)
                    act.activation(h_hi[:, t, :], psum[:, HT_BANK + t % 2, :], ACT.Copy).then_inc(m["h_hi_ready"], 1)
                for u in range(NU):
                    wait(act, m["yT_ready"], NU * p + max(u - 1, 0))
                    act.wait_ge(m["mix_ready"], NU * p + u + 1)
                    act.activation(mix_hi[:, u % 2, :], mix[:, u % 2, :], ACT.Copy).then_inc(m["mix_hi_ready"], 1)
                for j in range(EJ):
                    act.wait_ge(m["gated_ready"], EJ * p + j + 1)
                    act.activation(square[:, j, :], y[:, j, :], ACT.Square).then_inc(m["square_ready"], 1)
                    act.activation(y_hi[:, j, :], y[:, j, :], ACT.Copy, scale=norm_col(j)).then_inc(m["y_hi_ready"], 1)
                act.wait_ge(m["mean_ready"], p + 1)
                act.activation(rms[:], mean_sq[:], ACT.Sqrt).then_inc(m["rms_root"], 1)

            pair(0)
            with act.Fori(1, PAIRS) as p:
                pair(p)

        def ssm_vector():
            dve = nc.vector
            dve.wait_ge(m["a_exp"], 1)
            dve.tensor_scalar(a_col[0:NH, :], a_col[0:NH, :], -1.0, None, ALU.mult).then_inc(m["a_ready"], 1)
            dve.wait_ge(m["start_ready"], 1)
            STEPS = 2 + 2 * CJ
            def pair(p):
                count = [0]

                def step(ins):
                    count[0] += 1
                    ins.then_inc(m["dve_step"], 1)
                    dve.wait_ge(m["dve_step"], STEPS * p + count[0])

                dve.wait_ge(m["proj_ready"], MJ * p + 1)
                wait(dve, m["dt_ready"], p)
                step(dve.tensor_scalar(z[:], psum[0:NH, PROJ_BANK, :], dt_bias, None, ALU.add))
                step(dve.tensor_scalar(neg_abs[:], z[:], -1.0, None, ALU.mult))
                dve.tensor_tensor(neg_abs[:], neg_abs[:], z[:], ALU.min).then_inc(m["z_ready"], 1)
                dve.wait_ge(m["log_ready"], p + 1)
                wait(dve, m["decay_ready"], p)
                dve.scalar_tensor_tensor(dt[:], z[:], 0.0, neg_abs[:], ALU.max, ALU.add).then_inc(m["dt_ready"], 1)
                for n, i in enumerate(ORDER):
                    if i not in CONVS:
                        continue
                    j = i - EJ
                    wait(dve, m["tap_ready"], CJ * p + n)
                    for k in range(1, TAPS):
                        to = conv[:, j, :].rearrange("p (b t) -> p b t", b=2)[:, :, k:SEQ]
                        of = psum[:, PROJ_BANK + n % 2, :].rearrange("p (b t) -> p b t", b=2)[:, :, 0:SEQ - k]
                        ins = dve.scalar_tensor_tensor(to, of, tap(j, TAPS - 1 - k), to, ALU.mult, ALU.add)
                        if k < TAPS - 1:
                            step(ins)
                    ins.then_inc(m["taps_done"], 1)
                assert count[0] == STEPS
                dve.wait_ge(m["dtT_ready"], p + 1)
                dve.tensor_copy(dt_tok[:], psum[:, DT_BANK, 0:4 * NH].rearrange("p (t h) -> p t h", h=NH)).then_inc(m["dt_tok_ready"], 1)
                for b in range(2):
                    dve.wait_ge(m["gram_ready"], 2 * p + b + 1)
                    dve.tensor_copy(gram[:, b, :], psum[:, GRAM_BANK, 0:3 * P]).then_inc(m["gram_copied"], 1)
                for t in range(4):
                    dve.wait_ge(m["h_hi_ready"], 4 * p + t + 1)
                    dve.tensor_tensor(h_lo[:, t, :], psum[:, HT_BANK + t % 2, :], h_hi[:, t, :].bitcast(F32), ALU.subtract).then_inc(m["h_lo_ready"], 1)

                def decays(u):
                    j, b, a = SSM_UNITS[u]
                    if u == 0:
                        dve.wait_ge(m["decay_loaded"], 16 * p + 16)
                    wait(dve, m["mix_ready"], NU * p + max(u - 1, 0))
                    e = decay_all[:, 2 * j + a, b * SEQ:(b + 1) * SEQ]
                    dve.tensor_tensor_scan(since[:, u % 2, 0:SEQ], e, start_row[:], 0.0, ALU.mult, ALU.add)
                    dve.tensor_tensor_scan(since[:, u % 2, SEQ:3 * P], e[:, P:SEQ], start_row[:, 0:P], 0.0, ALU.mult, ALU.add) \
                        .then_inc(m["since_ready"], 1)

                def mixes(u):
                    j, b, a = SSM_UNITS[u]
                    if u == 0:
                        dve.wait_ge(m["dt_tok_ready"], p + 1)
                        dve.wait_ge(m["gram_copied"], 2 * p + 2)
                    wait(dve, m["mix_lo_ready"], NU * p + max(u - 1, 0))
                    dve.wait_ge(m["since_ready"], NU * p + u + 1)
                    for i, (c0, c1) in enumerate(((0, SEQ), (SEQ, 3 * P))):
                        ins = dve.scalar_tensor_tensor(mix[:, u % 2, c0:c1], since[:, u % 2, c0:c1], dt_tok[:, 2 * b + i, 2 * j + a:2 * j + a + 1],
                                                       gram[:, b, c0:c1], ALU.mult, ALU.mult)
                    ins.then_inc(m["mix_ready"], 1)

                def outputs(w):
                    j, b = divmod(w, 2)
                    dve.wait_ge(m["yT_ready"], NU * p + 2 * w + 2)
                    t = slice(b * SEQ, (b + 1) * SEQ)
                    for a in range(2):
                        rows = slice(a * HP, (a + 1) * HP)
                        ins = dve.scalar_tensor_tensor(y[rows, j, t], conv[rows, j, t], skip_col(j)[rows], psum[rows, YT_BANK + w % 2, a * SEQ:(a + 1) * SEQ],
                                                       ALU.mult, ALU.add)
                    ins.then_inc(m["y_ready"], 1)

                for u in range(NU + 1):
                    if u < NU:
                        decays(u)
                    if u > 0:
                        mixes(u - 1)
                    if u > 3 and u % 2 == 0:
                        outputs(u // 2 - 2)
                outputs(NU // 2 - 1)
                for j in range(EJ):
                    dve.wait_ge(m["y_hi_ready"], EJ * p + j + 1)
                    dve.scalar_tensor_tensor(y_lo[:, j, :], y[:, j, :], norm_col(j), y_hi[:, j, :].bitcast(F32), ALU.mult, ALU.subtract) \
                        .then_inc(m["y_lo_ready"], 1)
                dve.wait_ge(m["sum_ready"], p + 1)
                dve.tensor_scalar(mean_sq[:], psum[:, SUM_BANK, 0:4], 1.0 / E, SSM_EPS, ALU.mult, ALU.add).then_inc(m["mean_ready"], 1)
                dve.wait_ge(m["rms_root"], p + 1)
                inverse_root(rms[:], mean_sq[:], rms_tmp[:], m["root_step"], ROOT_STEPS * p)
                for t in range(4):
                    if t % 2 == 0:
                        dve.wait_ge(m["out_ready"], 2 * p + t // 2 + 1)
                    rows = x[:, bass.ds(4 * p + t, 1), :].rearrange("p a d -> p (a d)")
                    dve.scalar_tensor_tensor(rows, psum[:, OUT_BANK + t // 2, t % 2 * D:(t % 2 + 1) * D], rms[:, t:t + 1], rows,
                                             ALU.mult, ALU.add).then_inc(m["out_added"], 1)

            pair(0)
            with dve.Fori(1, PAIRS) as p:
                pair(p)

        def ssm_tensor():
            pe = nc.tensor
            pe.wait_ge(lnT_lo, 2 * LNT)
            pe.wait_ge(m["in_split"], 1)
            pe.wait_ge(m["start_ready"], 1)
            def pair(p):
                for n, i in enumerate(ORDER):
                    if n < 2:
                        wait(pe, m["gate_ready"], EJ * p)
                    elif n == 2:
                        pe.wait_ge(m["z_ready"], p + 1)
                    elif n < 9:
                        wait(pe, m["taps_done"], CJ * p + n - 2)
                    else:
                        wait(pe, m["gate_ready"], EJ * p + n - 8)
                    pairs = []
                    for c in range(DC):
                        w, t = slice(i * P, (i + 1) * P), bass.ds(p * PT, PT)
                        pairs += passes(in_hi[:, c, w], in_lo[:, c, w], xT_hi[:, c, t], xT_lo[:, c, t])
                    chain(psum[:, PROJ_BANK + n % 2, :], pairs).then_inc(m["proj_ready"], 1)
                pe.wait_ge(m["dt_ready"], p + 1)
                hold(pe, m["out_added"], 4 * p)
                for t in range(4):
                    last = pe.transpose(psum[:, DT_BANK, t * NH:(t + 1) * NH], dt[:, t * P:(t + 1) * P], ident[0:NH, 0:NH])
                last.then_inc(m["dtT_ready"], 1)
                pe.wait_ge(m["conv_ready"], CJ * p + 2)
                for b in range(2):
                    wait(pe, m["gram_copied"], 2 * p + b)
                    for k in range(2):
                        keys = conv[0:NS, EJ, b * SEQ + k * P:b * SEQ + (k + 1) * P]
                        rows = conv[0:NS, EJ + 1, b * SEQ + k * P:(b + 1) * SEQ]
                        last = pe.matmul(psum[:, GRAM_BANK, 2 * k * P:(2 + k) * P], keys, rows, start=True, stop=True)
                    last.then_inc(m["gram_ready"], 1)
                pe.wait_ge(m["conv_ready"], CJ * p + CJ)
                for t in range(4):
                    if t < 2:
                        wait(pe, m["out_added"], 4 * p)
                    else:
                        pe.wait_ge(m["h_lo_ready"], 4 * p + t - 1)
                    for j in range(EJ):
                        last = pe.transpose(psum[:, HT_BANK + t % 2, j * P:(j + 1) * P], conv[:, j, t * P:(t + 1) * P], ident[:])
                    last.then_inc(m["hT_ready"], 1)
                for u, (j, b, a) in enumerate(SSM_UNITS):
                    w = u // 2
                    if u == 0:
                        pe.wait_ge(m["h_lo_ready"], 4 * p + 4)
                    if a == 0:
                        wait(pe, m["y_ready"], 2 * EJ * p + max(w - 1, 0))
                    pe.wait_ge(m["mix_lo_ready"], NU * p + u + 1)
                    for i, (c0, c1) in enumerate(((0, SEQ), (SEQ, 3 * P))):
                        h = [q[:, 2 * b + i, j * P:(j + 1) * P] for q in (h_hi, h_lo)]
                        last = chain(psum[:, YT_BANK + w % 2, a * SEQ + i * P:(a + 1) * SEQ],
                                     passes(*h, mix_hi[:, u % 2, c0:c1], mix_lo[:, u % 2, c0:c1]), start=i == 0, stop=i == 1, skip_group_check=True)
                    last.then_inc(m["yT_ready"], 1)
                pe.wait_ge(m["square_ready"], EJ * p + EJ)
                for t in range(4):
                    for j in range(EJ):
                        last = pe.matmul(psum[:, SUM_BANK, t:t + 1], square[:, j, t * P:(t + 1) * P], ones_col[:], start=j == 0, stop=j == EJ - 1)
                last.then_inc(m["sum_ready"], 1)
                pe.wait_ge(m["y_lo_ready"], EJ * p + EJ)
                pe.wait_ge(m["ow_split"], 1)
                for t in range(4):
                    pairs = []
                    for j in range(EJ):
                        s = slice(t * P, (t + 1) * P)
                        pairs += passes(y_hi[:, j, s], y_lo[:, j, s], ow_hi[:, j, :], ow_lo[:, j, :])
                    last = chain(psum[:, OUT_BANK + t // 2, t % 2 * D:(t % 2 + 1) * D], pairs)
                    if t % 2:
                        last.then_inc(m["out_ready"], 1)

            pair(0)
            with pe.Fori(1, PAIRS) as p:
                pair(p)

        block = ctx.enter_context(nc.Block())

        @block.sync
        def _(sp):
            for q in range(PAIRS):
                sp.dma_start(xT_raw[:, :, q * BANK:(q + 1) * BANK],
                             x_cols.rearrange("(c p) t -> p c t", p=P)[:, :, q * BANK:(q + 1) * BANK]).then_inc(xT_loaded[q], 16)
                if q == 0:
                    sp.dma_start(aw_raw[:], attn_w[0]).then_inc(aw_loaded, 16)
            sp.dma_start(x[:], x_rows.rearrange("(i p) d -> p i d", p=P)).then_inc(x_loaded, 16)
            with sp.Fori(1, GROUPS) as g:
                sp.wait_ge(awo_split, g)
                sp.dma_start(aw_raw[:], attn_w[bass.ds(g, 1)].rearrange("a p n -> p (a n)")).then_inc(aw_loaded, 16)
            experts_sync(expert_layers[0], o_added, GROUPS * 2 * PAIRS)
            ssm_sync(expert_layers[0]["y_added"], 8)
            experts_sync(expert_layers[1], m["out_added"], TILES)
            sp.wait_ge(ln_done, NORMS * TILES)
            sp.dma_start(out.rearrange("(i p) d -> p i d", p=P), x[:]).then_inc(stored, 16)
            sp.wait_ge(stored, 16)

        @block.gpsimd
        def _(pool):
            pool.memset(ident[:], 0.0).then_inc(const_ready, 1)
            pool.memset(causal[:], 0.0).then_inc(const_ready, 1)
            pool.wait_ge(const_ready, 2)
            pool.affine_select(out=ident[:], in_=ident[:], compare_op=ALU.not_equal, fill=1.0, base=0,
                               pattern=[[-1, P]], channel_multiplier=1).then_inc(const_ready, 1)
            pool.affine_select(out=causal[:, P:2 * P], in_=causal[:, P:2 * P], compare_op=ALU.is_ge, fill=MASKED,
                               base=0, pattern=[[-1, P]], channel_multiplier=1).then_inc(const_ready, 1)

            def split_qkv(g):
                pool.tensor_copy(aw_hi[:, 0:WO], aw_raw[:, 0:WO]).then_inc(aw_hi_done, 1)
                pool.wait_ge(aw_hi_done, 2 * g + 1)
                pool.tensor_tensor(aw_lo[:, 0:WO], aw_raw[:, 0:WO], aw_hi[:, 0:WO].bitcast(F32), ALU.subtract).then_inc(aw_split, 1)

            def split_o(g):
                pool.tensor_copy(aw_hi[:, WO:WA], aw_raw[:, WO:WA]).then_inc(aw_hi_done, 1)
                pool.wait_ge(aw_hi_done, 2 * g + 2)
                pool.tensor_tensor(aw_lo[:, WO:WA], aw_raw[:, WO:WA], aw_hi[:, WO:WA].bitcast(F32), ALU.subtract).then_inc(awo_split, 1)

            def group(g, next_group):
                for i, jobs, u_s, u_t, u_v, u_o in attn_schedule(next_group):
                    if i == 1:
                        hold(pool, o_ready, g * (2 * PAIRS))
                        split_o(g)
                    if i == 13 and next_group:
                        pool.wait_ge(aw_loaded, 16 * g + 32)
                        hold(pool, qkv_ready, (g + 1) * (PAIRS * JOBS))
                        split_qkv(g + 1)
                    u = i - 1
                    if 0 <= u < UNITS:
                        hold(pool, r_ready, g * UNITS + u + 1)
                        pool.tensor_scalar(p_sb[:, u % 3, 0:P], p_sb[:, u % 3, 0:P], row_inv[:, u % 3, 0:1], None, ALU.mult)
                        pool.tensor_scalar(p_sb[:, u % 3, P:3 * P], p_sb[:, u % 3, P:3 * P], row_inv[:, u % 3, 1:2], None,
                                           ALU.mult).then_inc(p_scaled, 1)

            pool.wait_ge(aw_loaded, 16)
            split_qkv(0)
            group(0, True)
            with pool.Fori(1, GROUPS - 1) as g:
                group(g, True)
            group(GROUPS - 1, False)
            experts_pool(expert_layers[0], o_added, GROUPS * 2 * PAIRS)
            ssm_pool(expert_layers[0]["y_added"], 8)
            experts_pool(expert_layers[1], m["out_added"], TILES)

        @block.scalar
        def _(act):
            for q in range(PAIRS):
                act.wait_ge(xT_loaded[q], 16)
                act.activation(xT_hi[:, :, q * BANK:(q + 1) * BANK], xT_raw[:, :, q * BANK:(q + 1) * BANK],
                               ACT.Copy).then_inc(xT_hi_ready, 1)

            def qkv_high(g, bp, j):
                n = g * (PAIRS * JOBS) + bp * JOBS + j
                act.wait_ge(qkv_ready, n + 1)
                dst = (kT_hi if j % 2 else qT_hi)[:, bp % 2, j // 2, :] if j < 2 * HG else v_hi[:, bp % 2, j - 2 * HG, :]
                act.activation(dst, psum[:, QKV_BANK + j % 2, :], ACT.Copy).then_inc(qkv_hi, 1)

            def group(g, next_group):
                for i, jobs, u_s, u_t, u_v, u_o in attn_schedule(next_group):
                    if u_s is not None:
                        u = u_s
                        act.wait_ge(s_masked, g * UNITS + u + 1)
                        if u >= 3:
                            act.wait_ge(pT_ready, g * UNITS + u - 2)
                        act.activation(p_sb[:, u % 3, 0:P], s_sb[:, u % 2, 0:P], ACT.Exp, bias=neg_max[:, u % 3, 0:1], scale=-1.0,
                                       accum_out=row_sum[:, u % 3, 0:1])
                        act.activation(p_sb[:, u % 3, P:3 * P], s_sb[:, u % 2, P:3 * P], ACT.Exp, bias=neg_max[:, u % 3, 1:2], scale=-1.0,
                                       accum_out=row_sum[:, u % 3, 1:2]).then_inc(p_ready, 1)
                    for bp, j in jobs:
                        qkv_high(g, bp, j)
                    if u_t is not None:
                        u = u_t
                        act.wait_ge(pT_ready, g * UNITS + u + 1)
                        act.activation(pT_hi[:, u % 2, :], psum[:, PT_BANK, 0:3 * P], ACT.Copy).then_inc(pT_hi_ready, 1)
                    if u_v is not None:
                        u = u_v
                        act.wait_ge(z_ready, g * UNITS + u + 1)
                        act.activation(zT_hi[:, u % 2, :], psum[:, Z_BANK, 0:SEQ], ACT.Copy).then_inc(z_hi_ready, 1)

            for j in range(JOBS):
                qkv_high(0, 0, j)
            group(0, True)
            with act.Fori(1, GROUPS - 1) as g:
                group(g, True)
            group(GROUPS - 1, False)
            ln_scalar(0)
            experts_scalar(expert_layers[0])
            ln_scalar(1)
            ssm_scalar()
            ln_scalar(2)
            experts_scalar(expert_layers[1])
            ln_scalar(3, False)

        @block.vector
        def _(dve):
            for q in range(PAIRS):
                dve.wait_ge(xT_hi_ready, q + 1)
                dve.tensor_tensor(xT_lo[:, :, q * BANK:(q + 1) * BANK], xT_raw[:, :, q * BANK:(q + 1) * BANK],
                                  xT_hi[:, :, q * BANK:(q + 1) * BANK].bitcast(F32), ALU.subtract).then_inc(xT_lo_ready, 1)

            def qkv_low(g, bp, j):
                n = g * (PAIRS * JOBS) + bp * JOBS + j
                dve.wait_ge(qkv_hi, n + 1)
                if j < 2 * HG:
                    hi, lo = ((kT_hi, kT_lo) if j % 2 else (qT_hi, qT_lo))
                    hi, lo = hi[:, bp % 2, j // 2, :], lo[:, bp % 2, j // 2, :]
                else:
                    hi, lo = v_hi[:, bp % 2, j - 2 * HG, :], v_lo[:, bp % 2, j - 2 * HG, :]
                dve.tensor_tensor(lo, psum[:, QKV_BANK + j % 2, :], hi.bitcast(F32), ALU.subtract).then_inc(qkv_lo, 1)

            def group(g, next_group):
                for i, jobs, u_s, u_t, u_v, u_o in attn_schedule(next_group):
                    if u_s is not None:
                        u = u_s
                        if u >= 2:
                            dve.wait_ge(p_ready, g * UNITS + u - 1)
                        hold(dve, s_ready, g * UNITS + u + 1)
                        dve.tensor_tensor_reduce(s_sb[:, u % 2, 0:P], psum[:, S_BANK + u % 2, 0:P], causal[:, P:2 * P], -SCALE, 3e38,
                                                 ALU.add, ALU.min, neg_max[:, u % 3, 0:1])
                        dve.tensor_tensor_reduce(s_sb[:, u % 2, P:3 * P], psum[:, S_BANK + u % 2, P:3 * P], causal[:], -SCALE, 3e38,
                                                 ALU.add, ALU.min, neg_max[:, u % 3, 1:2]).then_inc(s_masked, 1)
                    if 0 <= i - 1 < UNITS:
                        u = i - 1
                        dve.wait_ge(p_ready, g * UNITS + u + 1)
                        dve.reciprocal(row_inv[:, u % 3, :], row_sum[:, u % 3, :]).then_inc(r_ready, 1)
                    for bp, j in jobs:
                        qkv_low(g, bp, j)
                    if u_t is not None:
                        u = u_t
                        dve.wait_ge(pT_hi_ready, g * UNITS + u + 1)
                        dve.tensor_tensor(pT_lo[:, u % 2, :], psum[:, PT_BANK, 0:3 * P], pT_hi[:, u % 2, :].bitcast(F32),
                                          ALU.subtract).then_inc(pT_lo_ready, 1)
                    if u_v is not None:
                        u = u_v
                        dve.wait_ge(z_hi_ready, g * UNITS + u + 1)
                        dve.tensor_tensor(zT_lo[:, u % 2, :], psum[:, Z_BANK, 0:SEQ], zT_hi[:, u % 2, :].bitcast(F32),
                                          ALU.subtract).then_inc(z_lo_ready, 1)
                    if u_o is not None and unit(u_o)[1] == HG - 1:
                        bp, _, b = unit(u_o)
                        dve.wait_ge(o_ready, g * (2 * PAIRS) + 2 * bp + b + 1)
                        rows = x[:, 4 * bp + 2 * b:4 * bp + 2 * b + 2, :]
                        dve.tensor_tensor(rows, psum[:, O_BANK + b, :].rearrange("p (i d) -> p i d", i=2), rows,
                                          ALU.add).then_inc(o_added, 1)

            for j in range(JOBS):
                qkv_low(0, 0, j)
            dve.wait_ge(const_ready, 4)
            dve.wait_ge(x_loaded, 16)
            group(0, True)
            with dve.Fori(1, GROUPS - 1) as g:
                group(g, True)
            group(GROUPS - 1, False)
            ln_vector(0, o_added, GROUPS * 2 * PAIRS)
            ln_lows(0)
            experts_vector(expert_layers[0])
            ln_vector(1, expert_layers[0]["y_added"], 8)
            ln_lows(1)
            ssm_vector()
            ln_vector(2, m["out_added"], TILES)
            ln_lows(2)
            experts_vector(expert_layers[1])
            ln_vector(3, expert_layers[1]["y_added"], 8)

        @block.tensor
        def _(pe):
            def qkv_job(g, bp, j):
                n = g * (PAIRS * JOBS) + bp * JOBS + j
                if not isinstance(n, int) or n >= 2:
                    pe.wait_ge(qkv_lo, n - 1)
                if j == 0 and bp % PAIRS == 0:
                    pe.wait_ge(aw_split, g + bp // PAIRS + 1)
                if isinstance(g, int) and g == 0 and bp == 0 and j == 0:
                    pe.wait_ge(xT_lo_ready, 1)
                if bp < PAIRS and j == 0:
                    pe.wait_ge(xT_lo_ready, bp + 1)
                bp %= PAIRS
                bank = psum[:, QKV_BANK + j % 2, :]
                if j < 2 * HG:
                    w0 = (WK if j % 2 else WQ) + j // 2 * DC * DH
                    pairs = []
                    for c in range(DC):
                        w = slice(w0 + c * DH, w0 + (c + 1) * DH)
                        m = slice(bp * BANK, (bp + 1) * BANK)
                        pairs += passes(aw_hi[:, w], aw_lo[:, w], xT_hi[:, c, m], xT_lo[:, c, m])
                    chain(bank, pairs).then_inc(qkv_ready, 1)
                else:
                    for i in range(2):
                        t0 = bp * BANK + (2 * (j - 2 * HG) + i) * P
                        pairs = []
                        for c in range(DC):
                            w = slice(WV + c * HG * DH, WV + (c + 1) * HG * DH)
                            pairs += passes(xT_hi[:, c, t0:t0 + P], xT_lo[:, c, t0:t0 + P], aw_hi[:, w], aw_lo[:, w])
                        last = chain(bank[:, i * HG * DH:(i + 1) * HG * DH], pairs)
                    last.then_inc(qkv_ready, 1)

            def scores(g, u):
                bp, h, b = unit(u)
                pe.wait_ge(qkv_lo, g * (PAIRS * JOBS) + bp * JOBS + 2 * h + 2)
                wait(pe, s_masked, g * UNITS + max(u - 1, 0))
                for i in range(2):
                    s = slice(b * SEQ + i * P, b * SEQ + (i + 1) * P)
                    m = slice(b * SEQ, b * SEQ + (i + 1) * P)
                    q, k = (qT_hi, qT_lo), (kT_hi, kT_lo)
                    last = chain(psum[:, S_BANK + u % 2, i * P:(2 * i + 1) * P], passes(
                        *(t[:, bp % 2, h, s] for t in q), *(t[:, bp % 2, h, m] for t in k)))
                last.then_inc(s_ready, 1)

            def transposes(g, u):
                pe.wait_ge(p_scaled, g * UNITS + u + 1)
                wait(pe, pT_lo_ready, g * UNITS + u)
                for i in range(3):
                    last = pe.transpose(psum[:, PT_BANK, i * P:(i + 1) * P], p_sb[:, u % 3, i * P:(i + 1) * P], ident[:])
                last.then_inc(pT_ready, 1)

            def values(g, u):
                bp, h, b = unit(u)
                pe.wait_ge(pT_lo_ready, g * UNITS + u + 1)
                pe.wait_ge(qkv_lo, g * (PAIRS * JOBS) + (bp + 1) * JOBS)
                wait(pe, z_lo_ready, g * UNITS + u)
                for i in range(2):
                    v = [t[:, bp % 2, b, i * HG * DH + h * DH:i * HG * DH + (h + 1) * DH] for t in (v_hi, v_lo)]
                    p = [t[:, u % 2, 2 * i * P:(2 + i) * P] for t in (pT_hi, pT_lo)]
                    last = chain(psum[:, Z_BANK, i * P:2 * P], passes(*v, *p), start=i == 0, stop=i == 1, skip_group_check=True)
                last.then_inc(z_ready, 1)

            def output(g, u):
                bp, h, b = unit(u)
                pe.wait_ge(z_lo_ready, g * UNITS + u + 1)
                if h == 0:
                    if u == 0:
                        pe.wait_ge(awo_split, g + 1)
                    wait(pe, o_added, g * (2 * PAIRS) + max(2 * bp + b - 1, 0))
                w = slice(WO + h * D, WO + (h + 1) * D)
                for i in range(2):
                    z = [t[:, u % 2, i * P:(i + 1) * P] for t in (zT_hi, zT_lo)]
                    last = chain(psum[:, O_BANK + b, i * D:(i + 1) * D], passes(*z, aw_hi[:, w], aw_lo[:, w]),
                                 start=h == 0 and i == 0, stop=h == HG - 1, skip_group_check=True)
                if h == HG - 1:
                    last.then_inc(o_ready, 1)

            def group(g, next_group):
                for i, jobs, u_s, u_t, u_v, u_o in attn_schedule(next_group):
                    if u_s is not None:
                        scores(g, u_s)
                    for bp, j in jobs:
                        qkv_job(g, bp, j)
                    if u_t is not None:
                        transposes(g, u_t)
                    if u_v is not None:
                        values(g, u_v)
                    if u_o is not None:
                        output(g, u_o)

            for j in range(JOBS):
                qkv_job(0, 0, j)
            pe.wait_ge(const_ready, 4)
            group(0, True)
            with pe.Fori(1, GROUPS - 1) as g:
                group(g, True)
            group(GROUPS - 1, False)
            ln_tensor(0)
            experts_tensor(expert_layers[0])
            ln_tensor(1)
            ssm_tensor()
            ln_tensor(2)
            experts_tensor(expert_layers[1])


def lay_out(inputs):
    import numpy as np

    a = {n: np.asarray(v) for n, v in inputs.items()}
    x = a["L0_attn_x"].reshape(T, D)
    def heads(w):
        return w.reshape(GROUPS, HG, DH, DC, P).transpose(0, 4, 1, 3, 2)
    q, k = (heads(a[f"L0_attn_W_{n}"]).reshape(GROUPS, P, -1) for n in "QK")
    v = heads(a["L0_attn_W_V"]).transpose(0, 1, 3, 2, 4).reshape(GROUPS, P, -1)
    o = a["L0_attn_W_O"].reshape(GROUPS, HG, D, DH).transpose(0, 3, 1, 2).reshape(GROUPS, P, -1)
    attn_w = np.concatenate([q, k, v, o], axis=2)

    def hidden_tiles(gate, up, down, layer):
        n = layer["tiles"]
        pad = n * P - layer["hidden"]
        gate, up = (np.pad(w, ((0, 0), (0, pad))).reshape(DC, P, n, P).transpose(2, 1, 0, 3).reshape(n, P, DC * P) for w in (gate, up))
        down = np.pad(down, ((0, pad), (0, 0))).reshape(n, P, D)
        return np.concatenate([gate, up, down], axis=2)

    def cols(w):
        return w.transpose(1, 0, 2).reshape(D, -1)

    l0_w = hidden_tiles(np.concatenate([a["L0_ffn_sg"], cols(a["L0_ffn_wg"])], 1),
                        np.concatenate([a["L0_ffn_su"], cols(a["L0_ffn_wu"])], 1),
                        np.concatenate([a["L0_ffn_sd"], a["L0_ffn_wd"].reshape(-1, D)], 0), L0)
    up = a["L1_ffn_expert_up_w"].transpose(0, 2, 1)
    sh = a["L1_ffn_shared_up_w"].T
    w, s = L1["width"], L1["shared"]
    l1_w = hidden_tiles(np.concatenate([sh[:, :s], cols(up[:, :, :w])], 1),
                        np.concatenate([sh[:, s:], cols(up[:, :, w:])], 1),
                        np.concatenate([a["L1_ffn_shared_down_w"].T, a["L1_ffn_expert_down_w"].transpose(0, 2, 1).reshape(-1, D)], 0), L1)
    rows = lambda w: w.reshape(DC, P, -1).transpose(1, 0, 2)

    pw = a["L1_attn_in_proj_w"]
    def tile(w, n):
        return np.pad(w, ((0, n * P - w.shape[0]),) + ((0, 0),) * (w.ndim - 1))
    cut = [E, 2 * E, 2 * E + NS, 2 * E + 2 * NS]
    g_, h_, b_, c_, d_ = np.split(pw, cut)
    in_w = np.concatenate([g_, h_, tile(b_, 1), tile(c_, 1), tile(d_, 1)])
    in_w = rows(np.ascontiguousarray(in_w.T))
    conv = np.concatenate([a["L1_attn_conv_w"], a["L1_attn_conv_b"][:, None]], 1)
    h_, b_, c_ = np.split(conv, [E, E + NS])
    conv = np.concatenate([h_, tile(b_, 1), tile(c_, 1)]).reshape(CJ, P, TAPS + 1).transpose(1, 0, 2).reshape(P, -1)
    per = lambda v: np.ascontiguousarray(v.reshape(EJ, P).T)
    ssm_cols = np.concatenate([conv, per(np.repeat(a["L1_attn_D"], HP)), per(a["L1_attn_norm_w"]),
                               tile(a["L1_attn_dt_bias"][:, None], 1), tile(a["L1_attn_A_log"][:, None], 1)], 1)
    out_w = a["L1_attn_out_proj_w"].T.reshape(EJ, P, D).transpose(1, 0, 2)
    out = dict(x_rows=x, x_cols=x.T, attn_w=attn_w, l0_gate=rows(a["L0_ffn_gate_w"]), l0_w=l0_w,
               l1_gate=rows(a["L1_ffn_gate_w"].T), l1_w=l1_w, in_w=in_w, ssm_cols=ssm_cols, out_w=out_w)
    return {n: np.ascontiguousarray(v) for n, v in out.items()}


def kernel(**inputs):
    import concourse.bacc as bacc
    from concourse.bass_utils import run_bass_kernel_spmd

    nc = bacc.Bacc("TRN2", target_bir_lowering=False, num_devices=1)
    arrays = lay_out(inputs)
    aps = {n: nc.dram_tensor(n, v.shape, mybir.dt.from_np(v.dtype), kind="ExternalInput").ap() for n, v in arrays.items()}
    out = nc.dram_tensor("out", (T, D), F32, kind="ExternalOutput").ap()
    program(nc, **aps, out=out)
    result = run_bass_kernel_spmd(nc, [arrays], core_ids=[0])
    return result.results[0]["out"].reshape(BATCH, SEQ, D)
```

```python
from contextlib import ExitStack

import concourse.bass as bass
from concourse import mybir

F32 = mybir.dt.float32
F32R = mybir.dt.float32r
ALU = mybir.AluOpType
ACT = mybir.ActivationFunctionType
AX = mybir.AxisListType

P = 128
BATCH, SEQ, D = 8, 256, 256
T = BATCH * SEQ
TILES = T // P
DC = D // P
BANK = 512
LN_EPS = 1e-5

HEADS, DH = 16, 128
HG = 2
GROUPS = HEADS // HG
PAIRS = BATCH // 2
UNITS = PAIRS * HG * 2
JOBS = 2 * HG + 2
WQ, WK, WV, WO = 0, HG * DC * DH, 2 * HG * DC * DH, 3 * HG * DC * DH
WA = 3 * HG * DC * DH + HG * D
MASKED = -1e9 * DH ** 0.5
SCALE = DH ** -0.5

HALF = T // 2
CHUNKS = HALF // BANK
WG, WU, WD, WF = 0, DC * P, 2 * DC * P, 2 * DC * P + D
SEL = 40
OUT = -1e30
SENTINEL = -2e30
TAKEN = -3e30
L0 = dict(name="l0", experts=32, width=96, shared=192, top=6)
L1 = dict(name="l1", experts=16, width=176, shared=352, top=4, groups=4, top_groups=2)
for _l in (L0, L1):
    _l["hidden"] = _l["shared"] + _l["experts"] * _l["width"]
    _l["tiles"] = -(-_l["hidden"] // P)

E, NH, HP, NS, TAPS = 512, 8, 64, 64, 4
EJ = E // P
MJ = 2 * EJ + 3
CJ = EJ + 2
PT = 2 * SEQ
SSM_EPS = 1e-6


def program(nc, x_rows, x_cols, attn_w, l0_gate, l0_w, l1_gate, l1_w, in_w, ssm_cols, out_w, out):
    with ExitStack() as ctx:
        def sem(name):
            return ctx.enter_context(nc.semaphore(name))

        def dram(name, shape):
            return nc.dram_tensor(name, shape, F32, kind="Internal").ap()

        def hold(eng, semaphore, count):
            if not isinstance(count, int) or count > 0:
                eng.wait_ge(semaphore, count)
                eng.sem_inc(held, 1)

        held = sem("held")

        def wait(eng, semaphore, count):
            if not isinstance(count, int) or count > 0:
                eng.wait_ge(semaphore, count)

        class Region:

            def __init__(self, at):
                self.at = at

            def __call__(self, name, shape, dt=F32):
                size = 4
                for n in shape[1:]:
                    size *= n
                t = nc.alloc_sbuf_tensor_at(name, shape, dt, offset=self.at)
                self.at += -(-size // 64) * 64
                assert self.at <= nc.sbuf_usable_end, (name, self.at)
                return t

        keep = Region(nc.sbuf_base + 64 - nc.sbuf_base % 64)
        ident = keep("ident", [P, P])
        causal = keep("causal", [P, 2 * P])
        x = keep("x", [P, TILES, D])
        xT_hi = keep("xT_hi", [P, DC, T], F32R)
        xT_lo = keep("xT_lo", [P, DC, T], F32R)
        stats = keep("stats", [P, TILES, 6])
        mv = keep("mv", [P, TILES, 2])
        var, rstd, rtmp = (keep(n, [P, TILES]) for n in ("var", "rstd", "rtmp"))
        psum = ctx.enter_context(nc.psum_tensor("psum", [P, 8, BANK], F32))

        x_loaded = sem("x_loaded")
        const_ready = sem("const_ready")

        r = Region(keep.at)
        xT_raw = r("xT_raw", [P, DC, T])
        aw_raw = r("aw_raw", [P, WA])
        aw_hi = r("aw_hi", [P, WA], F32R)
        aw_lo = r("aw_lo", [P, WA], F32R)
        qT_hi, qT_lo, kT_hi, kT_lo = (r(n, [P, 2, HG, 2 * SEQ], F32R) for n in ("qT_hi", "qT_lo", "kT_hi", "kT_lo"))
        v_hi, v_lo = (r(n, [P, 2, 2, 2 * HG * DH], F32R) for n in ("v_hi", "v_lo"))
        s_sb = r("s_sb", [P, 2, 3 * P])
        p_sb = r("p_sb", [P, 3, 3 * P])
        pT_hi, pT_lo = (r(n, [P, 2, 3 * P], F32R) for n in ("pT_hi", "pT_lo"))
        zT_hi, zT_lo = (r(n, [P, 2, SEQ], F32R) for n in ("zT_hi", "zT_lo"))
        neg_max, row_sum, row_inv = (r(n, [P, 3, 2]) for n in ("neg_max", "row_sum", "row_inv"))

        xT_loaded = [sem(f"xT_loaded{i}") for i in range(PAIRS)]
        xT_hi_ready, xT_lo_ready = sem("xT_hi_ready"), sem("xT_lo_ready")
        aw_loaded, aw_split = sem("aw_loaded"), sem("aw_split")
        aw_hi_done = sem("aw_hi_done")
        qkv_ready, qkv_hi, qkv_lo = sem("qkv_ready"), sem("qkv_hi"), sem("qkv_lo")
        s_ready, s_masked = sem("s_ready"), sem("s_masked")
        p_ready, r_ready, p_scaled = sem("p_ready"), sem("r_ready"), sem("p_scaled")
        pT_ready, pT_hi_ready, pT_lo_ready = sem("pT_ready"), sem("pT_hi_ready"), sem("pT_lo_ready")
        z_ready, z_hi_ready, z_lo_ready = sem("z_ready"), sem("z_hi_ready"), sem("z_lo_ready")
        o_ready, o_added = sem("o_ready"), sem("o_added")

        QKV_BANK, S_BANK, PT_BANK, Z_BANK, O_BANK = 0, 2, 4, 5, 6

        def passes(a_hi, a_lo, b_hi, b_lo):
            return ((a_hi, b_hi), (a_hi, b_lo), (a_lo, b_hi))

        def attn_schedule(next_group):
            lag_t, lag_v, lag_o = 2, 3, 4
            for i in range(UNITS + lag_o):
                jobs = []
                bp = i // (2 * HG)
                if i < UNITS - 2 * HG:
                    jobs = [(bp + 1, j) for j in ((0, 1), (2,), (3, 4), (5,))[i % 4]]
                elif i >= UNITS and next_group:
                    jobs = [(PAIRS, j) for j in ((0, 1), (2, 3), (4, 5), ())[i - UNITS]]
                yield i, jobs[:1], jobs[1:], i if i < UNITS else None, *(i - g if 0 <= i - g < UNITS else None for g in (lag_t, lag_v, lag_o))

        def unit(u):
            return u // (2 * HG), u % (2 * HG) // 2, u % 2

        ln_stat, ln_aggr, ln_var, ln_sqrt, ln_done = (sem(n) for n in ("ln_stat", "ln_aggr", "ln_var", "ln_sqrt", "ln_done"))
        ln_root = sem("ln_root")
        lnT_ready, lnT_hi, lnT_lo = sem("lnT_ready"), sem("lnT_hi"), sem("lnT_lo")
        stored = sem("stored")
        NORMS = 4
        LNT = DC * TILES // 4

        def inverse_root(root, value, tmp, done, base):
            dve = nc.vector
            dve.reciprocal(root, root).then_inc(done, 1)
            dve.wait_ge(done, base + 1)
            dve.tensor_tensor(tmp, root, root, ALU.mult).then_inc(done, 1)
            dve.wait_ge(done, base + 2)
            dve.tensor_tensor(tmp, tmp, value, ALU.mult).then_inc(done, 1)
            dve.wait_ge(done, base + 3)
            dve.tensor_scalar(tmp, tmp, -0.5, 1.5, ALU.mult, ALU.add).then_inc(done, 1)
            dve.wait_ge(done, base + 4)
            dve.tensor_tensor(root, root, tmp, ALU.mult).then_inc(done, 1)
            dve.wait_ge(done, base + ROOT_STEPS)

        ROOT_STEPS = 5

        def ln_vector(n, ready, count):
            dve = nc.vector
            dve.wait_ge(ready, count)
            for i in range(TILES):
                dve.bn_stats(stats[:, i, :], x[:, i, :]).then_inc(ln_stat, 1)
            for i in range(TILES):
                dve.wait_ge(ln_stat, n * TILES + i + 1)
                dve.bn_aggr(mv[:, i, :], stats[:, i, :]).then_inc(ln_aggr, 1)
            dve.wait_ge(ln_aggr, (n + 1) * TILES)
            dve.tensor_scalar(var[:], mv[:, :, 1], LN_EPS, None, ALU.add).then_inc(ln_var, 1)
            dve.wait_ge(ln_sqrt, n + 1)
            inverse_root(rstd[:], var[:], rtmp[:], ln_root, n * ROOT_STEPS)
            for i in range(TILES):
                dve.tensor_scalar(x[:, i, :], x[:, i, :], mv[:, i, 0:1], rstd[:, i:i + 1],
                                  ALU.subtract, ALU.mult).then_inc(ln_done, 1)

        def ln_lows(n):
            dve = nc.vector
            for b in range(LNT):
                c, q = b % DC, b // DC
                dve.wait_ge(lnT_hi, n * LNT + b + 1)
                dve.tensor_tensor(xT_lo[:, c, q * BANK:(q + 1) * BANK], psum[:, b, :],
                                  xT_hi[:, c, q * BANK:(q + 1) * BANK].bitcast(F32), ALU.subtract).then_inc(lnT_lo, 1)

        def ln_tensor(n):
            pe = nc.tensor
            if n == 0:
                pe.wait_ge(const_ready, 4)
            for b in range(LNT):
                c, q = b % DC, b // DC
                pe.wait_ge(ln_done, n * TILES + 4 * q + 4)
                for i in range(4):
                    last = pe.transpose(psum[:, b, i * P:(i + 1) * P], x[:, 4 * q + i, c * P:(c + 1) * P], ident[:])
                last.then_inc(lnT_ready, 1)

        def ln_scalar(n, transposed=True):
            act = nc.scalar
            act.wait_ge(ln_var, n + 1)
            act.activation(rstd[:], var[:], ACT.Sqrt).then_inc(ln_sqrt, 1)
            if not transposed:
                return
            for b in range(LNT):
                c, q = b % DC, b // DC
                act.wait_ge(lnT_ready, n * LNT + b + 1)
                act.activation(xT_hi[:, c, q * BANK:(q + 1) * BANK], psum[:, b, :], ACT.Copy).then_inc(lnT_hi, 1)

        def chain(out_ap, pairs, start=True, stop=True, **kw):
            for n, (w, m) in enumerate(pairs):
                last = nc.tensor.matmul(out_ap, w, m, start=start and n == 0, stop=stop and n == len(pairs) - 1, **kw)
            return last

        r = Region(keep.at)
        fw_raw = r("fw_raw", [P, 2, WF])
        fw_hi, fw_lo = r("fw_hi", [P, 2, WF], F32R), r("fw_lo", [P, 2, WF], F32R)
        comb = r("comb", [P, 2, HALF])
        gated, gated_comb, act_sb = r("gated", [P, 2, BANK]), r("gated_comb", [P, 2, BANK]), r("act_sb", [P, 2, BANK])
        act_hi, act_lo = r("act_hi", [P, 2, BANK], F32R), r("act_lo", [P, 2, BANK], F32R)
        yT = r("yT", [P, DC, HALF])
        gate_raw = r("gate_raw", [P, DC * 32])
        gate_hi, gate_lo = r("gate_hi", [P, DC * 32], F32R), r("gate_lo", [P, DC * 32], F32R)
        ones_row = r("ones_row", [1, T])
        logit, score, weight, comb_tok = (r(n, [P, TILES, 32]) for n in ("logit", "score", "weight", "comb_tok"))
        choice, chosen = r("choice", [P, TILES, SEL]), r("chosen", [P, TILES, SEL])
        top8, group_top8 = r("top8", [P, TILES, 8]), r("group_top8", [P, TILES, 8])
        row_stat = r("row_stat", [P, TILES])
        group_choice, group_chosen = r("group_choice", [P, TILES, 16]), r("group_chosen", [P, TILES, 16])
        combT = r("combT", [32, T])

        def signals(layer):
            names = ("gate_loaded gate_hi_done gate_split ones_ready ones_stored sentinels logits_ready score_ready shifted gate_step "
                     "comb_ready combT_ready combT_copied comb_stored w_hi_done gu_split d_split g_ready u_ready gated_ready "
                     "gated_comb_ready act_ready act_hi_ready act_lo_ready down_done y_copied yT_ready y_added").split()
            return dict({n: sem(f"{layer}_{n}") for n in names},
                        w_loaded=[sem(f"{layer}_w_loaded{i}") for i in range(2)],
                        comb_loaded=[sem(f"{layer}_comb_loaded{i}") for i in range(2)])

        expert_layers = [
            dict(**layer, norm=2 * i, w_dram=w, gate_dram=g, comb_dram=dram(f"comb_dram{i}", [layer["experts"] + 1, T]), **signals(f"l{i}"))
            for i, (layer, g, w) in enumerate(((L0, l0_gate, l0_w), (L1, l1_gate, l1_w)))]
        G_BANK, U_BANK, Y_BANK = 0, 2, 4

        def segments(f, j):
            cuts, row = [], lambda n: f["experts"] if n < f["shared"] or n >= f["hidden"] else (n - f["shared"]) // f["width"]
            for p in range(P):
                n = row(j * P + p)
                if cuts and cuts[-1][0] == n:
                    cuts[-1][2] = p + 1
                else:
                    cuts.append([n, p, p + 1])
            if len(cuts) == 1:
                cuts = [[cuts[0][0], 0, P // 2], [cuts[0][0], P // 2, P]]
            assert len(cuts) == 2
            return cuts

        def hidden_tiles(eng, f, body, tail):
            n = f["tiles"]
            pairs = (n - 1) // 2
            for h in range(2):
                for j in range(2):
                    body(h, j, h * n + j, (h * n + j) % 2, j == 0, False)
                with eng.Fori(1, pairs) as m:
                    for j in range(2):
                        body(h, 2 * m + j, 2 * m + j + h * n, (h * n + j) % 2, False, False)
                for j in range(2 * pairs, n):
                    body(h, j, h * n + j, (h * n + j) % 2, False, j == n - 1)
                tail(h)

        def experts_sync(f, free, count):
            sp = nc.sync
            sp.wait_ge(free, count)
            sp.dma_start(gate_raw[:, 0:DC * f["experts"]], f["gate_dram"].rearrange("p c e -> p (c e)")).then_inc(f["gate_loaded"], 16)
            sp.wait_ge(f["ones_ready"], 1)
            sp.dma_start(f["comb_dram"][f["experts"]:f["experts"] + 1, :], ones_row[:]).then_inc(f["ones_stored"], 16)
            stored_seen = False
            for n in range(2 * f["tiles"]):
                h, j = divmod(n, f["tiles"])
                if n >= 2:
                    sp.wait_ge(f["d_split"], n - 1)
                sp.dma_start(fw_raw[:, n % 2, :], f["w_dram"][j]).then_inc(f["w_loaded"][n % 2], 16)
                if n >= 2:
                    sp.wait_ge(f["gated_comb_ready"], CHUNKS * (n - 1))
                cuts = segments(f, j)
                if n == 0:
                    sp.wait_ge(f["ones_stored"], 16)
                if not stored_seen and any(row < f["experts"] for row, _, _ in cuts):
                    sp.wait_ge(f["combT_copied"], TILES // 4)
                    sp.dma_start(f["comb_dram"][0:f["experts"], :], combT[0:f["experts"], :]).then_inc(f["comb_stored"], 16)
                    sp.wait_ge(f["comb_stored"], 16)
                    stored_seen = True
                for row, p0, p1 in cuts:
                    sp.dma_start(comb[p0:p1, n % 2, :], f["comb_dram"][row, h * HALF:(h + 1) * HALF].partition_broadcast(p1 - p0)) \
                        .then_inc(f["comb_loaded"][n % 2], 16)

        def experts_pool(f, free, count):
            pool = nc.gpsimd
            pool.wait_ge(free, count)
            pool.memset(ones_row[:], 1.0).then_inc(f["ones_ready"], 1)
            pool.memset(choice[:], SENTINEL).then_inc(f["sentinels"], 1)
            pool.memset(group_choice[:], SENTINEL).then_inc(f["sentinels"], 1)
            pool.wait_ge(f["gate_loaded"], 16)
            cols = slice(0, DC * f["experts"])
            pool.tensor_copy(gate_hi[:, cols], gate_raw[:, cols]).then_inc(f["gate_hi_done"], 1)
            pool.wait_ge(f["gate_hi_done"], 1)
            pool.tensor_tensor(gate_lo[:, cols], gate_raw[:, cols], gate_hi[:, cols].bitcast(F32), ALU.subtract).then_inc(f["gate_split"], 1)

            def split(n, buf, part, done, steps):
                pool.tensor_copy(fw_hi[:, buf, part], fw_raw[:, buf, part]).then_inc(f["w_hi_done"], 1)
                pool.wait_ge(f["w_hi_done"], steps)
                pool.tensor_tensor(fw_lo[:, buf, part], fw_raw[:, buf, part], fw_hi[:, buf, part].bitcast(F32), ALU.subtract).then_inc(done, 1)

            def loads(n, buf):
                return (n - buf) * 8 + 16

            def tile(h, j, n, buf, first, last):
                for c in range(CHUNKS):
                    s = n * CHUNKS + c
                    if c == 0:
                        pool.wait_ge(f["comb_loaded"][buf], 2 * loads(n, buf))
                    if h or not first or c > 1:
                        pool.wait_ge(f["act_ready"], s - 1)
                    pool.wait_ge(f["gated_ready"], s + 1)
                    pool.tensor_tensor(gated_comb[:, c, :], gated[:, c, :], comb[:, buf, c * BANK:(c + 1) * BANK],
                                       ALU.mult).then_inc(f["gated_comb_ready"], 1)
                    if last and h == 1:
                        continue
                    if c == 0:
                        hold(pool, f["w_loaded"][1 - buf], loads(n + 1, 1 - buf))
                        split(n + 1, 1 - buf, slice(0, WD), f["gu_split"], 2 * n + 3)
                    elif c == 1:
                        split(n + 1, 1 - buf, slice(WD, WF), f["d_split"], 2 * n + 4)

            pool.wait_ge(f["w_loaded"][0], 16)
            split(0, 0, slice(0, WD), f["gu_split"], 1)
            split(0, 0, slice(WD, WF), f["d_split"], 2)
            hidden_tiles(pool, f, tile, lambda h: None)

        def experts_scalar(f):
            act = nc.scalar
            act.wait_ge(f["logits_ready"], 1)
            logits = psum[:, Y_BANK, 0:TILES * f["experts"]].rearrange("p (i e) -> p i e", e=f["experts"])
            if f["top"] == 6:
                act.activation(score[:, :, 0:f["experts"]], logits, ACT.Sigmoid).then_inc(f["score_ready"], 1)
            else:
                act.wait_ge(f["shifted"], 1)
                act.activation(score[:, :, 0:f["experts"]], weight[:, :, 0:f["experts"]], ACT.Exp).then_inc(f["score_ready"], 1)
            for b in range(TILES // 4):
                act.wait_ge(f["combT_ready"], b + 1)
                act.activation(combT[0:f["experts"], b * BANK:(b + 1) * BANK], psum[0:f["experts"], b, :], ACT.Copy).then_inc(f["combT_copied"], 1)

            def tile(h, j, n, buf, first, last):
                for c in range(CHUNKS):
                    s = n * CHUNKS + c
                    if h or not first:
                        act.wait_ge(f["gated_comb_ready"], s - 1)
                    act.wait_ge(f["g_ready"], s + 1)
                    act.activation(gated[:, c, :], psum[:, G_BANK + c, :], ACT.Silu).then_inc(f["gated_ready"], 1)
                    act.wait_ge(f["act_ready"], s + 1)
                    act.activation(act_hi[:, c, :], act_sb[:, c, :], ACT.Copy).then_inc(f["act_hi_ready"], 1)

            def tail(h):
                act.wait_ge(f["down_done"], (h + 1) * f["tiles"] * CHUNKS)
                for b in range(DC * CHUNKS):
                    d, c = divmod(b, CHUNKS)
                    if h:
                        act.wait_ge(f["yT_ready"], DC * CHUNKS)
                    act.activation(yT[:, d, c * BANK:(c + 1) * BANK], psum[:, Y_BANK + b, :], ACT.Copy).then_inc(f["y_copied"], 1)

            hidden_tiles(act, f, tile, tail)

        def experts_vector(f):
            dve = nc.vector
            steps = [0]

            def step(ins):
                steps[0] += 1
                ins.then_inc(f["gate_step"], 1)
                dve.wait_ge(f["gate_step"], steps[0])

            def per_row(t):
                return t.rearrange("p (i a) -> p i a", a=1)

            e = f["experts"]
            logits = psum[:, Y_BANK, 0:TILES * e].rearrange("p (i e) -> p i e", e=e)
            dve.wait_ge(f["logits_ready"], 1)
            dve.wait_ge(f["sentinels"], 2)
            if f["top"] == 6:
                dve.wait_ge(f["score_ready"], 1)
                step(dve.tensor_scalar(choice[:, :, 0:e], logits, 16.636, -88.0, ALU.min, ALU.max))
                wide = SEL
            else:
                step(dve.tensor_copy(logit[:, :, 0:e], logits))
                step(dve.tensor_reduce(row_stat[:], logit[:, :, 0:e], AX.X, ALU.max))
                dve.tensor_tensor(weight[:, :, 0:e], logit[:, :, 0:e], per_row(row_stat[:]).to_broadcast([P, TILES, e]),
                                  ALU.subtract).then_inc(f["shifted"], 1)
                groups = group_choice[:, :, 0:f["groups"]]
                step(dve.tensor_reduce(groups, logit[:, :, 0:e].rearrange("p i (g m) -> p i g m", g=f["groups"]), AX.X, ALU.max))
                for i in range(TILES):
                    last = dve.max(group_top8[:, i, :], group_choice[:, i, :])
                step(last)
                step(dve.memset(group_top8[:, :, f["top_groups"]:8], SENTINEL))
                for i in range(TILES):
                    last = dve.match_replace(group_chosen[:, i, :], group_top8[:, i, :], group_choice[:, i, :], TAKEN)
                step(last)
                step(dve.tensor_scalar(groups, group_chosen[:, :, 0:f["groups"]], TAKEN, None, ALU.is_equal))
                step(dve.tensor_scalar(group_chosen[:, :, 0:f["groups"]], groups, -OUT, OUT, ALU.mult, ALU.add))
                size = e // f["groups"]
                step(dve.tensor_tensor(choice[:, :, 0:e].rearrange("p i (g m) -> p i g m", g=f["groups"]),
                                       logit[:, :, 0:e].rearrange("p i (g m) -> p i g m", g=f["groups"]),
                                       group_chosen[:, :, 0:f["groups"]].rearrange("p i (g a) -> p i g a", a=1).to_broadcast([P, TILES, f["groups"], size]),
                                       ALU.add))
                dve.wait_ge(f["score_ready"], 1)
                step(dve.tensor_reduce(row_stat[:], score[:, :, 0:e], AX.X, ALU.add))
                step(dve.reciprocal(row_stat[:], row_stat[:]))
                step(dve.tensor_tensor(score[:, :, 0:e], score[:, :, 0:e], per_row(row_stat[:]).to_broadcast([P, TILES, e]), ALU.mult))
                wide = e + 8
            for i in range(TILES):
                last = dve.max(top8[:, i, :], choice[:, i, 0:wide])
            step(last)
            step(dve.memset(top8[:, :, f["top"]:8], SENTINEL))
            for i in range(TILES):
                last = dve.match_replace(chosen[:, i, 0:wide], top8[:, i, :], choice[:, i, 0:wide], TAKEN)
            step(last)
            step(dve.tensor_scalar(weight[:, :, 0:e], chosen[:, :, 0:e], TAKEN, None, ALU.is_equal))
            step(dve.tensor_tensor(weight[:, :, 0:e], weight[:, :, 0:e], score[:, :, 0:e], ALU.mult))
            step(dve.tensor_reduce(row_stat[:], weight[:, :, 0:e], AX.X, ALU.add))
            step(dve.tensor_scalar(row_stat[:], row_stat[:], 1e-20, None, ALU.add))
            step(dve.reciprocal(row_stat[:], row_stat[:]))
            dve.tensor_tensor(comb_tok[:, :, 0:e], weight[:, :, 0:e], per_row(row_stat[:]).to_broadcast([P, TILES, e]),
                              ALU.mult).then_inc(f["comb_ready"], 1)

            def tile(h, j, n, buf, first, last):
                for c in range(CHUNKS):
                    s = n * CHUNKS + c
                    dve.wait_ge(f["u_ready"], s + 1)
                    if h or not first:
                        dve.wait_ge(f["act_hi_ready"], s - 1)
                    dve.wait_ge(f["gated_comb_ready"], s + 1)
                    dve.tensor_tensor(act_sb[:, c, :], psum[:, U_BANK + c, :], gated_comb[:, c, :], ALU.mult).then_inc(f["act_ready"], 1)
                    dve.wait_ge(f["act_hi_ready"], s + 1)
                    dve.tensor_tensor(act_lo[:, c, :], act_sb[:, c, :], act_hi[:, c, :].bitcast(F32), ALU.subtract).then_inc(f["act_lo_ready"], 1)

            def tail(h):
                for b in range(4):
                    dve.wait_ge(f["yT_ready"], 4 * h + b + 1)
                    rows = x[:, h * TILES // 2 + 2 * b:h * TILES // 2 + 2 * b + 2, :]
                    dve.tensor_tensor(rows, psum[:, b, :].rearrange("p (i d) -> p i d", i=2), rows, ALU.add).then_inc(f["y_added"], 1)

            hidden_tiles(dve, f, tile, tail)

        def experts_tensor(f):
            pe = nc.tensor
            pe.wait_ge(f["gate_split"], 1)
            pe.wait_ge(lnT_lo, (f["norm"] + 1) * LNT)
            e = f["experts"]
            for i in range(TILES):
                pairs = []
                for c in range(DC):
                    t, w = slice(i * P, (i + 1) * P), slice(c * e, (c + 1) * e)
                    pairs += passes(xT_hi[:, c, t], xT_lo[:, c, t], gate_hi[:, w], gate_lo[:, w])
                last = chain(psum[:, Y_BANK, i * e:(i + 1) * e], pairs)
            last.then_inc(f["logits_ready"], 1)
            pe.wait_ge(f["comb_ready"], 1)
            for i in range(TILES):
                last = pe.transpose(psum[0:e, i // 4, i % 4 * P:(i % 4 + 1) * P], comb_tok[:, i, 0:e], ident[:])
                if i % 4 == 3:
                    last.then_inc(f["combT_ready"], 1)

            def down(n, c, buf, first, last_tile):
                s = n * CHUNKS + c
                if c == 0:
                    pe.wait_ge(f["d_split"], n + 1)
                for lows in range(2):
                    pe.wait_ge((f["act_lo_ready"] if lows else f["act_hi_ready"]), s + 1)
                    for d in range(DC):
                        w = slice(WD + d * P, WD + (d + 1) * P)
                        pairs = passes(fw_hi[:, buf, w], fw_lo[:, buf, w], act_hi[:, c, :], act_lo[:, c, :])
                        pairs = (pairs[0], pairs[2]) if not lows else pairs[1:2]
                        last = chain(psum[:, Y_BANK + d * CHUNKS + c, :], pairs, start=first and lows == 0, stop=last_tile and lows == 1,
                                     skip_group_check=True)
                last.then_inc(f["down_done"], 1)

            def tile(h, j, n, buf, first, last):
                for c in range(CHUNKS):
                    s = n * CHUNKS + c
                    if c == 0:
                        pe.wait_ge(f["gu_split"], n + 1)
                    if first and h == 0 and c == 0:
                        pe.wait_ge(f["combT_copied"], TILES // 4)
                    if first and h == 1 and c == 0:
                        pe.wait_ge(f["y_added"], 4)
                        pe.wait_ge(f["y_copied"], DC * CHUNKS)
                    if h or not first:
                        pe.wait_ge(f["gated_ready"], s - 1)
                    for w0, bank, ready in ((WG, G_BANK, f["g_ready"]), (WU, U_BANK, f["u_ready"])):
                        if w0 == WU and (h or not first):
                            pe.wait_ge(f["act_ready"], s - 1)
                        pairs = []
                        for k in range(DC):
                            w = slice(w0 + k * P, w0 + (k + 1) * P)
                            t = bass.ds(h * HALF + c * BANK, BANK)
                            pairs += passes(fw_hi[:, buf, w], fw_lo[:, buf, w], xT_hi[:, k, t], xT_lo[:, k, t])
                        chain(psum[:, bank + c, :], pairs).then_inc(ready, 1)
                    if c > 0:
                        down(n, c - 1, buf, first, last)
                    elif not first:
                        down(n - 1, CHUNKS - 1, 1 - buf, isinstance(j, int) and j == 1, False)

            def tail(h):
                down((h + 1) * f["tiles"] - 1, CHUNKS - 1, ((h + 1) * f["tiles"] - 1) % 2, False, True)
                pe.wait_ge(f["y_copied"], (h + 1) * DC * CHUNKS)
                for b in range(4):
                    for i in range(2):
                        for d in range(DC):
                            t = 2 * b + i
                            last = pe.transpose(psum[:, b, (i * DC + d) * P:(i * DC + d + 1) * P], yT[:, d, t * P:(t + 1) * P], ident[:])
                    last.then_inc(f["yT_ready"], 1)

            hidden_tiles(pe, f, tile, tail)

        r = Region(keep.at)
        in_hi, in_lo = r("in_hi", [P, DC, MJ * P], F32R), r("in_lo", [P, DC, MJ * P], F32R)
        ow_hi, ow_lo = r("ow_hi", [P, EJ, D], F32R), r("ow_lo", [P, EJ, D], F32R)
        raw = Region(r.at)
        in_raw, ow_raw = raw("in_raw", [P, DC, MJ * P]), raw("ow_raw", [P, EJ, D])
        h_hi, h_lo = r("h_hi", [P, 2, 2, E], F32R), r("h_lo", [P, 2, 2, E], F32R)
        cols = r("cols", [P, CJ * (TAPS + 1) + 2 * EJ + 2])
        start_row = r("start_row", [P, 2, 3, P])
        ones_col, a_col = r("ones_col", [P, 1]), r("a_col", [P, 1])
        conv = r("conv", [P, 2, CJ, PT])
        dt = r("dt", [NH, PT])
        ROW = 3 * P
        rows = r("rows", [NH, 2, ROW])
        neg_abs = rows[:].rearrange("h b c -> h (b c)")[:, 0:PT]
        RING = 3
        decay_all = r("decay_all", [P, RING, 2 * ROW])
        dt_tok = r("dt_tok", [P, 4, NH])
        silu_gate = r("silu_gate", [P, 2, PT])
        h_tok = r("h_tok", [P, 2, 4, E])
        gram = r("gram", [P, 2, 2, ROW])
        MIXES = 4
        mix = r("mix", [P, MIXES, 2, ROW])
        mix_hi, mix_lo = r("mix_hi", [P, 2, 2, SEQ], F32R), r("mix_lo", [P, 2, 2, SEQ], F32R)
        y = r("y", [P, 2, PT])
        square, square_sum = r("square", [P, PT]), r("square_sum", [P, PT])
        y_hi, y_lo = r("y_hi", [P, EJ, PT], F32R), r("y_lo", [P, EJ, PT], F32R)
        mean_sq, rms, rms_tmp = (r(n, [P, 4]) for n in ("mean_sq", "rms", "rms_tmp"))
        decay_dram = dram("decay_dram", [PAIRS, NH, 2 * ROW])

        tap = lambda j, k: cols[:, j * (TAPS + 1) + k:j * (TAPS + 1) + k + 1]
        at = CJ * (TAPS + 1)
        skip_col = lambda j: cols[:, at + j:at + j + 1]
        norm_col = lambda j: cols[:, at + EJ + j:at + EJ + j + 1]
        dt_bias, a_log = cols[0:NH, at + 2 * EJ:at + 2 * EJ + 1], cols[0:NH, at + 2 * EJ + 1:at + 2 * EJ + 2]

        names = ("in_loaded ow_loaded cols_loaded in_hi_done in_split ow_scaled ow_split start_ready a_exp a_ready proj_ready bank_read0 bank_read1 bank_read2 "
                 "z_step z_ready exp_ready log_ready dt_ready decay_ready rows_ready rows_stored decay_loaded0 decay_loaded1 "
                 "decay_loaded2 dtT_ready dt_tok_ready tap_ready tap_step conv_ready gram_ready gram_copied hT_ready h_tok_ready "
                 "h_hi_ready h_lo_ready since_ready mix_ready mix_hi_ready mix_lo_ready yT_ready y_ready gated_ready "
                 "square_ready square_added y_hi_ready y_lo_ready sum_ready mean_ready rms_root root_step out_ready out_added").split()
        m = {n: sem(f"ssm_{n}") for n in names}
        bank_read = m["bank_read0"], m["bank_read1"], m["bank_read2"]
        decay_loaded = m["decay_loaded0"], m["decay_loaded1"], m["decay_loaded2"]
        PROJ_BANKS, GRAM_BANK, YT_BANK = (0, 1, 5), 3, 6
        HT_BANKS = OUT_BANKS = 4, 2
        DT_COL, SUM_COL = 3 * P, 3 * P + 4 * NH
        HEADS_ALL = PAIRS * NH
        GATES = HEADS_ALL // 2
        TI_H, TI_B, TI_C, TI_DT = EJ, 2 * EJ, 2 * EJ + 1, 2 * EJ + 2

        def ssm_schedule():
            ahead = {0: (TI_DT,), 1: (TI_B, TI_C), 2: (TI_H, TI_H + 1), 3: (TI_H + 2,), 4: (TI_H + 3,)}
            gates = (3, 0, 0), (5, 0, 1), (6, 0, 2), (0, 1, 3)
            steps, k, n = [], 0, 0
            for g in range(-1, HEADS_ALL + 8):
                p, hd = divmod(g, NH)
                if g < 0:
                    want = [(0, i) for i in (TI_DT, TI_B, TI_C, TI_H, TI_H + 1, TI_H + 2, TI_H + 3)]
                else:
                    want = [(p + 1, i) for i in ahead.get(hd, ()) if p + 1 < PAIRS]
                    want += [(p - back, w) for at_hd, back, w in gates if at_hd == hd and 0 <= p - back < PAIRS]
                jobs = []
                for q, i in want:
                    conved = TI_H <= i < TI_DT
                    jobs.append((k, q, i, n if conved else None))
                    k, n = k + 1, n + conved
                steps.append((g, jobs))
            return steps

        gate_job = [job for _, jobs in ssm_schedule() for job in jobs if job[2] < EJ]

        def token_tiles(g):
            if g < 0:
                return 0, (0, 1, 2, 3)
            p, hd = divmod(g, NH)
            return p + 1, (0, 1, 2, 3) if hd == NH - 1 and p + 1 < PAIRS else ()

        def split_batches(g):
            q, hd = divmod(g + (g < 0), NH)
            return q, range(2) if q < PAIRS and hd == 0 and (q == 0) == (g < 0) else ()

        def convs(p, i):
            return p * CJ + (TI_B, TI_C, TI_H, TI_H + 1, TI_H + 2, TI_H + 3).index(i) + 1

        def ssm_sync(free, count):
            sp = nc.sync
            sp.wait_ge(free, count)
            sp.dma_start(in_raw[:], in_w).then_inc(m["in_loaded"], 16)
            sp.dma_start(cols[:], ssm_cols).then_inc(m["cols_loaded"], 16)
            sp.dma_start(ow_raw[:], out_w).then_inc(m["ow_loaded"], 16)
            for p in range(PAIRS):
                sp.wait_ge(m["rows_ready"], p + 1)
                sp.dma_start(decay_dram[p], rows[:].rearrange("h b c -> h (b c)")).then_inc(m["rows_stored"], 16)
                sp.wait_ge(m["rows_stored"], 16 * p + 16)
                for hd in range(NH):
                    g = p * NH + hd
                    wait(sp, m["since_ready"], g - RING + 1)
                    sp.dma_start(decay_all[:, g % RING, :], decay_dram[p, hd ^ 1].partition_broadcast(P)).then_inc(decay_loaded[g % RING], 16)

        def ssm_pool(free, count):
            pool = nc.gpsimd
            pool.wait_ge(free, count)
            for b in range(2):
                pool.memset(start_row[:, b, 1, :], 0.0)
                for i in (0, 2):
                    pool.tensor_copy(start_row[:, b, i, :], ident[:])
            pool.memset(ones_col[:], 1.0).then_inc(m["start_ready"], 1)
            pool.wait_ge(m["in_hi_done"], 1)
            pool.tensor_tensor(in_lo[:], in_raw[:], in_hi[:].bitcast(F32), ALU.subtract).then_inc(m["in_split"], 1)
            pool.wait_ge(m["in_hi_done"], 2)
            pool.tensor_tensor(ow_lo[:], ow_raw[:], ow_hi[:].bitcast(F32), ALU.subtract).then_inc(m["ow_split"], 1)
            pool.wait_ge(m["ow_split"], 1)
            for g, _ in ssm_schedule():
                if 0 <= g - 1 < HEADS_ALL:
                    pool.wait_ge(m["mix_hi_ready"], g)
                    wait(pool, m["yT_ready"], g - 2)
                    pool.tensor_tensor(mix_lo[:, (g - 1) % 2], mix[:, (g - 1) % MIXES, :, 0:SEQ], mix_hi[:, (g - 1) % 2].bitcast(F32),
                                       ALU.subtract).then_inc(m["mix_lo_ready"], 1)
                if 0 <= g < HEADS_ALL:
                    p = g // NH
                    pool.wait_ge(m["since_ready"], g + 1)
                    pool.wait_ge(m["gram_copied"], 2 * p + 2)
                    pool.tensor_tensor(mix[:, g % MIXES], mix[:, g % MIXES], gram[:, p % 2], ALU.mult).then_inc(m["mix_ready"], 1)
                w = (g - 4) // 2
                if g % 2 == 0 and 0 <= w < GATES:
                    k, _, _, _ = gate_job[w]
                    pool.wait_ge(bank_read[k % 3], k // 3 + 1)
                    pool.wait_ge(m["y_ready"], w + 1)
                    pool.tensor_tensor(y[:, w % 2, :], y[:, w % 2, :], silu_gate[:, w % 2, :], ALU.mult).then_inc(m["gated_ready"], 1)
                w = (g - 6) // 2
                if g % 2 == 0 and 0 <= w < GATES and w % EJ:
                    p, j = divmod(w, EJ)
                    pool.wait_ge(m["square_ready"], w + 1)
                    pool.wait_ge(m["square_ready"], EJ * p + 1)
                    wait(pool, m["square_added"], (EJ - 1) * p + j - 1)
                    pool.tensor_tensor(square_sum[:], square_sum[:], square[:], ALU.add).then_inc(m["square_added"], 1)
                q, batches = split_batches(g)
                for b in batches:
                    pool.wait_ge(m["h_hi_ready"], 2 * q + b + 1)
                    wait(pool, m["yT_ready"], (q - 1) * NH)
                    pool.tensor_tensor(h_lo[:, q % 2, b, :], h_tok[:, q % 2, 2 * b, :], h_hi[:, q % 2, b, :].bitcast(F32),
                                       ALU.subtract).then_inc(m["h_lo_ready"], 1)

        def ssm_scalar():
            act = nc.scalar
            act.wait_ge(m["cols_loaded"], 16)
            act.activation(a_col[0:NH, :], a_log, ACT.Exp).then_inc(m["a_exp"], 1)
            act.wait_ge(m["in_loaded"], 16)
            act.activation(in_hi[:], in_raw[:], ACT.Copy).then_inc(m["in_hi_done"], 1)
            act.wait_ge(m["ow_scaled"], EJ)
            act.activation(ow_hi[:], ow_raw[:], ACT.Copy).then_inc(m["in_hi_done"], 1)
            act.wait_ge(m["a_ready"], 1)

            def log_steps(q):
                act.wait_ge(m["z_ready"], q + 1)
                act.activation(neg_abs, neg_abs, ACT.Exp).then_inc(m["exp_ready"], 1)
                act.wait_ge(m["exp_ready"], q + 1)
                act.activation(neg_abs, neg_abs, ACT.Ln, bias=1.0).then_inc(m["log_ready"], 1)

            def step_decays(q):
                act.wait_ge(m["dt_ready"], q + 1)
                steps = dt[:].rearrange("h (b t) -> h b t", b=2)
                act.activation(rows[:, :, 0:SEQ], steps, ACT.Exp, scale=a_col[0:NH, :])
                act.activation(rows[:, :, SEQ:ROW], steps[:, :, P:SEQ], ACT.Exp, scale=a_col[0:NH, :]).then_inc(m["decay_ready"], 1)

            def projected(k, q, i, n):
                bank = psum[:, PROJ_BANKS[k % 3], :]
                if n is not None:
                    if q >= 2:
                        act.wait_ge(m["y_ready"], (q - 1) * EJ)
                    act.wait_ge(m["proj_ready"], k + 1)
                    act.activation(conv[:, q % 2, i - EJ, :], bank, ACT.Identity, bias=tap(i - EJ, TAPS),
                                   scale=tap(i - EJ, TAPS - 1)).then_inc(m["tap_ready"], 1)
                elif i < EJ:
                    w = q * EJ + i
                    wait(act, m["gated_ready"], w - 1)
                    act.wait_ge(m["proj_ready"], k + 1)
                    act.activation(silu_gate[:, w % 2, :], bank, ACT.Silu).then_inc(bank_read[k % 3], 1)

            def conv_silu(k, q, i, n):
                if n is not None:
                    act.wait_ge(bank_read[k % 3], k // 3 + 1)
                    act.activation(conv[:, q % 2, i - EJ, :], conv[:, q % 2, i - EJ, :], ACT.Silu).then_inc(m["conv_ready"], 1)

            schedule = ssm_schedule()
            for g, jobs in schedule:
                if g < 0:
                    log_steps(0)
                    step_decays(0)
                    for job in jobs:
                        projected(*job)
                        conv_silu(*job)
                if g >= 1:
                    for job in schedule[g][1]:
                        projected(*job)
                p, hd = divmod(g, NH)
                if 0 <= p < PAIRS - 1 and hd == 5:
                    step_decays(p + 1)
                if g >= 14 and (g - 14) % NH == 0:
                    act.wait_ge(m["mean_ready"], (g - 14) // NH + 1)
                    act.activation(rms[:], mean_sq[:], ACT.Sqrt).then_inc(m["rms_root"], 1)
                if g >= 2:
                    for job in schedule[g - 1][1]:
                        conv_silu(*job)
                if 0 <= g < HEADS_ALL:
                    act.wait_ge(m["mix_ready"], g + 1)
                    wait(act, m["yT_ready"], g - 1)
                    act.activation(mix_hi[:, g % 2], mix[:, g % MIXES, :, 0:SEQ], ACT.Copy).then_inc(m["mix_hi_ready"], 1)
                q, tiles = token_tiles(g)
                for b in range(2 if tiles else 0):
                    act.wait_ge(m["gram_ready"], 2 * q + b + 1)
                    wait(act, m["mix_ready"], (q - 1) * NH)
                    act.activation(gram[:, q % 2, b], psum[:, GRAM_BANK, 0:ROW], ACT.Copy).then_inc(m["gram_copied"], 1)
                q, batches = split_batches(g)
                for b in batches:
                    act.wait_ge(m["h_tok_ready"], 4 * q + 2 * b + 1)
                    if q == 0 and b == 0:
                        act.wait_ge(m["in_split"], 1)
                        act.wait_ge(m["ow_split"], 1)
                    wait(act, m["yT_ready"], (q - 1) * NH)
                    act.activation(h_hi[:, q % 2, b, :], h_tok[:, q % 2, 2 * b, :], ACT.Copy).then_inc(m["h_hi_ready"], 1)
                p, hd = divmod(g, NH)
                if 0 <= p < PAIRS - 1 and hd == 4:
                    log_steps(p + 1)
                w = (g - 5) // 2
                if g % 2 and 0 <= w < GATES:
                    p, j = divmod(w, EJ)
                    act.wait_ge(m["gated_ready"], w + 1)
                    if j == 0:
                        wait(act, m["out_ready"], 2 * p)
                        wait(act, m["sum_ready"], p)
                        act.activation(square_sum[:], y[:, w % 2, :], ACT.Square).then_inc(m["square_ready"], 1)
                    else:
                        wait(act, m["square_added"], (EJ - 1) * p + j - 1)
                        act.activation(square[:], y[:, w % 2, :], ACT.Square).then_inc(m["square_ready"], 1)
                    act.activation(y_hi[:, j, :], y[:, w % 2, :], ACT.Copy).then_inc(m["y_hi_ready"], 1)

        def ssm_vector():
            dve = nc.vector
            dve.wait_ge(m["a_exp"], 1)
            dve.tensor_scalar(a_col[0:NH, :], a_col[0:NH, :], -1.0, None, ALU.mult).then_inc(m["a_ready"], 1)
            dve.wait_ge(m["ow_loaded"], 16)
            for j in range(EJ):
                dve.tensor_scalar(ow_raw[:, j, :], ow_raw[:, j, :], norm_col(j), None, ALU.mult).then_inc(m["ow_scaled"], 1)
            dve.wait_ge(m["start_ready"], 1)

            def decays(g):
                dve.wait_ge(decay_loaded[g % RING], 16 * (g // RING) + 16)
                wait(dve, m["yT_ready"], g - MIXES + 1)
                wait(dve, m["mix_lo_ready"], g - MIXES + 1)
                dve.tensor_tensor_scan(mix[:, g % MIXES].rearrange("p b c -> p (b c)"), decay_all[:, g % RING, :],
                                       start_row[:].rearrange("p b i c -> p (b i c)"), 0.0, ALU.mult, ALU.add).then_inc(m["since_ready"], 1)

            def outputs(w):
                p, j = divmod(w, EJ)
                dve.wait_ge(m["yT_ready"], 2 * w + 2)
                wait(dve, m["y_lo_ready"], w - 1)
                dve.scalar_tensor_tensor(y[:, w % 2, :], conv[:, p % 2, j, :], skip_col(j), psum[:, YT_BANK + w % 2, :],
                                         ALU.mult, ALU.add).then_inc(m["y_ready"], 1)

            def steps_dt(k, q):
                bank = psum[0:NH, PROJ_BANKS[k % 3], :]
                dve.wait_ge(m["proj_ready"], k + 1)
                wait(dve, m["dtT_ready"], q)
                wait(dve, m["decay_ready"], q)
                dve.tensor_scalar(dt[:], bank, dt_bias, None, ALU.add).then_inc(bank_read[k % 3], 1)
                dve.wait_ge(bank_read[k % 3], k // 3 + 1)
                wait(dve, m["rows_stored"], 16 * q)
                dve.tensor_scalar(neg_abs, dt[:], -1.0, None, ALU.mult).then_inc(m["z_step"], 1)
                dve.wait_ge(m["z_step"], q + 1)
                dve.tensor_tensor(neg_abs, neg_abs, dt[:], ALU.min).then_inc(m["z_ready"], 1)

            def steps_sum(q):
                dve.wait_ge(m["log_ready"], q + 1)
                dve.scalar_tensor_tensor(dt[:], dt[:], 0.0, neg_abs, ALU.max, ALU.add).then_inc(m["dt_ready"], 1)

            def starts(q):
                dve.wait_ge(m["decay_ready"], q + 1)
                dve.memset(rows[:].rearrange("h b (i c) -> h b i c", i=3)[:, :, 0:3:2, 0:1], 0.0).then_inc(m["rows_ready"], 1)

            def taps(k, q, i, n):
                dve.wait_ge(m["tap_ready"], n + 1)
                for e in range(1, TAPS):
                    to = conv[:, q % 2, i - EJ, :].rearrange("p (b t) -> p b t", b=2)[:, :, e:SEQ]
                    of = psum[:, PROJ_BANKS[k % 3], :].rearrange("p (b t) -> p b t", b=2)[:, :, 0:SEQ - e]
                    ins = dve.scalar_tensor_tensor(to, of, tap(i - EJ, TAPS - 1 - e), to, ALU.mult, ALU.add)
                    if e < TAPS - 1:
                        ins.then_inc(m["tap_step"], 1)
                        dve.wait_ge(m["tap_step"], n * (TAPS - 2) + e)
                ins.then_inc(bank_read[k % 3], 1)

            def projected(k, q, i, n):
                if i == TI_DT:
                    steps_dt(k, q)
                elif n is not None:
                    taps(k, q, i, n)

            schedule = ssm_schedule()
            for g, jobs in schedule:
                p, hd = divmod(g, NH)
                if 0 <= p < PAIRS - 1 and hd == 5:
                    steps_sum(p + 1)
                e, rest = divmod(g - 14, NH)
                if e >= 0 and rest == 0:
                    dve.wait_ge(m["sum_ready"], e + 1)
                    dve.tensor_scalar(mean_sq[:], psum[:, GRAM_BANK, SUM_COL:SUM_COL + 4], 1.0 / E, SSM_EPS, ALU.mult, ALU.add) \
                        .then_inc(m["mean_ready"], 1)
                if 0 <= g < HEADS_ALL:
                    decays(g)
                if g < 0:
                    for job in jobs:
                        projected(*job)
                        if job[2] == TI_DT:
                            steps_sum(0)
                            starts(0)
                if g >= 1:
                    for job in schedule[g][1]:
                        projected(*job)
                p, hd = divmod(g, NH)
                if 0 <= p < PAIRS - 1 and hd == 5:
                    starts(p + 1)
                if g % 2 and 0 <= (g - 3) // 2 < GATES:
                    outputs((g - 3) // 2)
                w = (g - 6) // 2
                if g % 2 == 0 and 0 <= w < GATES:
                    dve.wait_ge(m["y_hi_ready"], w + 1)
                    dve.tensor_tensor(y_lo[:, w % EJ, :], y[:, w % 2, :], y_hi[:, w % EJ, :].bitcast(F32), ALU.subtract).then_inc(m["y_lo_ready"], 1)
                if g < 0 or p < PAIRS - 1 and hd == 6:
                    q = max(p + 1, 0)
                    dve.wait_ge(m["dtT_ready"], q + 1)
                    dve.tensor_copy(dt_tok[:], psum[:, GRAM_BANK, DT_COL:SUM_COL].rearrange("p (t h) -> p t h", h=NH)).then_inc(m["dt_tok_ready"], 1)
                q, tiles = token_tiles(g)
                for t in tiles:
                    if t == 0:
                        dve.wait_ge(m["dt_tok_ready"], q + 1)
                    dve.wait_ge(m["hT_ready"], 4 * q + t + 1)
                    wait(dve, m["yT_ready"], (q - 1) * NH)
                    wait(dve, m["h_lo_ready"], 2 * (q - 1))
                    dve.tensor_tensor(h_tok[:, q % 2, t, :].rearrange("p (h c) -> p h c", h=NH),
                                      psum[:, HT_BANKS[t % 2], :].rearrange("p (h c) -> p h c", h=NH),
                                      dt_tok[:, t, :].rearrange("p (h a) -> p h a", a=1).to_broadcast([P, NH, HP]), ALU.mult).then_inc(m["h_tok_ready"], 1)
                e, rest = divmod(g - 14, NH)
                if e >= 0 and rest == 0:
                    dve.wait_ge(m["rms_root"], e + 1)
                    inverse_root(rms[:], mean_sq[:], rms_tmp[:], m["root_step"], ROOT_STEPS * e)
                    for t in range(4):
                        if t % 2 == 0:
                            dve.wait_ge(m["out_ready"], 2 * e + t // 2 + 1)
                        dve.scalar_tensor_tensor(x[:, 4 * e + t, :], psum[:, OUT_BANKS[t // 2], t % 2 * D:(t % 2 + 1) * D], rms[:, t:t + 1],
                                                 x[:, 4 * e + t, :], ALU.mult, ALU.add).then_inc(m["out_added"], 1)

        def ssm_tensor():
            pe = nc.tensor
            pe.wait_ge(lnT_lo, 2 * LNT)
            pe.wait_ge(m["in_split"], 1)
            pe.wait_ge(m["start_ready"], 1)

            def products(g):
                p, hd = divmod(g, NH)
                if hd == 0:
                    pe.wait_ge(m["h_tok_ready"], 4 * p + 4)
                    pe.wait_ge(m["h_lo_ready"], 2 * p + 2)
                wait(pe, m["y_ready"], g // 2 - 1)
                pe.wait_ge(m["mix_lo_ready"], g + 1)
                for b in range(2):
                    n = HP if hd % 2 else 2 * HP
                    c = slice(hd // 2 * 2 * HP, hd // 2 * 2 * HP + n)
                    to = psum[0:n, YT_BANK + g // 2 % 2, b * SEQ:(b + 1) * SEQ]
                    chain(to, passes(h_hi[:, p % 2, b, c], h_lo[:, p % 2, b, c], mix_hi[:, g % 2, b, :], mix_lo[:, g % 2, b, :]),
                          stop=False, skip_group_check=True)
                    last = pe.matmul(to[:, P:SEQ], h_tok[:, p % 2, 2 * b + 1, c], mix[:, g % MIXES, b, SEQ:ROW],
                                     start=False, stop=True, skip_group_check=True)
                last.then_inc(m["yT_ready"], 1)

            def squares(p):
                pe.wait_ge(m["square_added"], (EJ - 1) * (p + 1))
                for t in range(4):
                    last = pe.matmul(psum[:, GRAM_BANK, SUM_COL + t:SUM_COL + t + 1], square_sum[:, t * P:(t + 1) * P], ones_col[:],
                                     start=True, stop=True)
                last.then_inc(m["sum_ready"], 1)

            def project_out(p):
                pe.wait_ge(m["y_lo_ready"], EJ * p + EJ)
                pe.wait_ge(m["ow_split"], 1)
                pe.wait_ge(m["h_tok_ready"], 4 * min(p + 2, PAIRS))
                wait(pe, m["out_added"], 4 * p)
                for t in range(4):
                    pairs = []
                    for j in range(EJ):
                        s = slice(t * P, (t + 1) * P)
                        pairs += passes(y_hi[:, j, s], y_lo[:, j, s], ow_hi[:, j, :], ow_lo[:, j, :])
                    last = chain(psum[:, OUT_BANKS[t // 2], t % 2 * D:(t % 2 + 1) * D], pairs)
                    if t % 2:
                        last.then_inc(m["out_ready"], 1)

            def turn_steps(q):
                pe.wait_ge(m["dt_ready"], q + 1)
                wait(pe, m["mean_ready"], q - 1)
                for i in range(4):
                    last = pe.transpose(psum[:, GRAM_BANK, DT_COL + i * NH:DT_COL + (i + 1) * NH], dt[:, i * P:(i + 1) * P], ident[0:NH, 0:NH])
                last.then_inc(m["dtT_ready"], 1)

            def turns(q):
                pe.wait_ge(m["conv_ready"], convs(q, TI_H + EJ - 1))
                wait(pe, m["out_added"], 4 * (q - 1))
                for b in range(2):
                    if b == 0:
                        pe.wait_ge(m["dt_tok_ready"], q + 1)
                    else:
                        pe.wait_ge(m["gram_copied"], 2 * q + 1)
                    for i in range(2):
                        keys = conv[0:NS, q % 2, EJ, b * SEQ + i * P:b * SEQ + (i + 1) * P]
                        later = conv[0:NS, q % 2, EJ + 1, b * SEQ + i * P:(b + 1) * SEQ]
                        last = pe.matmul(psum[:, GRAM_BANK, 2 * i * P:(2 + i) * P], keys, later, start=True, stop=True)
                    last.then_inc(m["gram_ready"], 1)
                    for t in (2 * b, 2 * b + 1):
                        wait(pe, m["h_tok_ready"], 4 * q + t - 1)
                        for j in range(EJ):
                            last = pe.transpose(psum[:, HT_BANKS[t % 2], j * P:(j + 1) * P], conv[:, q % 2, j, t * P:(t + 1) * P], ident[:])
                        last.then_inc(m["hT_ready"], 1)

            def project(k, q, i, n):
                wait(pe, bank_read[k % 3], k // 3)
                pairs = []
                for c in range(DC):
                    v, t = slice(i * P, (i + 1) * P), slice(q * PT, (q + 1) * PT)
                    pairs += passes(in_hi[:, c, v], in_lo[:, c, v], xT_hi[:, c, t], xT_lo[:, c, t])
                chain(psum[:, PROJ_BANKS[k % 3], :], pairs).then_inc(m["proj_ready"], 1)

            for g, jobs in ssm_schedule():
                q, tiles = token_tiles(g)
                if tiles and g >= 0:
                    turns(q)
                p, rest = divmod(g - 13, NH)
                if p >= 0 and rest == 0:
                    squares(p)
                    project_out(p)
                for job in jobs[:1]:
                    project(*job)
                if 0 <= g - 1 < HEADS_ALL:
                    products(g - 1)
                for job in jobs[1:]:
                    project(*job)
                if g < 0:
                    turn_steps(0)
                    turns(0)
                p, hd = divmod(g, NH)
                if 0 <= p < PAIRS - 1 and hd == 6:
                    turn_steps(p + 1)

        block = ctx.enter_context(nc.Block())

        @block.sync
        def _(sp):
            for q in range(PAIRS):
                sp.dma_start(xT_raw[:, :, q * BANK:(q + 1) * BANK],
                             x_cols.rearrange("(c p) t -> p c t", p=P)[:, :, q * BANK:(q + 1) * BANK]).then_inc(xT_loaded[q], 16)
                if q == 0:
                    sp.dma_start(aw_raw[:], attn_w[0]).then_inc(aw_loaded, 16)
            sp.dma_start(x[:], x_rows.rearrange("(i p) d -> p i d", p=P)).then_inc(x_loaded, 16)
            with sp.Fori(1, GROUPS) as g:
                sp.wait_ge(aw_split, 4 * g)
                sp.dma_start(aw_raw[:], attn_w[bass.ds(g, 1)].rearrange("a p n -> p (a n)")).then_inc(aw_loaded, 16)
            experts_sync(expert_layers[0], o_added, GROUPS * 2 * PAIRS)
            ssm_sync(expert_layers[0]["y_added"], 8)
            experts_sync(expert_layers[1], m["out_added"], TILES)
            sp.wait_ge(ln_done, NORMS * TILES)
            sp.dma_start(out.rearrange("(i p) d -> p i d", p=P), x[:]).then_inc(stored, 16)
            sp.wait_ge(stored, 16)

        @block.gpsimd
        def _(pool):
            pool.memset(ident[:], 0.0).then_inc(const_ready, 1)
            pool.memset(causal[:], 0.0).then_inc(const_ready, 1)
            pool.wait_ge(const_ready, 2)
            pool.affine_select(out=ident[:], in_=ident[:], compare_op=ALU.not_equal, fill=1.0, base=0,
                               pattern=[[-1, P]], channel_multiplier=1).then_inc(const_ready, 1)
            pool.affine_select(out=causal[:, P:2 * P], in_=causal[:, P:2 * P], compare_op=ALU.is_ge, fill=MASKED,
                               base=0, pattern=[[-1, P]], channel_multiplier=1).then_inc(const_ready, 1)

            def low_part(g, part):
                pool.wait_ge(aw_hi_done, 4 * g + part + 1)
                w = slice(part * WK, (part + 1) * WK)
                pool.tensor_tensor(aw_lo[:, w], aw_raw[:, w], aw_hi[:, w].bitcast(F32), ALU.subtract).then_inc(aw_split, 1)

            for part in range(4):
                low_part(0, part)
            with pool.Fori(1, GROUPS) as g:
                for part in range(4):
                    low_part(g, part)
            experts_pool(expert_layers[0], o_added, GROUPS * 2 * PAIRS)
            ssm_pool(expert_layers[0]["y_added"], 8)
            experts_pool(expert_layers[1], m["out_added"], TILES)

        @block.scalar
        def _(act):
            def tokens_high(q):
                act.wait_ge(xT_loaded[q], 16)
                act.activation(xT_hi[:, :, q * BANK:(q + 1) * BANK], xT_raw[:, :, q * BANK:(q + 1) * BANK],
                               ACT.Copy).then_inc(xT_hi_ready, 1)

            def high_part(g, part):
                if part == 0:
                    act.wait_ge(aw_loaded, 16 * g + 16)
                w = slice(part * WK, (part + 1) * WK)
                act.activation(aw_hi[:, w], aw_raw[:, w], ACT.Copy).then_inc(aw_hi_done, 1)

            def qkv_high(g, bp, j):
                n = g * (PAIRS * JOBS) + bp * JOBS + j
                act.wait_ge(qkv_ready, n + 1)
                dst = (kT_hi if j % 2 else qT_hi)[:, bp % 2, j // 2, :] if j < 2 * HG else v_hi[:, bp % 2, j - 2 * HG, :]
                act.activation(dst, psum[:, QKV_BANK + j % 2, :], ACT.Copy).then_inc(qkv_hi, 1)

            def group(g, next_group):
                for i, jobs, more_jobs, u_s, u_t, u_v, u_o in attn_schedule(next_group):
                    if i == 2:
                        wait(act, o_ready, g * (2 * PAIRS))
                        high_part(g, 3)
                    if 11 <= i < 14 and next_group:
                        act.wait_ge(qkv_ready, (g + 1) * (PAIRS * JOBS) - (3, 2, 0)[i - 11])
                        high_part(g + 1, i - 11)
                    if u_s is not None:
                        u = u_s
                        act.wait_ge(s_masked, g * UNITS + u + 1)
                        if u >= 3:
                            act.wait_ge(pT_ready, g * UNITS + u - 2)
                        act.activation(p_sb[:, u % 3, 0:P], s_sb[:, u % 2, 0:P], ACT.Exp, bias=neg_max[:, u % 3, 0:1], scale=-1.0,
                                       accum_out=row_sum[:, u % 3, 0:1])
                        act.activation(p_sb[:, u % 3, P:3 * P], s_sb[:, u % 2, P:3 * P], ACT.Exp, bias=neg_max[:, u % 3, 1:2], scale=-1.0,
                                       accum_out=row_sum[:, u % 3, 1:2]).then_inc(p_ready, 1)
                    for bp, j in jobs:
                        qkv_high(g, bp, j)
                    if u_t is not None:
                        u = u_t
                        act.wait_ge(pT_ready, g * UNITS + u + 1)
                        act.activation(pT_hi[:, u % 2, :], psum[:, PT_BANK, 0:3 * P], ACT.Copy).then_inc(pT_hi_ready, 1)
                    if u_v is not None:
                        u = u_v
                        act.wait_ge(z_ready, g * UNITS + u + 1)
                        act.activation(zT_hi[:, u % 2, :], psum[:, Z_BANK, 0:SEQ], ACT.Copy).then_inc(z_hi_ready, 1)
                    for bp, j in more_jobs:
                        qkv_high(g, bp, j)

            tokens_high(0)
            for part in range(3):
                high_part(0, part)
            for j in range(JOBS):
                qkv_high(0, 0, j)
                if j < PAIRS - 1:
                    tokens_high(j + 1)
            group(0, True)
            with act.Fori(1, GROUPS - 1) as g:
                group(g, True)
            group(GROUPS - 1, False)
            ln_scalar(0)
            experts_scalar(expert_layers[0])
            ln_scalar(1)
            ssm_scalar()
            ln_scalar(2)
            experts_scalar(expert_layers[1])
            ln_scalar(3, False)

        @block.vector
        def _(dve):
            def tokens_low(q):
                dve.wait_ge(xT_hi_ready, q + 1)
                dve.tensor_tensor(xT_lo[:, :, q * BANK:(q + 1) * BANK], xT_raw[:, :, q * BANK:(q + 1) * BANK],
                                  xT_hi[:, :, q * BANK:(q + 1) * BANK].bitcast(F32), ALU.subtract).then_inc(xT_lo_ready, 1)

            def qkv_low(g, bp, j):
                n = g * (PAIRS * JOBS) + bp * JOBS + j
                dve.wait_ge(qkv_hi, n + 1)
                if j < 2 * HG:
                    hi, lo = ((kT_hi, kT_lo) if j % 2 else (qT_hi, qT_lo))
                    hi, lo = hi[:, bp % 2, j // 2, :], lo[:, bp % 2, j // 2, :]
                else:
                    hi, lo = v_hi[:, bp % 2, j - 2 * HG, :], v_lo[:, bp % 2, j - 2 * HG, :]
                dve.tensor_tensor(lo, psum[:, QKV_BANK + j % 2, :], hi.bitcast(F32), ALU.subtract).then_inc(qkv_lo, 1)

            def group(g, next_group):
                for i, jobs, more_jobs, u_s, u_t, u_v, u_o in attn_schedule(next_group):
                    if u_s is not None:
                        u = u_s
                        if u >= 2:
                            dve.wait_ge(p_ready, g * UNITS + u - 1)
                        hold(dve, s_ready, g * UNITS + u + 1)
                        dve.tensor_tensor_reduce(s_sb[:, u % 2, 0:P], psum[:, S_BANK + u % 2, 0:P], causal[:, P:2 * P], -SCALE, 3e38,
                                                 ALU.add, ALU.min, neg_max[:, u % 3, 0:1])
                        dve.tensor_tensor_reduce(s_sb[:, u % 2, P:3 * P], psum[:, S_BANK + u % 2, P:3 * P], causal[:], -SCALE, 3e38,
                                                 ALU.add, ALU.min, neg_max[:, u % 3, 1:2]).then_inc(s_masked, 1)
                    if 0 <= i - 1 < UNITS:
                        u = i - 1
                        dve.wait_ge(p_ready, g * UNITS + u + 1)
                        dve.reciprocal(row_inv[:, u % 3, :], row_sum[:, u % 3, :]).then_inc(r_ready, 1)
                        dve.wait_ge(r_ready, g * UNITS + u + 1)
                        dve.tensor_scalar(p_sb[:, u % 3, 0:P], p_sb[:, u % 3, 0:P], row_inv[:, u % 3, 0:1], None, ALU.mult)
                        dve.tensor_scalar(p_sb[:, u % 3, P:3 * P], p_sb[:, u % 3, P:3 * P], row_inv[:, u % 3, 1:2], None,
                                          ALU.mult).then_inc(p_scaled, 1)
                    for bp, j in jobs:
                        qkv_low(g, bp, j)
                    if u_t is not None:
                        u = u_t
                        dve.wait_ge(pT_hi_ready, g * UNITS + u + 1)
                        dve.tensor_tensor(pT_lo[:, u % 2, :], psum[:, PT_BANK, 0:3 * P], pT_hi[:, u % 2, :].bitcast(F32),
                                          ALU.subtract).then_inc(pT_lo_ready, 1)
                    if u_v is not None:
                        u = u_v
                        dve.wait_ge(z_hi_ready, g * UNITS + u + 1)
                        dve.tensor_tensor(zT_lo[:, u % 2, :], psum[:, Z_BANK, 0:SEQ], zT_hi[:, u % 2, :].bitcast(F32),
                                          ALU.subtract).then_inc(z_lo_ready, 1)
                    for bp, j in more_jobs:
                        qkv_low(g, bp, j)
                    if u_o is not None and unit(u_o)[1] == HG - 1:
                        bp, _, b = unit(u_o)
                        dve.wait_ge(o_ready, g * (2 * PAIRS) + 2 * bp + b + 1)
                        rows = x[:, 4 * bp + 2 * b:4 * bp + 2 * b + 2, :]
                        dve.tensor_tensor(rows, psum[:, O_BANK + b, :].rearrange("p (i d) -> p i d", i=2), rows,
                                          ALU.add).then_inc(o_added, 1)

            tokens_low(0)
            for j in range(JOBS):
                qkv_low(0, 0, j)
                if j < PAIRS - 1:
                    tokens_low(j + 1)
            dve.wait_ge(const_ready, 4)
            dve.wait_ge(x_loaded, 16)
            group(0, True)
            with dve.Fori(1, GROUPS - 1) as g:
                group(g, True)
            group(GROUPS - 1, False)
            ln_vector(0, o_added, GROUPS * 2 * PAIRS)
            ln_lows(0)
            experts_vector(expert_layers[0])
            ln_vector(1, expert_layers[0]["y_added"], 8)
            ln_lows(1)
            ssm_vector()
            ln_vector(2, m["out_added"], TILES)
            ln_lows(2)
            experts_vector(expert_layers[1])
            ln_vector(3, expert_layers[1]["y_added"], 8)

        @block.tensor
        def _(pe):
            def qkv_job(g, bp, j):
                n = g * (PAIRS * JOBS) + bp * JOBS + j
                if not isinstance(n, int) or n >= 2:
                    pe.wait_ge(qkv_lo, n - 1)
                if bp % PAIRS == 0 and j in (0, 1, 2 * HG):
                    pe.wait_ge(aw_split, 4 * (g + bp // PAIRS) + (1, 2, 3)[min(j, 2)])
                if bp < PAIRS and j == 0:
                    pe.wait_ge(xT_lo_ready, bp + 1)
                bp %= PAIRS
                bank = psum[:, QKV_BANK + j % 2, :]
                if j < 2 * HG:
                    w0 = (WK if j % 2 else WQ) + j // 2 * DC * DH
                    pairs = []
                    for c in range(DC):
                        w = slice(w0 + c * DH, w0 + (c + 1) * DH)
                        m = slice(bp * BANK, (bp + 1) * BANK)
                        pairs += passes(aw_hi[:, w], aw_lo[:, w], xT_hi[:, c, m], xT_lo[:, c, m])
                    chain(bank, pairs).then_inc(qkv_ready, 1)
                else:
                    for i in range(2):
                        t0 = bp * BANK + (2 * (j - 2 * HG) + i) * P
                        pairs = []
                        for c in range(DC):
                            w = slice(WV + c * HG * DH, WV + (c + 1) * HG * DH)
                            pairs += passes(xT_hi[:, c, t0:t0 + P], xT_lo[:, c, t0:t0 + P], aw_hi[:, w], aw_lo[:, w])
                        last = chain(bank[:, i * HG * DH:(i + 1) * HG * DH], pairs)
                    last.then_inc(qkv_ready, 1)

            def scores(g, u):
                bp, h, b = unit(u)
                pe.wait_ge(qkv_lo, g * (PAIRS * JOBS) + bp * JOBS + 2 * h + 2)
                wait(pe, s_masked, g * UNITS + max(u - 1, 0))
                for i in range(2):
                    s = slice(b * SEQ + i * P, b * SEQ + (i + 1) * P)
                    m = slice(b * SEQ, b * SEQ + (i + 1) * P)
                    q, k = (qT_hi, qT_lo), (kT_hi, kT_lo)
                    last = chain(psum[:, S_BANK + u % 2, i * P:(2 * i + 1) * P], passes(
                        *(t[:, bp % 2, h, s] for t in q), *(t[:, bp % 2, h, m] for t in k)))
                last.then_inc(s_ready, 1)

            def transposes(g, u):
                pe.wait_ge(p_scaled, g * UNITS + u + 1)
                wait(pe, pT_lo_ready, g * UNITS + u)
                for i in range(3):
                    last = pe.transpose(psum[:, PT_BANK, i * P:(i + 1) * P], p_sb[:, u % 3, i * P:(i + 1) * P], ident[:])
                last.then_inc(pT_ready, 1)

            def values(g, u):
                bp, h, b = unit(u)
                pe.wait_ge(pT_lo_ready, g * UNITS + u + 1)
                pe.wait_ge(qkv_lo, g * (PAIRS * JOBS) + (bp + 1) * JOBS)
                wait(pe, z_lo_ready, g * UNITS + u)
                for i in range(2):
                    v = [t[:, bp % 2, b, i * HG * DH + h * DH:i * HG * DH + (h + 1) * DH] for t in (v_hi, v_lo)]
                    p = [t[:, u % 2, 2 * i * P:(2 + i) * P] for t in (pT_hi, pT_lo)]
                    last = chain(psum[:, Z_BANK, i * P:2 * P], passes(*v, *p), start=i == 0, stop=i == 1, skip_group_check=True)
                last.then_inc(z_ready, 1)

            def output(g, u):
                bp, h, b = unit(u)
                pe.wait_ge(z_lo_ready, g * UNITS + u + 1)
                if h == 0:
                    if u == 0:
                        pe.wait_ge(aw_split, 4 * g + 4)
                    wait(pe, o_added, g * (2 * PAIRS) + max(2 * bp + b - 1, 0))
                w = slice(WO + h * D, WO + (h + 1) * D)
                for i in range(2):
                    z = [t[:, u % 2, i * P:(i + 1) * P] for t in (zT_hi, zT_lo)]
                    last = chain(psum[:, O_BANK + b, i * D:(i + 1) * D], passes(*z, aw_hi[:, w], aw_lo[:, w]),
                                 start=h == 0 and i == 0, stop=h == HG - 1, skip_group_check=True)
                if h == HG - 1:
                    last.then_inc(o_ready, 1)

            def group(g, next_group):
                for i, jobs, more_jobs, u_s, u_t, u_v, u_o in attn_schedule(next_group):
                    if u_s is not None:
                        scores(g, u_s)
                    for bp, j in jobs:
                        qkv_job(g, bp, j)
                    if u_t is not None:
                        transposes(g, u_t)
                    if u_v is not None:
                        values(g, u_v)
                    for bp, j in more_jobs:
                        qkv_job(g, bp, j)
                    if u_o is not None:
                        output(g, u_o)

            for j in range(JOBS):
                qkv_job(0, 0, j)
            pe.wait_ge(const_ready, 4)
            group(0, True)
            with pe.Fori(1, GROUPS - 1) as g:
                group(g, True)
            group(GROUPS - 1, False)
            ln_tensor(0)
            experts_tensor(expert_layers[0])
            ln_tensor(1)
            ssm_tensor()
            ln_tensor(2)
            experts_tensor(expert_layers[1])


def lay_out(inputs):
    import numpy as np

    a = {n: np.asarray(v) for n, v in inputs.items()}
    x = a["L0_attn_x"].reshape(T, D)
    def heads(w):
        return w.reshape(GROUPS, HG, DH, DC, P).transpose(0, 4, 1, 3, 2)
    q, k = (heads(a[f"L0_attn_W_{n}"]).reshape(GROUPS, P, -1) for n in "QK")
    v = heads(a["L0_attn_W_V"]).transpose(0, 1, 3, 2, 4).reshape(GROUPS, P, -1)
    o = a["L0_attn_W_O"].reshape(GROUPS, HG, D, DH).transpose(0, 3, 1, 2).reshape(GROUPS, P, -1)
    attn_w = np.concatenate([q, k, v, o], axis=2)

    def hidden_tiles(gate, up, down, layer):
        n = layer["tiles"]
        pad = n * P - layer["hidden"]
        gate, up = (np.pad(w, ((0, 0), (0, pad))).reshape(DC, P, n, P).transpose(2, 1, 0, 3).reshape(n, P, DC * P) for w in (gate, up))
        down = np.pad(down, ((0, pad), (0, 0))).reshape(n, P, D)
        return np.concatenate([gate, up, down], axis=2)

    def cols(w):
        return w.transpose(1, 0, 2).reshape(D, -1)

    l0_w = hidden_tiles(np.concatenate([a["L0_ffn_sg"], cols(a["L0_ffn_wg"])], 1),
                        np.concatenate([a["L0_ffn_su"], cols(a["L0_ffn_wu"])], 1),
                        np.concatenate([a["L0_ffn_sd"], a["L0_ffn_wd"].reshape(-1, D)], 0), L0)
    up = a["L1_ffn_expert_up_w"].transpose(0, 2, 1)
    sh = a["L1_ffn_shared_up_w"].T
    w, s = L1["width"], L1["shared"]
    l1_w = hidden_tiles(np.concatenate([sh[:, :s], cols(up[:, :, :w])], 1),
                        np.concatenate([sh[:, s:], cols(up[:, :, w:])], 1),
                        np.concatenate([a["L1_ffn_shared_down_w"].T, a["L1_ffn_expert_down_w"].transpose(0, 2, 1).reshape(-1, D)], 0), L1)
    rows = lambda w: w.reshape(DC, P, -1).transpose(1, 0, 2)

    pw = a["L1_attn_in_proj_w"]
    def tile(w, n):
        return np.pad(w, ((0, n * P - w.shape[0]),) + ((0, 0),) * (w.ndim - 1))
    cut = [E, 2 * E, 2 * E + NS, 2 * E + 2 * NS]
    g_, h_, b_, c_, d_ = np.split(pw, cut)
    in_w = np.concatenate([g_, h_, tile(b_, 1), tile(c_, 1), tile(d_, 1)])
    in_w = rows(np.ascontiguousarray(in_w.T))
    conv = np.concatenate([a["L1_attn_conv_w"], a["L1_attn_conv_b"][:, None]], 1)
    h_, b_, c_ = np.split(conv, [E, E + NS])
    conv = np.concatenate([h_, tile(b_, 1), tile(c_, 1)]).reshape(CJ, P, TAPS + 1).transpose(1, 0, 2).reshape(P, -1)
    per = lambda v: np.ascontiguousarray(v.reshape(EJ, P).T)
    ssm_cols = np.concatenate([conv, per(np.repeat(a["L1_attn_D"], HP)), per(a["L1_attn_norm_w"]),
                               tile(a["L1_attn_dt_bias"][:, None], 1), tile(a["L1_attn_A_log"][:, None], 1)], 1)
    out_w = a["L1_attn_out_proj_w"].T.reshape(EJ, P, D).transpose(1, 0, 2)
    out = dict(x_rows=x, x_cols=x.T, attn_w=attn_w, l0_gate=rows(a["L0_ffn_gate_w"]), l0_w=l0_w,
               l1_gate=rows(a["L1_ffn_gate_w"].T), l1_w=l1_w, in_w=in_w, ssm_cols=ssm_cols, out_w=out_w)
    return {n: np.ascontiguousarray(v) for n, v in out.items()}


def kernel(**inputs):
    import concourse.bacc as bacc
    from concourse.bass_utils import run_bass_kernel_spmd

    nc = bacc.Bacc("TRN2", target_bir_lowering=False, num_devices=1)
    arrays = lay_out(inputs)
    aps = {n: nc.dram_tensor(n, v.shape, mybir.dt.from_np(v.dtype), kind="ExternalInput").ap() for n, v in arrays.items()}
    out = nc.dram_tensor("out", (T, D), F32, kind="ExternalOutput").ap()
    program(nc, **aps, out=out)
    result = run_bass_kernel_spmd(nc, [arrays], core_ids=[0])
    return result.results[0]["out"].reshape(BATCH, SEQ, D)
```

```python
from contextlib import ExitStack

import concourse.bass as bass
from concourse import mybir

F32 = mybir.dt.float32
F32R = mybir.dt.float32r
I32 = mybir.dt.int32
ALU = mybir.AluOpType
ACT = mybir.ActivationFunctionType
AX = mybir.AxisListType

P = 128
BATCH, SEQ, D = 8, 256, 256
T = BATCH * SEQ
TILES = T // P
DC = D // P
BANK = 512
LN_EPS = 1e-5

HEADS, DH = 16, 128
HG = 2
GROUPS = HEADS // HG
PAIRS = BATCH // 2
UNITS = PAIRS * HG * 2
JOBS = 2 * HG + 2
WQ, WK, WV, WO = 0, HG * DC * DH, 2 * HG * DC * DH, 3 * HG * DC * DH
WA = 3 * HG * DC * DH + HG * D
MASKED = -1e9 * DH ** 0.5
SCALE = DH ** -0.5

HALF = T // 2
CHUNKS = HALF // BANK
WG, WU, WD, WF = 0, DC * P, 2 * DC * P, 2 * DC * P + D
SEL = 40
OUT = -1e30
SENTINEL = -2e30
TAKEN = -3e30
L0 = dict(name="l0", experts=32, width=96, shared=192, top=6)
L1 = dict(name="l1", experts=16, width=176, shared=352, top=4, groups=4, top_groups=2)
for _l in (L0, L1):
    _l["hidden"] = _l["shared"] + _l["experts"] * _l["width"]
    _l["tiles"] = -(-_l["hidden"] // P)

E, NH, HP, NS, TAPS = 512, 8, 64, 64, 4
EJ = E // P
MJ = 2 * EJ + 3
CJ = EJ + 2
PT = 2 * SEQ
SSM_EPS = 1e-6


def program(nc, x_rows, x_cols, attn_w, l0_gate, l0_w, l1_gate, l1_w, in_w, ssm_cols, out_w, out):
    with ExitStack() as ctx:
        def sem(name):
            return ctx.enter_context(nc.semaphore(name))

        def dram(name, shape):
            return nc.dram_tensor(name, shape, F32, kind="Internal").ap()

        def hold(eng, semaphore, count):
            if not isinstance(count, int) or count > 0:
                eng.wait_ge(semaphore, count)
                eng.sem_inc(held, 1)

        held = sem("held")

        def wait(eng, semaphore, count):
            if not isinstance(count, int) or count > 0:
                eng.wait_ge(semaphore, count)

        class Region:

            def __init__(self, at):
                self.at = at

            def __call__(self, name, shape, dt=F32):
                size = 4
                for n in shape[1:]:
                    size *= n
                t = nc.alloc_sbuf_tensor_at(name, shape, dt, offset=self.at)
                self.at += -(-size // 64) * 64
                assert self.at <= nc.sbuf_usable_end, (name, self.at)
                return t

        keep = Region(nc.sbuf_base + 64 - nc.sbuf_base % 64)
        ident = keep("ident", [P, P])
        causal_at = keep.at
        causal = keep("causal", [P, 2 * P])
        x = keep("x", [P, TILES, D])
        xT_hi = keep("xT_hi", [P, DC, T], F32R)
        xT_lo = keep("xT_lo", [P, DC, T], F32R)
        stats = keep("stats", [P, TILES, 6])
        mv = keep("mv", [P, TILES, 2])
        var, rstd, rtmp = (keep(n, [P, TILES]) for n in ("var", "rstd", "rtmp"))
        psum = ctx.enter_context(nc.psum_tensor("psum", [P, 8, BANK], F32))

        x_loaded = sem("x_loaded")
        const_ready = sem("const_ready")

        r = Region(keep.at)
        xT_raw = r("xT_raw", [P, DC, T])
        aw_raw = r("aw_raw", [P, WA])
        aw_hi = r("aw_hi", [P, WA], F32R)
        aw_lo = r("aw_lo", [P, WA], F32R)
        qT_hi, qT_lo, kT_hi, kT_lo = (r(n, [P, 2, HG, 2 * SEQ], F32R) for n in ("qT_hi", "qT_lo", "kT_hi", "kT_lo"))
        v_hi, v_lo = (r(n, [P, 2, 2, 2 * HG * DH], F32R) for n in ("v_hi", "v_lo"))
        s_sb = r("s_sb", [P, 2, 3 * P])
        p_sb = r("p_sb", [P, 3, 3 * P])
        pT_hi, pT_lo = (r(n, [P, 2, 3 * P], F32R) for n in ("pT_hi", "pT_lo"))
        zT_hi, zT_lo = (r(n, [P, 2, SEQ], F32R) for n in ("zT_hi", "zT_lo"))
        neg_max, row_sum, row_inv = (r(n, [P, 3, 2]) for n in ("neg_max", "row_sum", "row_inv"))

        xT_loaded = [sem(f"xT_loaded{i}") for i in range(PAIRS)]
        xT_hi_ready, xT_lo_ready = sem("xT_hi_ready"), sem("xT_lo_ready")
        aw_loaded, aw_split = sem("aw_loaded"), sem("aw_split")
        aw_hi_done = sem("aw_hi_done")
        qkv_ready, qkv_hi, qkv_lo = sem("qkv_ready"), sem("qkv_hi"), sem("qkv_lo")
        s_ready, s_masked = sem("s_ready"), sem("s_masked")
        p_ready, r_ready, p_scaled = sem("p_ready"), sem("r_ready"), sem("p_scaled")
        pT_ready, pT_hi_ready, pT_lo_ready = sem("pT_ready"), sem("pT_hi_ready"), sem("pT_lo_ready")
        z_ready, z_hi_ready, z_lo_ready = sem("z_ready"), sem("z_hi_ready"), sem("z_lo_ready")
        o_ready, o_added = sem("o_ready"), sem("o_added")

        QKV_BANK, S_BANK, PT_BANK, Z_BANK, O_BANK = 0, 2, 4, 5, 6

        def passes(a_hi, a_lo, b_hi, b_lo):
            return ((a_hi, b_hi), (a_hi, b_lo), (a_lo, b_hi))

        def attn_schedule(next_group):
            lag_t, lag_v, lag_o = 2, 3, 4
            for i in range(UNITS + lag_o):
                jobs = []
                bp = i // (2 * HG)
                if i < UNITS - 2 * HG:
                    jobs = [(bp + 1, j) for j in ((0, 1), (2,), (3, 4), (5,))[i % 4]]
                elif UNITS - 3 <= i < UNITS - 3 + JOBS and next_group:
                    jobs = [(PAIRS, i - (UNITS - 3))]
                yield i, jobs[:1], jobs[1:], i if i < UNITS else None, *(i - g if 0 <= i - g < UNITS else None for g in (lag_t, lag_v, lag_o))

        def unit(u):
            return u // (2 * HG), u % (2 * HG) // 2, u % 2

        ln_stat, ln_aggr, ln_var, ln_done = (sem(n) for n in ("ln_stat", "ln_aggr", "ln_var", "ln_done"))
        ln_root = sem("ln_root")
        lnT_ready, lnT_hi, lnT_lo = sem("lnT_ready"), sem("lnT_hi"), sem("lnT_lo")
        stored = sem("stored")
        NORMS = 4
        HALF_TILES = TILES // 2
        LNT = DC * HALF_TILES // 4

        def inverse_root(root, value, tmp, done, base):
            dve = nc.vector
            count = base

            def step(ins):
                nonlocal count
                count += 1
                ins.then_inc(done, 1)
                dve.wait_ge(done, count)

            step(dve.tensor_scalar(root.bitcast(I32), value.bitcast(I32), 1, None, ALU.logical_shift_right))
            step(dve.tensor_scalar(root.bitcast(I32), root.bitcast(I32), -1, 0x5f3759df, ALU.mult, ALU.add))
            for _ in range(3):
                step(dve.tensor_tensor(tmp, root, root, ALU.mult))
                step(dve.scalar_tensor_tensor(tmp, tmp, -0.5, value, ALU.mult, ALU.mult))
                step(dve.scalar_tensor_tensor(root, tmp, 1.5, root, ALU.add, ALU.mult))
            assert count == base + ROOT_STEPS

        ROOT_STEPS = 11

        def half(u):
            return range(u % 2 * HALF_TILES, (u % 2 + 1) * HALF_TILES)

        def ln_stats(u, quad, ready, count):
            dve = nc.vector
            dve.wait_ge(ready, count)
            tiles = half(u)[4 * quad:4 * quad + 4]
            seen = u * HALF_TILES + 4 * quad
            for i in tiles:
                dve.bn_stats(stats[:, i, :], x[:, i, :]).then_inc(ln_stat, 1)
            for k, i in enumerate(tiles):
                dve.wait_ge(ln_stat, seen + k + 1)
                dve.bn_aggr(mv[:, i, :], stats[:, i, :]).then_inc(ln_aggr, 1)
            if quad == 1:
                dve.wait_ge(ln_aggr, (u + 1) * HALF_TILES)
                s = slice(half(u)[0], half(u)[-1] + 1)
                dve.tensor_scalar(var[:, s], mv[:, s, 1], LN_EPS, None, ALU.add).then_inc(ln_var, 1)

        def ln_scales(u):
            dve = nc.vector
            dve.wait_ge(ln_var, u + 1)
            s = slice(half(u)[0], half(u)[-1] + 1)
            inverse_root(rstd[:, s], var[:, s], rtmp[:, s], ln_root, u * ROOT_STEPS)

        def ln_rows(u, quad):
            dve = nc.vector
            for i in half(u)[4 * quad:4 * quad + 4]:
                dve.tensor_scalar(x[:, i, :], x[:, i, :], mv[:, i, 0:1], rstd[:, i:i + 1],
                                  ALU.subtract, ALU.mult).then_inc(ln_done, 1)

        def turned(u, b):
            t0 = u % 2 * HALF + b // DC * BANK
            return u * LNT + b, b % DC, slice(t0, t0 + BANK)

        def ln_turns(u, quad, banks):
            pe = nc.tensor
            for b in (2 * quad, 2 * quad + 1):
                n, c, _ = turned(u, b)
                if b >= len(banks):
                    pe.wait_ge(lnT_lo, n + 1 - len(banks))
                pe.wait_ge(ln_done, u * HALF_TILES + 4 * quad + 4)
                for k in range(4):
                    last = pe.transpose(psum[:, banks[b % len(banks)], k * P:(k + 1) * P], x[:, half(u)[4 * quad + k], c * P:(c + 1) * P], ident[:])
                last.then_inc(lnT_ready, 1)

        def ln_highs(u, quad, banks):
            act = nc.scalar
            for b in (2 * quad, 2 * quad + 1):
                n, c, t = turned(u, b)
                act.wait_ge(lnT_ready, n + 1)
                act.activation(xT_hi[:, c, t], psum[:, banks[b % len(banks)], :], ACT.Copy).then_inc(lnT_hi, 1)

        def ln_lows(u, quad, banks):
            dve = nc.vector
            for b in (2 * quad, 2 * quad + 1):
                n, c, t = turned(u, b)
                dve.wait_ge(lnT_hi, n + 1)
                dve.tensor_tensor(xT_lo[:, c, t], psum[:, banks[b % len(banks)], :], xT_hi[:, c, t].bitcast(F32), ALU.subtract).then_inc(lnT_lo, 1)

        def chain(out_ap, pairs, start=True, stop=True, **kw):
            for n, (w, m) in enumerate(pairs):
                last = nc.tensor.matmul(out_ap, w, m, start=start and n == 0, stop=stop and n == len(pairs) - 1, **kw)
            return last

        def weight_tensors(layer, r, logits_at):
            t = {n: r(f"{layer}_{n}", [P, 2, WF], dt) for n, dt in (("fw_raw", F32), ("fw_hi", F32R), ("fw_lo", F32R))}
            t["comb"] = r(f"{layer}_comb", [P, 2, HALF])
            for n, dt in (("gate_raw", F32), ("gate_hi", F32R), ("gate_lo", F32R)):
                t[n] = r(f"{layer}_{n}", [P, DC * 32], dt)
            for n, wide in (("logit", 32), ("score", 32), ("weight", 32), ("comb_tok", 32), ("choice", SEL), ("chosen", SEL),
                            ("top8", 8), ("group_top8", 8), ("group_choice", 16), ("group_chosen", 16)):
                t[n] = r(f"{layer}_{n}", [P, HALF_TILES, wide])
            t["row_stat"] = r(f"{layer}_row_stat", [P, HALF_TILES])
            t["combT"] = r(f"{layer}_combT", [32, HALF])
            t["logitT"] = logits_at(f"{layer}_logitT", [32, HALF])
            return t

        def hidden_tensors(layer, r):
            t = {n: r(f"{layer}_{n}", [P, 2, BANK], dt)
                 for n, dt in (("gated", F32), ("gated_comb", F32), ("act_sb", F32), ("act_hi", F32R), ("act_lo", F32R))}
            t["yT"] = r(f"{layer}_yT", [P, DC, HALF])
            return t

        def ssm_tensors_early(r):
            small = Region(causal_at)
            t = dict(cols=small("cols", [P, CJ * (TAPS + 1) + 2 * EJ + 2]))
            for n, shape in (("ones_col", [P, 1]), ("a_col", [P, 1]), ("dt_tok", [P, 4, NH]), ("mean_sq", [P, 4]), ("rms", [P, 4]), ("rms_tmp", [P, 4])):
                t[n] = small(n, shape)
            t["start_row"] = r("start_row", [P, 2, 3, P])
            t["gate_at"] = r.at
            t["in_gate"] = r("in_gate_hi", [P, DC, EJ * P], F32R), r("in_gate_lo", [P, DC, EJ * P], F32R)
            t["ow"] = r("ow_hi", [P, EJ, D], F32R), r("ow_lo", [P, EJ, D], F32R)
            t["dead_at"] = r.at
            t["in_rest"] = r("in_rest_hi", [P, DC, (MJ - EJ) * P], F32R), r("in_rest_lo", [P, DC, (MJ - EJ) * P], F32R)
            raw = Region(r.at)
            t["in_raw"], t["ow_raw"] = raw("in_raw", [P, DC, MJ * P]), raw("ow_raw", [P, EJ, D])
            t["pair0"] = ssm_tensors_pair(0, r)
            return t

        def ssm_tensors_pair(q, r):
            return dict(conv=r(f"conv{q}", [P, CJ, PT]), h_tok=r(f"h_tok{q}", [P, 4, E]),
                        h_hi=r(f"h_hi{q}", [P, 2, E], F32R), h_lo=r(f"h_lo{q}", [P, 2, E], F32R))

        gating = {n: sem(n) for n in ("gate_loaded gate_hi_done gate_split sentinels logitT_ready logitT_copied logits_ready score_ready logit_read shifted gate_step "
                                      "comb_ready combT_ready combT_copied comb_stored").split()}

        def signals(layer):
            names = ("gu_hi d_hi gu_split d_split g_ready u_ready gated_ready gated_comb_ready act_ready act_hi_ready act_lo_ready "
                     "down_done y_copied yT_ready y_added").split()
            return dict({n: sem(f"{layer}_{n}") for n in names}, **gating,
                        w_loaded=[sem(f"{layer}_w_loaded{i}") for i in range(2)],
                        comb_loaded=[sem(f"{layer}_comb_loaded{i}") for i in range(2)])

        l0_low, l0_high = Region(keep.at), Region(r.at)
        l0_hidden = hidden_tensors("l0", l0_low)
        ones_row, ones_dram = l0_high("ones_row", [1, HALF]), dram("ones_dram", [1, HALF])
        ssm_early = Region(l0_low.at)
        early = ssm_tensors_early(ssm_early)
        layers = (("l0", L0, l0_gate, l0_w, l0_hidden, weight_tensors("l0", l0_high, l0_high)),
                  ("l1", L1, l1_gate, l1_w, hidden_tensors("l1", Region(keep.at)), weight_tensors("l1", Region(early["dead_at"]), Region(early["gate_at"]))))
        expert_layers = [
            dict(**layer, layer=i, norm=2 * i, w_dram=w, gate_dram=g, comb_dram=dram(f"{name}_comb_dram", [layer["experts"], T]), **hidden, **weights, **signals(name))
            for i, (name, layer, g, w, hidden, weights) in enumerate(layers)]
        ones_ready, ones_stored = sem("ones_ready"), sem("ones_stored")
        G_BANK, U_BANK, Y_BANK = 0, 2, 4
        FIRST_NORM_BANKS, FIRST_GATE_BANKS, FIRST_TURN_BANKS = (0, 1, 2, 3), (0, 1, 2), (6, 7)
        NORM_BANKS, GATE_BANKS = (4, 5, 6, 7), (5, 7, 5)

        def segments(f, j):
            cuts, row = [], lambda n: f["experts"] if n < f["shared"] or n >= f["hidden"] else (n - f["shared"]) // f["width"]
            for p in range(P):
                n = row(j * P + p)
                if cuts and cuts[-1][0] == n:
                    cuts[-1][2] = p + 1
                else:
                    cuts.append([n, p, p + 1])
            if len(cuts) == 1:
                cuts = [[cuts[0][0], 0, P // 2], [cuts[0][0], P // 2, P]]
            assert len(cuts) == 2
            return cuts

        def hidden_tiles(eng, f, body, tail, hooks):
            n = f["tiles"]
            pairs = (n - 1) // 2

            def written(h, j):
                body(h, j, h * n + j, (h * n + j) % 2, j == 0, j == n - 1)
                if (h, j) in hooks:
                    hooks[h, j]()

            for h in range(2):
                for j in range(2):
                    written(h, j)
                with eng.Fori(1, pairs) as m:
                    for j in range(2):
                        body(h, 2 * m + j, 2 * m + j + h * n, (h * n + j) % 2, False, False)
                for j in range(2 * pairs, n):
                    written(h, j)
                tail(h)

        def loads(n, buf):
            return (n - buf) * 8 + 16

        def experts_sync(f, hooks):
            sp = nc.sync
            sp.dma_start(f["gate_raw"][:, 0:DC * f["experts"]], f["gate_dram"].rearrange("p c e -> p (c e)")).then_inc(f["gate_loaded"], 16)
            for n in range(2 * f["tiles"]):
                h, j = divmod(n, f["tiles"])
                if n in hooks:
                    hooks[n]()
                if n >= 2:
                    sp.wait_ge(f["d_split"], n - 1)
                sp.dma_start(f["fw_raw"][:, n % 2, :], f["w_dram"][j]).then_inc(f["w_loaded"][n % 2], 16)
                if n >= 2:
                    sp.wait_ge(f["gated_comb_ready"], CHUNKS * (n - 1))
                if j == f["shared"] // P:
                    sp.wait_ge(f["combT_copied"], 4 * f["layer"] + 2 * h + 2)
                    sp.dma_start(f["comb_dram"][:, h * HALF:(h + 1) * HALF], f["combT"][0:f["experts"], :]).then_inc(f["comb_stored"], 16)
                    sp.wait_ge(f["comb_stored"], 32 * f["layer"] + 16 * h + 16)
                for row, p0, p1 in segments(f, j):
                    src = ones_dram[0] if row == f["experts"] else f["comb_dram"][row, h * HALF:(h + 1) * HALF]
                    sp.dma_start(f["comb"][p0:p1, n % 2, :], src.partition_broadcast(p1 - p0)).then_inc(f["comb_loaded"][n % 2], 16)

        def gate_start(f):
            pool = nc.gpsimd
            pool.memset(f["choice"][:], SENTINEL).then_inc(f["sentinels"], 1)
            pool.memset(f["group_choice"][:], SENTINEL).then_inc(f["sentinels"], 1)
            pool.wait_ge(f["gate_loaded"], 16 * f["layer"] + 16)
            c = slice(0, DC * f["experts"])
            pool.tensor_copy(f["gate_hi"][:, c], f["gate_raw"][:, c]).then_inc(f["gate_hi_done"], 1)
            pool.wait_ge(f["gate_hi_done"], f["layer"] + 1)
            pool.tensor_tensor(f["gate_lo"][:, c], f["gate_raw"][:, c], f["gate_hi"][:, c].bitcast(F32), ALU.subtract).then_inc(f["gate_split"], 1)

        def gate_logits(f, h, banks):
            pe = nc.tensor
            e = f["experts"]
            pe.wait_ge(f["gate_split"], f["layer"] + 1)
            pe.wait_ge(lnT_lo, (2 * f["norm"] + h + 1) * LNT)
            for b in range(2):
                pairs = []
                for c in range(DC):
                    t, w = slice(h * HALF + b * BANK, h * HALF + (b + 1) * BANK), slice(c * e, (c + 1) * e)
                    pairs += passes(f["gate_hi"][:, w], f["gate_lo"][:, w], xT_hi[:, c, t], xT_lo[:, c, t])
                chain(psum[0:e, banks[b], :], pairs).then_inc(f["logitT_ready"], 1)

        def gate_logits_copy(f, h, banks):
            act = nc.scalar
            e = f["experts"]
            for b in range(2):
                act.wait_ge(f["logitT_ready"], 4 * f["layer"] + 2 * h + b + 1)
                wait(act, f["logits_ready"], 2 * f["layer"] + h)
                act.activation(f["logitT"][0:e, b * BANK:(b + 1) * BANK], psum[0:e, banks[b], :], ACT.Copy).then_inc(f["logitT_copied"], 1)

        def gate_logits_turn(f, h, banks):
            pe = nc.tensor
            e = f["experts"]
            for k in range(HALF_TILES):
                pe.wait_ge(f["logitT_copied"], 4 * f["layer"] + 2 * h + k // 4 + 1)
                last = pe.transpose(psum[:, banks[2], k * e:(k + 1) * e], f["logitT"][0:e, k * P:(k + 1) * P], ident[0:e, 0:e])
            last.then_inc(f["logits_ready"], 1)

        def gate_score(f, h, bank):
            act = nc.scalar
            e = f["experts"]
            wait(act, f["comb_ready"], 2 * f["layer"] + h)
            if f["top"] == 6:
                act.wait_ge(f["logits_ready"], 2 * f["layer"] + h + 1)
                logits = psum[:, bank, 0:HALF_TILES * e].rearrange("p (i e) -> p i e", e=e)
                act.activation(f["score"][:, :, 0:e], logits, ACT.Sigmoid).then_inc(f["score_ready"], 1)
            else:
                act.wait_ge(f["shifted"], h + 1)
                act.activation(f["score"][:, :, 0:e], f["weight"][:, :, 0:e], ACT.Exp).then_inc(f["score_ready"], 1)

        gate_steps = [0]

        def gate_step(f, ins):
            gate_steps[0] += 1
            ins.then_inc(f["gate_step"], 1)
            nc.vector.wait_ge(f["gate_step"], gate_steps[0])

        def per_row(t):
            return t.rearrange("p (i a) -> p i a", a=1)

        def gate_read(f, h, bank):
            dve = nc.vector
            e = f["experts"]
            logits = psum[:, bank, 0:HALF_TILES * e].rearrange("p (i e) -> p i e", e=e)
            wait(dve, f["comb_ready"], 2 * f["layer"] + h)
            dve.wait_ge(f["logits_ready"], 2 * f["layer"] + h + 1)
            dve.wait_ge(f["sentinels"], 2 * f["layer"] + 2)
            if f["top"] == 6:
                dve.wait_ge(f["score_ready"], 2 * f["layer"] + h + 1)
                dve.tensor_scalar(f["choice"][:, :, 0:e], logits, 16.636, -88.0, ALU.min, ALU.max).then_inc(f["logit_read"], 1)
            else:
                dve.tensor_copy(f["logit"][:, :, 0:e], logits).then_inc(f["logit_read"], 1)
            dve.wait_ge(f["logit_read"], 2 * f["layer"] + h + 1)

        def gate_groups(f, h):
            dve = nc.vector
            if f["top"] == 6:
                return
            e, size = f["experts"], f["experts"] // f["groups"]
            logit, choice, chosen, best = f["logit"], f["group_choice"], f["group_chosen"], f["group_top8"]
            by_group = logit[:, :, 0:e].rearrange("p i (g m) -> p i g m", g=f["groups"])
            gate_step(f, dve.tensor_reduce(f["row_stat"][:], logit[:, :, 0:e], AX.X, ALU.max))
            dve.tensor_tensor(f["weight"][:, :, 0:e], logit[:, :, 0:e], per_row(f["row_stat"][:]).to_broadcast([P, HALF_TILES, e]),
                              ALU.subtract).then_inc(f["shifted"], 1)
            groups = choice[:, :, 0:f["groups"]]
            gate_step(f, dve.tensor_reduce(groups, by_group, AX.X, ALU.max))
            for i in range(HALF_TILES):
                last = dve.max(best[:, i, :], choice[:, i, :])
            gate_step(f, last)
            gate_step(f, dve.memset(best[:, :, f["top_groups"]:8], SENTINEL))
            for i in range(HALF_TILES):
                last = dve.match_replace(chosen[:, i, :], best[:, i, :], choice[:, i, :], TAKEN)
            gate_step(f, last)
            gate_step(f, dve.tensor_scalar(groups, chosen[:, :, 0:f["groups"]], TAKEN, None, ALU.is_equal))
            gate_step(f, dve.tensor_scalar(chosen[:, :, 0:f["groups"]], groups, -OUT, OUT, ALU.mult, ALU.add))
            gate_step(f, dve.tensor_tensor(f["choice"][:, :, 0:e].rearrange("p i (g m) -> p i g m", g=f["groups"]), by_group,
                                           chosen[:, :, 0:f["groups"]].rearrange("p i (g a) -> p i g a", a=1)
                                           .to_broadcast([P, HALF_TILES, f["groups"], size]), ALU.add))

        def gate_choose(f, h):
            dve = nc.vector
            e, top = f["experts"], f["top"]
            score, weight, choice, chosen, stat = f["score"], f["weight"], f["choice"], f["chosen"], f["row_stat"]
            if top != 6:
                dve.wait_ge(f["score_ready"], 2 * f["layer"] + h + 1)
                gate_step(f, dve.tensor_reduce(stat[:], score[:, :, 0:e], AX.X, ALU.add))
                gate_step(f, dve.reciprocal(stat[:], stat[:]))
                gate_step(f, dve.tensor_tensor(score[:, :, 0:e], score[:, :, 0:e], per_row(stat[:]).to_broadcast([P, HALF_TILES, e]), ALU.mult))
            wide = e + 8
            for i in range(HALF_TILES):
                last = dve.max(f["top8"][:, i, :], choice[:, i, 0:wide])
            gate_step(f, last)
            gate_step(f, dve.memset(f["top8"][:, :, top:8], SENTINEL))
            for i in range(HALF_TILES):
                last = dve.match_replace(chosen[:, i, 0:wide], f["top8"][:, i, :], choice[:, i, 0:wide], TAKEN)
            gate_step(f, last)
            gate_step(f, dve.tensor_scalar(weight[:, :, 0:e], chosen[:, :, 0:e], TAKEN, None, ALU.is_equal))
            gate_step(f, dve.tensor_tensor(weight[:, :, 0:e], weight[:, :, 0:e], score[:, :, 0:e], ALU.mult))
            gate_step(f, dve.tensor_reduce(stat[:], weight[:, :, 0:e], AX.X, ALU.add))
            gate_step(f, dve.tensor_scalar(stat[:], stat[:], 1e-20, None, ALU.add))
            gate_step(f, dve.reciprocal(stat[:], stat[:]))
            wait(dve, f["combT_ready"], 4 * f["layer"] + 2 * h)
            dve.tensor_tensor(f["comb_tok"][:, :, 0:e], weight[:, :, 0:e], per_row(stat[:]).to_broadcast([P, HALF_TILES, e]),
                              ALU.mult).then_inc(f["comb_ready"], 1)

        def gate_turns(f, h, banks):
            pe = nc.tensor
            pe.wait_ge(f["comb_ready"], 2 * f["layer"] + h + 1)
            for k in range(HALF_TILES):
                last = pe.transpose(psum[0:f["experts"], banks[k // 4], k % 4 * P:(k % 4 + 1) * P], f["comb_tok"][:, k, 0:f["experts"]], ident[:])
                if k % 4 == 3:
                    last.then_inc(f["combT_ready"], 1)

        def gate_copy(f, h, banks):
            dve = nc.vector
            for b in range(2):
                dve.wait_ge(f["combT_ready"], 4 * f["layer"] + 2 * h + b + 1)
                wait(dve, f["comb_stored"], 32 * f["layer"] + 16 * h)
                dve.tensor_copy(f["combT"][0:f["experts"], b * BANK:(b + 1) * BANK], psum[0:f["experts"], banks[b], :]).then_inc(f["combT_copied"], 1)

        TURN_BANKS = 1, 3

        def weights_high(f, n, buf, part):
            act = nc.scalar
            if part == 0:
                act.wait_ge(f["w_loaded"][buf], loads(n, buf))
            w = slice(WD, WF) if part else slice(0, WD)
            act.activation(f["fw_hi"][:, buf, w], f["fw_raw"][:, buf, w], ACT.Copy).then_inc(f["d_hi"] if part else f["gu_hi"], 1)

        def weights_low(f, n, buf, part):
            pool = nc.gpsimd
            w = slice(WD, WF) if part else slice(0, WD)
            pool.wait_ge(f["d_hi"] if part else f["gu_hi"], n + 1)
            pool.tensor_tensor(f["fw_lo"][:, buf, w], f["fw_raw"][:, buf, w], f["fw_hi"][:, buf, w].bitcast(F32),
                               ALU.subtract).then_inc(f["d_split"] if part else f["gu_split"], 1)

        def experts_pool(f, hooks):
            pool = nc.gpsimd
            gated, gated_comb, comb = f["gated"], f["gated_comb"], f["comb"]

            def tile(h, j, n, buf, first, last):
                for c in range(CHUNKS):
                    s = n * CHUNKS + c
                    if c == 0:
                        pool.wait_ge(f["comb_loaded"][buf], 2 * loads(n, buf))
                    if h or not first or c > 1:
                        pool.wait_ge(f["act_ready"], s - 1)
                    pool.wait_ge(f["gated_ready"], s + 1)
                    pool.tensor_tensor(gated_comb[:, c, :], gated[:, c, :], comb[:, buf, c * BANK:(c + 1) * BANK],
                                       ALU.mult).then_inc(f["gated_comb_ready"], 1)
                    if not (last and h == 1):
                        weights_low(f, n + 1, 1 - buf, c)

            hidden_tiles(pool, f, tile, lambda h: None, hooks)

        def experts_scalar(f, hooks, second_norm, transposed):
            act = nc.scalar

            def gates(n, c):
                act.wait_ge(f["g_ready"], n * CHUNKS + c + 1)
                act.activation(f["gated"][:, c, :], psum[:, G_BANK + c, :], ACT.Silu).then_inc(f["gated_ready"], 1)

            def highs(n, c):
                act.wait_ge(f["act_ready"], n * CHUNKS + c + 1)
                act.activation(f["act_hi"][:, c, :], f["act_sb"][:, c, :], ACT.Copy).then_inc(f["act_hi_ready"], 1)

            def tile(h, j, n, buf, first, last):
                if first and h == 0:
                    for c in range(CHUNKS):
                        gates(n, c)
                    second_norm()
                for c in range(CHUNKS):
                    s = n * CHUNKS + c
                    if h or not first:
                        act.wait_ge(f["gated_comb_ready"], s - 1)
                        gates(n, c)
                    if not (last and h == 1):
                        weights_high(f, n + 1, 1 - buf, c)
                    highs(n, c)
                    if first and h == 0 and c == 0 and f["top"] == 6:
                        gate_score(f, 1, GATE_BANKS[2])

            def tail(h):
                act.wait_ge(f["down_done"], (h + 1) * f["tiles"] * CHUNKS)
                if h:
                    act.wait_ge(f["yT_ready"], DC * CHUNKS)
                for c in range(CHUNKS):
                    act.activation(f["yT"][:, 0, c * BANK:(c + 1) * BANK], psum[:, Y_BANK + c, :], ACT.Copy).then_inc(f["y_copied"], 1)
                if h and transposed:
                    for quad in range(2):
                        ln_highs(2 * (f["norm"] + 1), quad, (0, 1, 2, 3))

            hidden_tiles(act, f, tile, tail, hooks)

        def experts_vector(f, hooks, transposed):
            dve = nc.vector
            act_sb, act_hi, act_lo = f["act_sb"], f["act_hi"], f["act_lo"]

            def tile(h, j, n, buf, first, last):
                for c in range(CHUNKS):
                    s = n * CHUNKS + c
                    dve.wait_ge(f["u_ready"], s + 1)
                    if h or not first:
                        dve.wait_ge(f["act_hi_ready"], s - 1)
                    dve.wait_ge(f["gated_comb_ready"], s + 1)
                    dve.tensor_tensor(act_sb[:, c, :], psum[:, U_BANK + c, :], f["gated_comb"][:, c, :], ALU.mult).then_inc(f["act_ready"], 1)
                    dve.wait_ge(f["act_hi_ready"], s + 1)
                    dve.tensor_tensor(act_lo[:, c, :], act_sb[:, c, :], act_hi[:, c, :].bitcast(F32), ALU.subtract).then_inc(f["act_lo_ready"], 1)
                    if first and h == 0 and c == 0:
                        gate_read(f, 1, GATE_BANKS[2])

            def tail(h):
                u = 2 * (f["norm"] + 1) + h
                dve.wait_ge(f["down_done"], (h + 1) * f["tiles"] * CHUNKS)
                if h:
                    dve.wait_ge(f["yT_ready"], DC * CHUNKS)
                for c in range(CHUNKS):
                    dve.tensor_copy(f["yT"][:, 1, c * BANK:(c + 1) * BANK], psum[:, Y_BANK + CHUNKS + c, :]).then_inc(f["y_copied"], 1)
                if h == 0:
                    gate_copy(f, 1, TURN_BANKS)
                if h and transposed:
                    for quad in range(2):
                        ln_lows(u - 1, quad, (0, 1, 2, 3))
                for b in range(4):
                    dve.wait_ge(f["yT_ready"], 4 * h + b + 1)
                    rows = x[:, h * HALF_TILES + 2 * b:h * HALF_TILES + 2 * b + 2, :]
                    dve.tensor_tensor(rows, psum[:, Y_BANK + b, :].rearrange("p (i d) -> p i d", i=2), rows, ALU.add).then_inc(f["y_added"], 1)
                    if h and b % 2:
                        ln_stats(u, b // 2, f["y_added"], 4 * h + b + 1)

            hidden_tiles(dve, f, tile, tail, hooks)

        def experts_tensor(f, hooks, second_norm, transposed):
            pe = nc.tensor
            n_tiles, yT = f["tiles"], f["yT"]
            fw_hi, fw_lo, act_hi, act_lo = f["fw_hi"], f["fw_lo"], f["act_hi"], f["act_lo"]

            def gate_up(h, n, buf, c, first):
                s = n * CHUNKS + c
                if c == 0:
                    pe.wait_ge(f["gu_split"], n + 1)
                if first and h == 0 and c == 0:
                    pe.wait_ge(lnT_lo, (2 * f["norm"] + 1) * LNT)
                    pe.wait_ge(f["logit_read"], 2 * f["layer"] + 1)
                if first and h == 1 and c == 1:
                    pe.wait_ge(f["combT_copied"], 4 * f["layer"] + 4)
                if h or not first:
                    pe.wait_ge(f["gated_ready"], s - 1)
                for w0, bank, ready in ((WG, G_BANK, f["g_ready"]), (WU, U_BANK, f["u_ready"])):
                    if w0 == WU and (h or not first):
                        pe.wait_ge(f["act_ready"], s - 1)
                    elif w0 == WU and f["layer"]:
                        pe.wait_ge(*((m["mean_ready"], PAIRS) if c else (m["out_added"], T // P)))
                    pairs = []
                    for k in range(DC):
                        w = slice(w0 + k * P, w0 + (k + 1) * P)
                        t = bass.ds(h * HALF + c * BANK, BANK)
                        pairs += passes(fw_hi[:, buf, w], fw_lo[:, buf, w], xT_hi[:, k, t], xT_lo[:, k, t])
                    chain(psum[:, bank + c, :], pairs).then_inc(ready, 1)

            def down(n, c, buf, first, last_tile):
                s = n * CHUNKS + c
                if c == 0:
                    pe.wait_ge(f["d_split"], n + 1)
                for lows in range(2):
                    pe.wait_ge((f["act_lo_ready"] if lows else f["act_hi_ready"]), s + 1)
                    for d in range(DC):
                        w = slice(WD + d * P, WD + (d + 1) * P)
                        pairs = passes(fw_hi[:, buf, w], fw_lo[:, buf, w], act_hi[:, c, :], act_lo[:, c, :])
                        pairs = (pairs[0], pairs[2]) if not lows else pairs[1:2]
                        last = chain(psum[:, Y_BANK + d * CHUNKS + c, :], pairs, start=first and lows == 0, stop=last_tile and lows == 1,
                                     skip_group_check=True)
                last.then_inc(f["down_done"], 1)

            def tile(h, j, n, buf, first, last):
                for c in range(CHUNKS):
                    if not (first and h == 1 and c == 0):
                        gate_up(h, n, buf, c, first)
                    if c == 0 and not first:
                        if h == 0 and isinstance(j, int) and j == 1:
                            pe.wait_ge(f["logit_read"], 2 * f["layer"] + 2)
                        down(n - 1, CHUNKS - 1, 1 - buf, isinstance(j, int) and j == 1, False)
                    elif c:
                        if first and h == 0:
                            second_norm()
                        elif first:
                            pe.wait_ge(f["y_added"], 4)
                        down(n, c - 1, buf, first, last)

            def tail(h):
                n = (h + 1) * n_tiles
                down(n - 1, CHUNKS - 1, (n - 1) % 2, False, True)
                if h == 0:
                    gate_turns(f, 1, TURN_BANKS)
                    gate_up(1, n, n % 2, 0, True)
                elif transposed:
                    for quad in range(2):
                        ln_turns(2 * (f["norm"] + 1), quad, (0, 1, 2, 3))
                pe.wait_ge(f["y_copied"], (h + 1) * DC * CHUNKS)
                for b in range(4):
                    for i in range(2):
                        for d in range(DC):
                            t = 2 * b + i
                            last = pe.transpose(psum[:, Y_BANK + b, (i * DC + d) * P:(i * DC + d + 1) * P], yT[:, d, t * P:(t + 1) * P], ident[:])
                    last.then_inc(f["yT_ready"], 1)

            hidden_tiles(pe, f, tile, tail, hooks)

        cols, start_row, ones_col, a_col, dt_tok, mean_sq, rms, rms_tmp = (
            early[n] for n in ("cols", "start_row", "ones_col", "a_col", "dt_tok", "mean_sq", "rms", "rms_tmp"))
        in_parts, in_raw, ow_raw = (early["in_gate"], early["in_rest"]), early["in_raw"], early["ow_raw"]
        ow_hi, ow_lo = early["ow"]
        pair1 = ssm_tensors_pair(1, Region(keep.at))
        conv, h_tok, h_hi, h_lo = ((early["pair0"][n], pair1[n]) for n in ("conv", "h_tok", "h_hi", "h_lo"))
        r = ssm_early
        dt = r("dt", [NH, PT])
        ROW = 3 * P
        rows = r("rows", [NH, 2, ROW])
        neg_abs = rows[:].rearrange("h b c -> h (b c)")[:, 0:PT]
        RING = 3
        decay_all = r("decay_all", [P, RING, 2 * ROW])
        silu_gate = r("silu_gate", [P, 2, PT])
        gram = r("gram", [P, 2, 2, ROW])
        MIXES = 4
        mix = r("mix", [P, MIXES, 2, ROW])
        mix_hi, mix_lo = r("mix_hi", [P, 2, 2, SEQ], F32R), r("mix_lo", [P, 2, 2, SEQ], F32R)
        y = r("y", [P, 2, PT])
        square, square_sum = r("square", [P, PT]), r("square_sum", [P, PT])
        y_hi, y_lo = r("y_hi", [P, EJ, PT], F32R), r("y_lo", [P, EJ, PT], F32R)
        decay_dram = dram("decay_dram", [PAIRS, NH, 2 * ROW])

        tap = lambda j, k: cols[:, j * (TAPS + 1) + k:j * (TAPS + 1) + k + 1]
        at = CJ * (TAPS + 1)
        skip_col = lambda j: cols[:, at + j:at + j + 1]
        norm_col = lambda j: cols[:, at + EJ + j:at + EJ + j + 1]
        dt_bias, a_log = cols[0:NH, at + 2 * EJ:at + 2 * EJ + 1], cols[0:NH, at + 2 * EJ + 1:at + 2 * EJ + 2]

        SSM_GATE_BANKS = 0, 1, 5
        names = ("loaded in_hi_done ow_hi_done in_split ow_scaled ow_split start_ready a_exp a_ready proj_ready bank_read0 bank_read1 bank_read2 "
                 "z_step z_ready exp_ready log_ready dt_ready decay_ready rows_ready rows_stored decay_loaded0 decay_loaded1 "
                 "decay_loaded2 dtT_ready dt_tok_ready tap_ready tap_step conv_ready gram_ready gram_copied hT_ready h_tok_ready "
                 "h_hi_ready h_lo_ready since_ready mix_ready mix_hi_ready mix_lo_ready yT_ready y_ready gated_ready "
                 "square_ready square_added y_hi_ready y_lo_ready sum_ready mean_ready root_step out_ready out_added").split()
        m = {n: sem(f"ssm_{n}") for n in names}
        bank_read = m["bank_read0"], m["bank_read1"], m["bank_read2"]
        decay_loaded = m["decay_loaded0"], m["decay_loaded1"], m["decay_loaded2"]
        PROJ_BANKS, GRAM_BANK, YT_BANK = (0, 1, 5), 3, 6
        HT_BANKS = OUT_BANKS = 4, 2
        DT_COL, SUM_COL = 3 * P, 3 * P + 4 * NH
        HEADS_ALL = PAIRS * NH
        GRAM_STEPS = 3, 4
        GATES = HEADS_ALL // 2
        TI_H, TI_B, TI_C, TI_DT = EJ, 2 * EJ, 2 * EJ + 1, 2 * EJ + 2

        def ssm_schedule():
            ahead = {0: (TI_DT,), 1: (TI_B, TI_C), 2: (TI_H, TI_H + 1), 3: (TI_H + 2,), 4: (TI_H + 3,)}
            gates = (3, 0), (5, 1), (6, 2), (7, 3)
            steps, k, n = [], 0, 0
            for g in range(-1, HEADS_ALL + 8):
                p, hd = divmod(g, NH)
                if g < 0:
                    want = [(0, i) for i in (TI_DT, TI_B, TI_C, TI_H, TI_H + 1, TI_H + 2, TI_H + 3)]
                else:
                    want = [(p + 1, i) for i in ahead.get(hd, ()) if p + 1 < PAIRS]
                    want += [(p, w) for at_hd, w in gates if at_hd == hd and p < PAIRS]
                jobs = []
                for q, i in want:
                    conved = TI_H <= i < TI_DT
                    jobs.append((k, q, i, n if conved else None))
                    k, n = k + 1, n + conved
                steps.append((g, jobs))
            return steps

        POOL_LOWS = HEADS_ALL - 6
        PROJECTIONS = PAIRS * (TI_DT + 1)
        gate_job = [job for _, jobs in ssm_schedule() for job in jobs if job[2] < EJ]

        def token_tiles(g):
            if g < 0:
                return 0, (0, 1, 2, 3)
            p, hd = divmod(g, NH)
            return p + 1, (0, 1, 2, 3) if hd == NH - 1 and p + 1 < PAIRS else ()

        def split_batches(g):
            q, hd = divmod(g + (g < 0), NH)
            return q, range(2) if q < PAIRS and hd == 0 and (q == 0) == (g < 0) else ()

        def convs(p, i):
            return p * CJ + (TI_B, TI_C, TI_H, TI_H + 1, TI_H + 2, TI_H + 3).index(i) + 1

        def ssm_loads():
            sp = nc.sync
            sp.wait_ge(o_added, GROUPS * 2 * PAIRS)
            sp.dma_start(in_raw[:], in_w).then_inc(m["loaded"], 16)
            sp.dma_start(cols[:], ssm_cols).then_inc(m["loaded"], 16)
            sp.dma_start(ow_raw[:], out_w).then_inc(m["loaded"], 16)

        def in_part(n):
            return in_raw[:, :, EJ * P:MJ * P] if n else in_raw[:, :, 0:EJ * P]

        def in_high(n):
            act = nc.scalar
            act.wait_ge(m["loaded"], 3 * 16)
            act.activation(in_parts[n][0][:], in_part(n), ACT.Copy).then_inc(m["in_hi_done"], 1)

        def in_low(n):
            pool = nc.gpsimd
            pool.wait_ge(m["in_hi_done"], n + 1)
            pool.tensor_tensor(in_parts[n][1][:], in_part(n), in_parts[n][0][:].bitcast(F32), ALU.subtract).then_inc(m["in_split"], 1)

        def out_scale():
            dve = nc.vector
            dve.wait_ge(m["loaded"], 3 * 16)
            for j in range(EJ):
                dve.tensor_scalar(ow_raw[:, j, :], ow_raw[:, j, :], norm_col(j), None, ALU.mult).then_inc(m["ow_scaled"], 1)

        def out_high():
            act = nc.scalar
            act.wait_ge(m["ow_scaled"], EJ)
            act.activation(ow_hi[:], ow_raw[:], ACT.Copy).then_inc(m["ow_hi_done"], 1)

        def out_low():
            pool = nc.gpsimd
            pool.wait_ge(m["ow_hi_done"], 1)
            pool.tensor_tensor(ow_lo[:], ow_raw[:], ow_hi[:].bitcast(F32), ALU.subtract).then_inc(m["ow_split"], 1)

        def ssm_constants():
            pool = nc.gpsimd
            pool.wait_ge(o_added, GROUPS * 2 * PAIRS)
            for b in range(2):
                pool.memset(start_row[:, b, 1, :], 0.0)
                for i in (0, 2):
                    pool.tensor_copy(start_row[:, b, i, :], ident[:])
            pool.memset(ones_col[:], 1.0).then_inc(m["start_ready"], 1)

        def ssm_sync():
            sp = nc.sync
            for p in range(PAIRS):
                sp.wait_ge(m["rows_ready"], p + 1)
                sp.dma_start(decay_dram[p], rows[:].rearrange("h b c -> h (b c)")).then_inc(m["rows_stored"], 16)
                sp.wait_ge(m["rows_stored"], 16 * p + 16)
                for hd in range(NH):
                    g = p * NH + hd
                    wait(sp, m["since_ready"], g - RING + 1)
                    sp.dma_start(decay_all[:, g % RING, :], decay_dram[p, hd ^ 1].partition_broadcast(P)).then_inc(decay_loaded[g % RING], 16)

        def low_parts(eng, g):
            eng.wait_ge(m["mix_hi_ready"], g + 1)
            wait(eng, m["yT_ready"], g - 1)
            eng.tensor_tensor(mix_lo[:, g % 2], mix[:, g % MIXES, :, 0:SEQ], mix_hi[:, g % 2].bitcast(F32), ALU.subtract) \
                .then_inc(m["mix_lo_ready"], 1)

        def ssm_pool(hooks):
            pool = nc.gpsimd
            for g, _ in ssm_schedule():
                if 0 <= g - 1 < POOL_LOWS:
                    low_parts(pool, g - 1)
                if 0 <= g < HEADS_ALL:
                    p = g // NH
                    pool.wait_ge(m["since_ready"], g + 1)
                    pool.wait_ge(m["gram_copied"], 2 * p + 2)
                    pool.tensor_tensor(mix[:, g % MIXES], mix[:, g % MIXES], gram[:, p % 2], ALU.mult).then_inc(m["mix_ready"], 1)
                w = (g - 4) // 2
                if g % 2 == 0 and 0 <= w < GATES:
                    k, _, _, _ = gate_job[w]
                    pool.wait_ge(bank_read[k % 3], k // 3 + 1)
                    pool.wait_ge(m["y_ready"], w + 1)
                    pool.tensor_tensor(y[:, w % 2, :], y[:, w % 2, :], silu_gate[:, w % 2, :], ALU.mult).then_inc(m["gated_ready"], 1)
                w = (g - 6) // 2
                if g % 2 == 0 and 0 <= w < GATES and w % EJ:
                    p, j = divmod(w, EJ)
                    pool.wait_ge(m["square_ready"], w + 1)
                    wait(pool, m["square_added"], (EJ - 1) * p + j - 1)
                    pool.tensor_tensor(square_sum[:], square_sum[:], square[:], ALU.add).then_inc(m["square_added"], 1)
                if g in hooks:
                    hooks[g]()

        def ssm_scalar(hooks):
            act = nc.scalar
            act.wait_ge(m["loaded"], 3 * 16)
            act.activation(a_col[0:NH, :], a_log, ACT.Exp).then_inc(m["a_exp"], 1)
            act.wait_ge(m["a_ready"], 1)

            def log_steps(q):
                act.wait_ge(m["z_ready"], q + 1)
                act.activation(neg_abs, neg_abs, ACT.Exp).then_inc(m["exp_ready"], 1)
                act.wait_ge(m["exp_ready"], q + 1)
                act.activation(neg_abs, neg_abs, ACT.Ln, bias=1.0).then_inc(m["log_ready"], 1)

            def step_decays(q):
                act.wait_ge(m["dt_ready"], q + 1)
                steps = dt[:].rearrange("h (b t) -> h b t", b=2)
                act.activation(rows[:, :, 0:SEQ], steps, ACT.Exp, scale=a_col[0:NH, :])
                act.activation(rows[:, :, SEQ:ROW], steps[:, :, P:SEQ], ACT.Exp, scale=a_col[0:NH, :]).then_inc(m["decay_ready"], 1)

            def projected(k, q, i, n):
                bank = psum[:, PROJ_BANKS[k % 3], :]
                if n is not None:
                    if q == 0:
                        act.wait_ge(m["in_split"], 2)
                        act.wait_ge(m["ow_split"], 1)
                    if q >= 2:
                        act.wait_ge(m["y_ready"], (q - 1) * EJ)
                    act.wait_ge(m["proj_ready"], k + 1)
                    act.activation(conv[q % 2][:, i - EJ, :], bank, ACT.Identity, bias=tap(i - EJ, TAPS),
                                   scale=tap(i - EJ, TAPS - 1)).then_inc(m["tap_ready"], 1)
                elif i < EJ:
                    w = q * EJ + i
                    wait(act, m["gated_ready"], w - 1)
                    act.wait_ge(m["proj_ready"], k + 1)
                    act.activation(silu_gate[:, w % 2, :], bank, ACT.Silu).then_inc(bank_read[k % 3], 1)

            def conv_silu(k, q, i, n):
                if n is not None:
                    act.wait_ge(bank_read[k % 3], k // 3 + 1)
                    act.activation(conv[q % 2][:, i - EJ, :], conv[q % 2][:, i - EJ, :], ACT.Silu).then_inc(m["conv_ready"], 1)

            schedule = ssm_schedule()
            for g, jobs in schedule:
                if g < 0:
                    for i, job in enumerate(jobs):
                        projected(*job)
                        if i == 1:
                            log_steps(0)
                        if i == 2:
                            step_decays(0)
                        if i >= 2:
                            conv_silu(*jobs[i - 1])
                    conv_silu(*jobs[-1])
                p, hd = divmod(g, NH)
                if g < 0 or p < PAIRS - 1 and hd - 1 in GRAM_STEPS:
                    q = max(p + 1, 0)
                    for b in range(2) if g < 0 else (hd - 1 - GRAM_STEPS[0],):
                        act.wait_ge(m["gram_ready"], 2 * q + b + 1)
                        wait(act, m["mix_ready"], (q - 1) * NH)
                        act.activation(gram[:, q % 2, b], psum[:, GRAM_BANK, 0:ROW], ACT.Copy).then_inc(m["gram_copied"], 1)
                if g >= 1:
                    for job in schedule[g][1]:
                        projected(*job)
                p, hd = divmod(g, NH)
                if 0 <= p < PAIRS - 1 and hd == 2:
                    step_decays(p + 1)
                if g >= 2:
                    for job in schedule[g - 1][1]:
                        conv_silu(*job)
                if g >= 0:
                    q, batches = split_batches(g)
                    for b in batches:
                        act.wait_ge(m["h_tok_ready"], 4 * q + 2 * b + 1)
                        wait(act, m["yT_ready"], (q - 1) * NH)
                        act.activation(h_hi[q % 2][:, b, :], h_tok[q % 2][:, 2 * b, :], ACT.Copy).then_inc(m["h_hi_ready"], 1)
                p, hd = divmod(g, NH)
                if 0 <= p < PAIRS - 1 and hd == 1:
                    log_steps(p + 1)
                if 0 <= g < HEADS_ALL:
                    act.wait_ge(m["mix_ready"], g + 1)
                    wait(act, m["yT_ready"], g - 1)
                    act.activation(mix_hi[:, g % 2], mix[:, g % MIXES, :, 0:SEQ], ACT.Copy).then_inc(m["mix_hi_ready"], 1)
                if g < 0:
                    q, batches = split_batches(g)
                    for b in batches:
                        act.wait_ge(m["h_tok_ready"], 4 * q + 2 * b + 1)
                        wait(act, m["yT_ready"], (q - 1) * NH)
                        act.activation(h_hi[q % 2][:, b, :], h_tok[q % 2][:, 2 * b, :], ACT.Copy).then_inc(m["h_hi_ready"], 1)
                w = (g - 5) // 2
                if g % 2 and 0 <= w < GATES:
                    p, j = divmod(w, EJ)
                    act.wait_ge(m["gated_ready"], w + 1)
                    if j == 0:
                        wait(act, m["out_ready"], 2 * p)
                        wait(act, m["sum_ready"], p)
                        act.activation(square_sum[:], y[:, w % 2, :], ACT.Square).then_inc(m["square_ready"], 1)
                    else:
                        wait(act, m["square_added"], (EJ - 1) * p + j - 1)
                        act.activation(square[:], y[:, w % 2, :], ACT.Square).then_inc(m["square_ready"], 1)
                    act.activation(y_hi[:, j, :], y[:, w % 2, :], ACT.Copy).then_inc(m["y_hi_ready"], 1)
                if g in hooks:
                    hooks[g]()

        def ssm_vector(hooks):
            dve = nc.vector
            dve.wait_ge(m["a_exp"], 1)
            dve.tensor_scalar(a_col[0:NH, :], a_col[0:NH, :], -1.0, None, ALU.mult).then_inc(m["a_ready"], 1)
            dve.wait_ge(m["start_ready"], 1)

            def decays(g):
                dve.wait_ge(decay_loaded[g % RING], 16 * (g // RING) + 16)
                wait(dve, m["yT_ready"], g - MIXES + 1)
                wait(dve, m["mix_lo_ready"], g - MIXES + 1)
                dve.tensor_tensor_scan(mix[:, g % MIXES].rearrange("p b c -> p (b c)"), decay_all[:, g % RING, :],
                                       start_row[:].rearrange("p b i c -> p (b i c)"), 0.0, ALU.mult, ALU.add).then_inc(m["since_ready"], 1)

            def outputs(w):
                p, j = divmod(w, EJ)
                dve.wait_ge(m["yT_ready"], 2 * w + 2)
                wait(dve, m["y_lo_ready"], w - 1)
                dve.scalar_tensor_tensor(y[:, w % 2, :], conv[p % 2][:, j, :], skip_col(j), psum[:, YT_BANK + w % 2, :],
                                         ALU.mult, ALU.add).then_inc(m["y_ready"], 1)

            def steps_dt(k, q):
                bank = psum[0:NH, PROJ_BANKS[k % 3], :]
                dve.wait_ge(m["proj_ready"], k + 1)
                wait(dve, m["dtT_ready"], q)
                wait(dve, m["decay_ready"], q)
                dve.tensor_scalar(dt[:], bank, dt_bias, None, ALU.add).then_inc(bank_read[k % 3], 1)
                dve.wait_ge(bank_read[k % 3], k // 3 + 1)
                wait(dve, m["rows_stored"], 16 * q)
                dve.tensor_scalar(neg_abs, dt[:], -1.0, None, ALU.mult).then_inc(m["z_step"], 1)
                dve.wait_ge(m["z_step"], q + 1)
                dve.tensor_tensor(neg_abs, neg_abs, dt[:], ALU.min).then_inc(m["z_ready"], 1)

            def steps_sum(q):
                dve.wait_ge(m["log_ready"], q + 1)
                dve.scalar_tensor_tensor(dt[:], dt[:], 0.0, neg_abs, ALU.max, ALU.add).then_inc(m["dt_ready"], 1)

            def starts(q):
                dve.wait_ge(m["decay_ready"], q + 1)
                dve.memset(rows[:].rearrange("h b (i c) -> h b i c", i=3)[:, :, 0:3:2, 0:1], 0.0).then_inc(m["rows_ready"], 1)

            def taps(k, q, i, n):
                dve.wait_ge(m["tap_ready"], n + 1)
                for e in range(1, TAPS):
                    to = conv[q % 2][:, i - EJ, :].rearrange("p (b t) -> p b t", b=2)[:, :, e:SEQ]
                    of = psum[:, PROJ_BANKS[k % 3], :].rearrange("p (b t) -> p b t", b=2)[:, :, 0:SEQ - e]
                    ins = dve.scalar_tensor_tensor(to, of, tap(i - EJ, TAPS - 1 - e), to, ALU.mult, ALU.add)
                    if e < TAPS - 1:
                        ins.then_inc(m["tap_step"], 1)
                        dve.wait_ge(m["tap_step"], n * (TAPS - 2) + e)
                ins.then_inc(bank_read[k % 3], 1)

            def projected(k, q, i, n):
                if i == TI_DT:
                    steps_dt(k, q)
                elif n is not None:
                    taps(k, q, i, n)

            schedule = ssm_schedule()
            for g, jobs in schedule:
                p, hd = divmod(g, NH)
                if 0 <= p < PAIRS - 1 and hd == 2:
                    steps_sum(p + 1)
                e, rest = divmod(g - 14, NH)
                if e >= 0 and rest == 0:
                    dve.wait_ge(m["sum_ready"], e + 1)
                    dve.tensor_scalar(mean_sq[:], psum[:, GRAM_BANK, SUM_COL:SUM_COL + 4], 1.0 / E, SSM_EPS, ALU.mult, ALU.add) \
                        .then_inc(m["mean_ready"], 1)
                if 0 < g + 1 < HEADS_ALL:
                    decays(g + 1)
                if POOL_LOWS <= g - 1 < HEADS_ALL:
                    low_parts(dve, g - 1)
                if g < 0:
                    for i, job in enumerate(jobs):
                        projected(*job)
                        if i == 1:
                            steps_sum(0)
                        if i == 2:
                            starts(0)
                        if ("first", i) in hooks:
                            hooks["first", i]()
                    decays(0)
                if g >= 1:
                    for job in schedule[g][1]:
                        projected(*job)
                p, hd = divmod(g, NH)
                if 0 <= p < PAIRS - 1 and hd == 2:
                    starts(p + 1)
                if g % 2 and 0 <= (g - 3) // 2 < GATES:
                    outputs((g - 3) // 2)
                if g >= 0:
                    q, batches = split_batches(g)
                    for b in batches:
                        dve.wait_ge(m["h_hi_ready"], 2 * q + b + 1)
                        wait(dve, m["yT_ready"], (q - 1) * NH)
                        dve.tensor_tensor(h_lo[q % 2][:, b, :], h_tok[q % 2][:, 2 * b, :], h_hi[q % 2][:, b, :].bitcast(F32),
                                           ALU.subtract).then_inc(m["h_lo_ready"], 1)
                w = (g - 6) // 2
                if g % 2 == 0 and 0 <= w < GATES:
                    dve.wait_ge(m["y_hi_ready"], w + 1)
                    dve.tensor_tensor(y_lo[:, w % EJ, :], y[:, w % 2, :], y_hi[:, w % EJ, :].bitcast(F32), ALU.subtract).then_inc(m["y_lo_ready"], 1)
                if g < 0 or p < PAIRS - 1 and hd == 6:
                    q = max(p + 1, 0)
                    dve.wait_ge(m["dtT_ready"], q + 1)
                    dve.tensor_copy(dt_tok[:], psum[:, GRAM_BANK, DT_COL:SUM_COL].rearrange("p (t h) -> p t h", h=NH)).then_inc(m["dt_tok_ready"], 1)
                q, tiles = token_tiles(g)
                for t in tiles:
                    if t == 0:
                        dve.wait_ge(m["dt_tok_ready"], q + 1)
                    dve.wait_ge(m["hT_ready"], 4 * q + t + 1)
                    wait(dve, m["yT_ready"], (q - 1) * NH)
                    wait(dve, m["h_lo_ready"], 2 * (q - 1))
                    dve.tensor_tensor(h_tok[q % 2][:, t, :].rearrange("p (h c) -> p h c", h=NH),
                                      psum[:, HT_BANKS[t % 2], :].rearrange("p (h c) -> p h c", h=NH),
                                      dt_tok[:, t, :].rearrange("p (h a) -> p h a", a=1).to_broadcast([P, NH, HP]), ALU.mult).then_inc(m["h_tok_ready"], 1)
                if g < 0:
                    q, batches = split_batches(g)
                    for b in batches:
                        dve.wait_ge(m["h_hi_ready"], 2 * q + b + 1)
                        wait(dve, m["yT_ready"], (q - 1) * NH)
                        dve.tensor_tensor(h_lo[q % 2][:, b, :], h_tok[q % 2][:, 2 * b, :], h_hi[q % 2][:, b, :].bitcast(F32),
                                           ALU.subtract).then_inc(m["h_lo_ready"], 1)
                e, rest = divmod(g - 14, NH)
                if e >= 0 and rest == 0:
                    dve.wait_ge(m["mean_ready"], e + 1)
                    inverse_root(rms[:], mean_sq[:], rms_tmp[:], m["root_step"], ROOT_STEPS * e)
                    for t in range(4):
                        if t % 2 == 0:
                            dve.wait_ge(m["out_ready"], 2 * e + t // 2 + 1)
                        dve.scalar_tensor_tensor(x[:, 4 * e + t, :], psum[:, OUT_BANKS[t // 2], t % 2 * D:(t % 2 + 1) * D], rms[:, t:t + 1],
                                                 x[:, 4 * e + t, :], ALU.mult, ALU.add).then_inc(m["out_added"], 1)
                if g in hooks:
                    hooks[g]()

        def ssm_tensor(hooks):
            pe = nc.tensor
            pe.wait_ge(m["in_split"], 2)
            pe.wait_ge(m["start_ready"], 1)

            def products(g):
                p, hd = divmod(g, NH)
                if hd == 0:
                    pe.wait_ge(m["h_tok_ready"], 4 * p + 4)
                    pe.wait_ge(m["h_lo_ready"], 2 * p + 2)
                wait(pe, m["y_ready"], g // 2 - 1)
                pe.wait_ge(m["mix_lo_ready"], g + 1)
                for b in range(2):
                    n = HP if hd % 2 else 2 * HP
                    c = slice(hd // 2 * 2 * HP, hd // 2 * 2 * HP + n)
                    to = psum[0:n, YT_BANK + g // 2 % 2, b * SEQ:(b + 1) * SEQ]
                    chain(to, passes(h_hi[p % 2][:, b, c], h_lo[p % 2][:, b, c], mix_hi[:, g % 2, b, :], mix_lo[:, g % 2, b, :]),
                          stop=False, skip_group_check=True)
                    last = pe.matmul(to[:, P:SEQ], h_tok[p % 2][:, 2 * b + 1, c], mix[:, g % MIXES, b, SEQ:ROW],
                                     start=False, stop=True, skip_group_check=True)
                last.then_inc(m["yT_ready"], 1)

            def squares(p):
                pe.wait_ge(m["square_added"], (EJ - 1) * (p + 1))
                pe.wait_ge(m["gram_copied"], 2 * min(p + 3, PAIRS))
                for t in range(4):
                    last = pe.matmul(psum[:, GRAM_BANK, SUM_COL + t:SUM_COL + t + 1], square_sum[:, t * P:(t + 1) * P], ones_col[:],
                                     start=True, stop=True)
                last.then_inc(m["sum_ready"], 1)

            def project_out(p):
                pe.wait_ge(m["y_lo_ready"], EJ * p + EJ)
                pe.wait_ge(m["ow_split"], 1)
                pe.wait_ge(m["h_tok_ready"], 4 * min(p + 2, PAIRS))
                wait(pe, m["out_added"], 4 * p)
                for t in range(4):
                    pairs = []
                    for j in range(EJ):
                        s = slice(t * P, (t + 1) * P)
                        pairs += passes(y_hi[:, j, s], y_lo[:, j, s], ow_hi[:, j, :], ow_lo[:, j, :])
                    last = chain(psum[:, OUT_BANKS[t // 2], t % 2 * D:(t % 2 + 1) * D], pairs)
                    if t % 2:
                        last.then_inc(m["out_ready"], 1)

            def turn_steps(q):
                pe.wait_ge(m["dt_ready"], q + 1)
                pe.wait_ge(m["gram_copied"], 2 * q + 2)
                wait(pe, m["mean_ready"], q - 1)
                for i in range(4):
                    last = pe.transpose(psum[:, GRAM_BANK, DT_COL + i * NH:DT_COL + (i + 1) * NH], dt[:, i * P:(i + 1) * P], ident[0:NH, 0:NH])
                last.then_inc(m["dtT_ready"], 1)

            def keys_rows(q, b):
                pe.wait_ge(m["conv_ready"], convs(q, TI_C))
                if b == 0:
                    wait(pe, m["dt_tok_ready"], q)
                    wait(pe, m["mean_ready"], q - 2)
                else:
                    pe.wait_ge(m["gram_copied"], 2 * q + 1)
                for i in range(2):
                    keys = conv[q % 2][0:NS, EJ, b * SEQ + i * P:b * SEQ + (i + 1) * P]
                    later = conv[q % 2][0:NS, EJ + 1, b * SEQ + i * P:(b + 1) * SEQ]
                    last = pe.matmul(psum[:, GRAM_BANK, 2 * i * P:(2 + i) * P], keys, later, start=True, stop=True)
                last.then_inc(m["gram_ready"], 1)

            def turns(q):
                pe.wait_ge(m["conv_ready"], convs(q, TI_H + EJ - 1))
                wait(pe, m["out_added"], 4 * (q - 1))
                wait(pe, lnT_lo, 4 * LNT if q else 0)
                for t in range(4):
                    wait(pe, m["h_tok_ready"], 4 * q + t - 1)
                    for j in range(EJ):
                        last = pe.transpose(psum[:, HT_BANKS[t % 2], j * P:(j + 1) * P], conv[q % 2][:, j, t * P:(t + 1) * P], ident[:])
                    last.then_inc(m["hT_ready"], 1)

            def project(k, q, i, n):
                if i == TI_DT:
                    pe.wait_ge(lnT_lo, (2 + q // 2 + 1) * LNT)
                wait(pe, bank_read[k % 3], k // 3)
                if k == 2:
                    pe.wait_ge(expert_layers[0]["y_added"], 8)
                hi, lo = in_parts[i >= EJ]
                col = (i - EJ if i >= EJ else i) * P
                v, t = slice(col, col + P), slice(q * PT, (q + 1) * PT)
                pairs = []
                for c in range(DC):
                    pairs += passes(hi[:, c, v], lo[:, c, v], xT_hi[:, c, t], xT_lo[:, c, t])
                chain(psum[:, PROJ_BANKS[k % 3], :], pairs).then_inc(m["proj_ready"], 1)

            for g, jobs in ssm_schedule():
                for job in jobs[:1]:
                    project(*job)
                if 0 <= g - 1 < HEADS_ALL:
                    products(g - 1)
                for job in jobs[1:]:
                    project(*job)
                p, rest = divmod(g - 13, NH)
                if p >= 0 and rest == 0:
                    squares(p)
                    project_out(p)
                if g < 0:
                    for b in range(2):
                        keys_rows(0, b)
                    turn_steps(0)
                    turns(0)
                p, hd = divmod(g, NH)
                if 0 <= p < PAIRS - 1:
                    if hd in GRAM_STEPS:
                        keys_rows(p + 1, hd - GRAM_STEPS[0])
                    if hd == 6:
                        turn_steps(p + 1)
                    if hd == 7:
                        turns(p + 1)
                if g in hooks:
                    hooks[g]()

        block = ctx.enter_context(nc.Block())

        @block.sync
        def _(sp):
            def store(h, quad, quads):
                t0, n = h * HALF_TILES + 4 * quad, 4 * quads
                sp.wait_ge(ln_done, (NORMS - 1) * TILES + t0 + n)
                sp.dma_start(out.rearrange("(i p) d -> p i d", p=P)[:, t0:t0 + n, :], x[:, t0:t0 + n, :]).then_inc(stored, 16)

            for q in range(PAIRS):
                sp.dma_start(xT_raw[:, :, q * BANK:(q + 1) * BANK],
                             x_cols.rearrange("(c p) t -> p c t", p=P)[:, :, q * BANK:(q + 1) * BANK]).then_inc(xT_loaded[q], 16)
                if q == 0:
                    sp.dma_start(aw_raw[:], attn_w[0]).then_inc(aw_loaded, 16)
            sp.dma_start(x[:], x_rows.rearrange("(i p) d -> p i d", p=P)).then_inc(x_loaded, 16)
            with sp.Fori(1, GROUPS) as g:
                sp.wait_ge(aw_split, 4 * g)
                sp.dma_start(aw_raw[:], attn_w[bass.ds(g, 1)].rearrange("a p n -> p (a n)")).then_inc(aw_loaded, 16)
            sp.wait_ge(ones_ready, 1)
            sp.dma_start(ones_dram, ones_row[:]).then_inc(ones_stored, 16)
            sp.wait_ge(ones_stored, 16)
            l0, l1 = expert_layers
            experts_sync(l0, {3: ssm_loads})
            ssm_sync()
            sp.wait_ge(m["y_ready"], (PAIRS - 1) * EJ)
            experts_sync(l1, {l1["tiles"] + 4: lambda: store(0, 0, 2)})
            store(1, 0, 1)
            store(1, 1, 1)
            sp.wait_ge(stored, 16 * 3)

        @block.gpsimd
        def _(pool):
            pool.memset(ones_row[:], 1.0).then_inc(ones_ready, 1)
            pool.memset(ident[:], 0.0).then_inc(const_ready, 1)
            pool.memset(causal[:], 0.0).then_inc(const_ready, 1)
            pool.wait_ge(const_ready, 2)
            pool.affine_select(out=ident[:], in_=ident[:], compare_op=ALU.not_equal, fill=1.0, base=0,
                               pattern=[[-1, P]], channel_multiplier=1).then_inc(const_ready, 1)
            pool.affine_select(out=causal[:, P:2 * P], in_=causal[:, P:2 * P], compare_op=ALU.is_ge, fill=MASKED,
                               base=0, pattern=[[-1, P]], channel_multiplier=1).then_inc(const_ready, 1)

            def low_part(g, part):
                pool.wait_ge(aw_hi_done, 4 * g + part + 1)
                w = slice(part * WK, (part + 1) * WK)
                pool.tensor_tensor(aw_lo[:, w], aw_raw[:, w], aw_hi[:, w].bitcast(F32), ALU.subtract).then_inc(aw_split, 1)

            for part in range(4):
                low_part(0, part)
            with pool.Fori(1, GROUPS) as g:
                for part in range(4):
                    low_part(g, part)
            l0, l1 = expert_layers
            gate_start(l0)
            for part in range(2):
                weights_low(l0, 0, 0, part)
            experts_pool(l0, {(0, 1): ssm_constants, (0, l0["tiles"] - 1): lambda: in_low(0), (1, 0): lambda: in_low(1), (1, 1): out_low})
            def next_weights():
                for part in range(2):
                    weights_low(l1, 0, 0, part)

            ssm_pool({26: lambda: gate_start(l1), 34: next_weights})
            experts_pool(l1, {})

        @block.scalar
        def _(act):
            def tokens_high(q):
                act.wait_ge(xT_loaded[q], 16)
                act.activation(xT_hi[:, :, q * BANK:(q + 1) * BANK], xT_raw[:, :, q * BANK:(q + 1) * BANK],
                               ACT.Copy).then_inc(xT_hi_ready, 1)

            def high_part(g, part):
                if part == 0:
                    act.wait_ge(aw_loaded, 16 * g + 16)
                w = slice(part * WK, (part + 1) * WK)
                act.activation(aw_hi[:, w], aw_raw[:, w], ACT.Copy).then_inc(aw_hi_done, 1)

            def qkv_high(g, bp, j):
                n = g * (PAIRS * JOBS) + bp * JOBS + j
                act.wait_ge(qkv_ready, n + 1)
                dst = (kT_hi if j % 2 else qT_hi)[:, bp % 2, j // 2, :] if j < 2 * HG else v_hi[:, bp % 2, j - 2 * HG, :]
                act.activation(dst, psum[:, QKV_BANK + j % 2, :], ACT.Copy).then_inc(qkv_hi, 1)

            def group(g, next_group, hooks={}):
                for i, jobs, more_jobs, u_s, u_t, u_v, u_o in attn_schedule(next_group):
                    if i == 2:
                        wait(act, o_ready, g * (2 * PAIRS))
                        high_part(g, 3)
                    if 10 <= i < 13 and next_group:
                        act.wait_ge(qkv_ready, (g + 1) * (PAIRS * JOBS) - (3, 2, 0)[i - 10])
                        high_part(g + 1, i - 10)
                    if u_s is not None:
                        u = u_s
                        act.wait_ge(s_masked, g * UNITS + u + 1)
                        if u >= 3:
                            act.wait_ge(pT_ready, g * UNITS + u - 2)
                        act.activation(p_sb[:, u % 3, 0:P], s_sb[:, u % 2, 0:P], ACT.Exp, bias=neg_max[:, u % 3, 0:1], scale=-1.0,
                                       accum_out=row_sum[:, u % 3, 0:1])
                        act.activation(p_sb[:, u % 3, P:3 * P], s_sb[:, u % 2, P:3 * P], ACT.Exp, bias=neg_max[:, u % 3, 1:2], scale=-1.0,
                                       accum_out=row_sum[:, u % 3, 1:2]).then_inc(p_ready, 1)
                    for bp, j in jobs:
                        qkv_high(g, bp, j)
                    if u_t is not None:
                        u = u_t
                        act.wait_ge(pT_ready, g * UNITS + u + 1)
                        act.activation(pT_hi[:, u % 2, :], psum[:, PT_BANK, 0:3 * P], ACT.Copy).then_inc(pT_hi_ready, 1)
                    if u_v is not None:
                        u = u_v
                        act.wait_ge(z_ready, g * UNITS + u + 1)
                        act.activation(zT_hi[:, u % 2, :], psum[:, Z_BANK, 0:SEQ], ACT.Copy).then_inc(z_hi_ready, 1)
                    for bp, j in more_jobs:
                        qkv_high(g, bp, j)
                    if i in hooks:
                        hooks[i]()

            def first_weights():
                for part in range(2):
                    weights_high(expert_layers[0], 0, 0, part)

            def first_logits():
                gate_logits_copy(expert_layers[0], 0, FIRST_GATE_BANKS)
                gate_score(expert_layers[0], 0, FIRST_GATE_BANKS[2])

            last_hooks = {6: first_weights, 15: lambda: ln_highs(0, 0, FIRST_NORM_BANKS), 17: lambda: ln_highs(0, 1, FIRST_NORM_BANKS),
                          18: first_logits}
            tokens_high(0)
            for part in range(3):
                high_part(0, part)
            for j in range(JOBS):
                qkv_high(0, 0, j)
                if j < PAIRS - 1:
                    tokens_high(j + 1)
            group(0, True)
            with act.Fori(1, GROUPS - 1) as g:
                group(g, True)
            group(GROUPS - 1, False, last_hooks)
            l0, l1 = expert_layers

            def second_norm(f):
                u = 2 * f["norm"] + 1
                for quad in range(2):
                    ln_highs(u, quad, NORM_BANKS)
                gate_logits_copy(f, 1, GATE_BANKS)

            def last_split():
                in_high(1)
                out_high()

            experts_scalar(l0, {(0, l0["tiles"] - 1): lambda: in_high(0), (1, 0): last_split}, lambda: second_norm(l0), True)
            def turned_highs(u, quad):
                return lambda: ln_highs(u, quad, HT_BANKS)

            hooks = {3: turned_highs(3, 0), 5: turned_highs(3, 1)}
            def next_weights():
                for part in range(2):
                    weights_high(l1, 0, 0, part)

            hooks.update({31: turned_highs(4, 0), 32: turned_highs(4, 1), 30: next_weights,
                          33: lambda: gate_logits_copy(l1, 0, SSM_GATE_BANKS), 35: lambda: gate_score(l1, 0, SSM_GATE_BANKS[2])})
            ssm_scalar(hooks)
            experts_scalar(l1, {(0, 0): lambda: gate_score(l1, 1, GATE_BANKS[2])}, lambda: second_norm(l1), False)

        @block.vector
        def _(dve):
            def tokens_low(q):
                dve.wait_ge(xT_hi_ready, q + 1)
                dve.tensor_tensor(xT_lo[:, :, q * BANK:(q + 1) * BANK], xT_raw[:, :, q * BANK:(q + 1) * BANK],
                                  xT_hi[:, :, q * BANK:(q + 1) * BANK].bitcast(F32), ALU.subtract).then_inc(xT_lo_ready, 1)

            def qkv_low(g, bp, j):
                n = g * (PAIRS * JOBS) + bp * JOBS + j
                dve.wait_ge(qkv_hi, n + 1)
                if j < 2 * HG:
                    hi, lo = ((kT_hi, kT_lo) if j % 2 else (qT_hi, qT_lo))
                    hi, lo = hi[:, bp % 2, j // 2, :], lo[:, bp % 2, j // 2, :]
                else:
                    hi, lo = v_hi[:, bp % 2, j - 2 * HG, :], v_lo[:, bp % 2, j - 2 * HG, :]
                dve.tensor_tensor(lo, psum[:, QKV_BANK + j % 2, :], hi.bitcast(F32), ALU.subtract).then_inc(qkv_lo, 1)

            def group(g, next_group, hooks={}):
                for i, jobs, more_jobs, u_s, u_t, u_v, u_o in attn_schedule(next_group):
                    if u_s is not None:
                        u = u_s
                        if u >= 2:
                            dve.wait_ge(p_ready, g * UNITS + u - 1)
                        hold(dve, s_ready, g * UNITS + u + 1)
                        dve.tensor_tensor_reduce(s_sb[:, u % 2, 0:P], psum[:, S_BANK + u % 2, 0:P], causal[:, P:2 * P], -SCALE, 3e38,
                                                 ALU.add, ALU.min, neg_max[:, u % 3, 0:1])
                        dve.tensor_tensor_reduce(s_sb[:, u % 2, P:3 * P], psum[:, S_BANK + u % 2, P:3 * P], causal[:], -SCALE, 3e38,
                                                 ALU.add, ALU.min, neg_max[:, u % 3, 1:2]).then_inc(s_masked, 1)
                    if 0 <= i - 1 < UNITS:
                        u = i - 1
                        dve.wait_ge(p_ready, g * UNITS + u + 1)
                        dve.reciprocal(row_inv[:, u % 3, :], row_sum[:, u % 3, :]).then_inc(r_ready, 1)
                        dve.wait_ge(r_ready, g * UNITS + u + 1)
                        dve.tensor_scalar(p_sb[:, u % 3, 0:P], p_sb[:, u % 3, 0:P], row_inv[:, u % 3, 0:1], None, ALU.mult)
                        dve.tensor_scalar(p_sb[:, u % 3, P:3 * P], p_sb[:, u % 3, P:3 * P], row_inv[:, u % 3, 1:2], None,
                                          ALU.mult).then_inc(p_scaled, 1)
                    for bp, j in jobs:
                        qkv_low(g, bp, j)
                    if u_t is not None:
                        u = u_t
                        dve.wait_ge(pT_hi_ready, g * UNITS + u + 1)
                        dve.tensor_tensor(pT_lo[:, u % 2, :], psum[:, PT_BANK, 0:3 * P], pT_hi[:, u % 2, :].bitcast(F32),
                                          ALU.subtract).then_inc(pT_lo_ready, 1)
                    if u_v is not None:
                        u = u_v
                        dve.wait_ge(z_hi_ready, g * UNITS + u + 1)
                        dve.tensor_tensor(zT_lo[:, u % 2, :], psum[:, Z_BANK, 0:SEQ], zT_hi[:, u % 2, :].bitcast(F32),
                                          ALU.subtract).then_inc(z_lo_ready, 1)
                    for bp, j in more_jobs:
                        qkv_low(g, bp, j)
                    if u_o is not None and unit(u_o)[1] == HG - 1:
                        bp, _, b = unit(u_o)
                        dve.wait_ge(o_ready, g * (2 * PAIRS) + 2 * bp + b + 1)
                        rows = x[:, 4 * bp + 2 * b:4 * bp + 2 * b + 2, :]
                        dve.tensor_tensor(rows, psum[:, O_BANK + b, :].rearrange("p (i d) -> p i d", i=2), rows,
                                          ALU.add).then_inc(o_added, 1)
                    if i in hooks:
                        hooks[i]()

            def quad_stats(quad):
                return lambda: ln_stats(quad // 2, quad % 2, o_added, (GROUPS - 1) * 2 * PAIRS + 2 * quad + 2)

            def first_rows():
                ln_scales(0)
                ln_rows(0, 0)

            def first_choice():
                gate_read(expert_layers[0], 0, FIRST_GATE_BANKS[2])
                gate_choose(expert_layers[0], 0)

            last_hooks = {8: quad_stats(0), 12: quad_stats(1), 13: first_rows, 14: lambda: ln_rows(0, 1), 15: lambda: ln_lows(0, 0, FIRST_NORM_BANKS),
                          16: quad_stats(2), 17: lambda: ln_lows(0, 1, FIRST_NORM_BANKS), 18: first_choice}
            tokens_low(0)
            for j in range(JOBS):
                qkv_low(0, 0, j)
                if j < PAIRS - 1:
                    tokens_low(j + 1)
            dve.wait_ge(const_ready, 4)
            dve.wait_ge(x_loaded, 16)
            group(0, True)
            with dve.Fori(1, GROUPS - 1) as g:
                group(g, True)
            group(GROUPS - 1, False, last_hooks)
            l0, l1 = expert_layers

            def second_norm(f):
                u = 2 * f["norm"] + 1
                ln_scales(u)
                for quad in range(2):
                    ln_rows(u, quad)
                gate_copy(f, 0, FIRST_TURN_BANKS)
                for quad in range(2):
                    ln_lows(u, quad, NORM_BANKS)

            def both_stats(u, ready):
                for quad in range(2):
                    ln_stats(u, quad, ready, 2 * quad + 2)

            def both_rows(u):
                ln_scales(u)
                for quad in range(2):
                    ln_rows(u, quad)

            ln_stats(1, 1, o_added, (GROUPS - 1) * 2 * PAIRS + 8)
            second_norm(l0)

            experts_vector(l0, {(0, 0): lambda: gate_groups(l0, 1), (0, 1): lambda: gate_choose(l0, 1),
                                (0, l0["tiles"] - 1): out_scale, (1, 0): lambda: both_stats(2, l0["y_added"]), (1, 1): lambda: both_rows(2)}, True)
            def turned_lows(u, quad):
                return lambda: ln_lows(u, quad, HT_BANKS)

            hooks = {("first", 2): lambda: ln_scales(3), 0: lambda: ln_rows(3, 0), 1: lambda: ln_rows(3, 1), 3: turned_lows(3, 0), 5: turned_lows(3, 1)}
            def next_rows():
                ln_scales(4)
                ln_rows(4, 0)

            def next_logits():
                gate_read(l1, 0, SSM_GATE_BANKS[2])
                gate_groups(l1, 0)

            hooks.update({24: lambda: ln_stats(4, 0, m["out_added"], 4), 25: lambda: ln_stats(4, 1, m["out_added"], 8), 27: next_rows,
                          28: lambda: ln_rows(4, 1), 31: turned_lows(4, 0), 32: turned_lows(4, 1), 34: lambda: ln_stats(5, 0, m["out_added"], 12),
                          35: next_logits, 36: lambda: gate_choose(l1, 0)})
            ssm_vector(hooks)
            ln_stats(5, 1, m["out_added"], 16)
            second_norm(l1)
            experts_vector(l1, {(0, 0): lambda: gate_groups(l1, 1), (0, 1): lambda: gate_choose(l1, 1),
                                (1, 0): lambda: both_stats(6, l1["y_added"]), (1, 1): lambda: both_rows(6)}, False)
            both_rows(7)

        @block.tensor
        def _(pe):
            def qkv_job(g, bp, j):
                n = g * (PAIRS * JOBS) + bp * JOBS + j
                if not isinstance(n, int) or n >= 2:
                    pe.wait_ge(qkv_lo, n - 1)
                if bp % PAIRS == 0 and j in (0, 1, 2 * HG):
                    pe.wait_ge(aw_split, 4 * (g + bp // PAIRS) + (1, 2, 3)[min(j, 2)])
                if bp < PAIRS and j == 0:
                    pe.wait_ge(xT_lo_ready, bp + 1)
                bp %= PAIRS
                bank = psum[:, QKV_BANK + j % 2, :]
                if j < 2 * HG:
                    w0 = (WK if j % 2 else WQ) + j // 2 * DC * DH
                    pairs = []
                    for c in range(DC):
                        w = slice(w0 + c * DH, w0 + (c + 1) * DH)
                        m = slice(bp * BANK, (bp + 1) * BANK)
                        pairs += passes(aw_hi[:, w], aw_lo[:, w], xT_hi[:, c, m], xT_lo[:, c, m])
                    chain(bank, pairs).then_inc(qkv_ready, 1)
                else:
                    for i in range(2):
                        t0 = bp * BANK + (2 * (j - 2 * HG) + i) * P
                        pairs = []
                        for c in range(DC):
                            w = slice(WV + c * HG * DH, WV + (c + 1) * HG * DH)
                            pairs += passes(xT_hi[:, c, t0:t0 + P], xT_lo[:, c, t0:t0 + P], aw_hi[:, w], aw_lo[:, w])
                        last = chain(bank[:, i * HG * DH:(i + 1) * HG * DH], pairs)
                    last.then_inc(qkv_ready, 1)

            def scores(g, u):
                bp, h, b = unit(u)
                pe.wait_ge(qkv_lo, g * (PAIRS * JOBS) + bp * JOBS + 2 * h + 2)
                wait(pe, s_masked, g * UNITS + max(u - 1, 0))
                for i in range(2):
                    s = slice(b * SEQ + i * P, b * SEQ + (i + 1) * P)
                    m = slice(b * SEQ, b * SEQ + (i + 1) * P)
                    q, k = (qT_hi, qT_lo), (kT_hi, kT_lo)
                    last = chain(psum[:, S_BANK + u % 2, i * P:(2 * i + 1) * P], passes(
                        *(t[:, bp % 2, h, s] for t in q), *(t[:, bp % 2, h, m] for t in k)))
                last.then_inc(s_ready, 1)

            def transposes(g, u):
                pe.wait_ge(p_scaled, g * UNITS + u + 1)
                wait(pe, pT_lo_ready, g * UNITS + u)
                for i in range(3):
                    last = pe.transpose(psum[:, PT_BANK, i * P:(i + 1) * P], p_sb[:, u % 3, i * P:(i + 1) * P], ident[:])
                last.then_inc(pT_ready, 1)

            def values(g, u):
                bp, h, b = unit(u)
                pe.wait_ge(pT_lo_ready, g * UNITS + u + 1)
                pe.wait_ge(qkv_lo, g * (PAIRS * JOBS) + (bp + 1) * JOBS)
                wait(pe, z_lo_ready, g * UNITS + u)
                for i in range(2):
                    v = [t[:, bp % 2, b, i * HG * DH + h * DH:i * HG * DH + (h + 1) * DH] for t in (v_hi, v_lo)]
                    p = [t[:, u % 2, 2 * i * P:(2 + i) * P] for t in (pT_hi, pT_lo)]
                    last = chain(psum[:, Z_BANK, i * P:2 * P], passes(*v, *p), start=i == 0, stop=i == 1, skip_group_check=True)
                last.then_inc(z_ready, 1)

            def output(g, u):
                bp, h, b = unit(u)
                pe.wait_ge(z_lo_ready, g * UNITS + u + 1)
                if h == 0:
                    if u == 0:
                        pe.wait_ge(aw_split, 4 * g + 4)
                    wait(pe, o_added, g * (2 * PAIRS) + max(2 * bp + b - 1, 0))
                w = slice(WO + h * D, WO + (h + 1) * D)
                for i in range(2):
                    z = [t[:, u % 2, i * P:(i + 1) * P] for t in (zT_hi, zT_lo)]
                    last = chain(psum[:, O_BANK + b, i * D:(i + 1) * D], passes(*z, aw_hi[:, w], aw_lo[:, w]),
                                 start=h == 0 and i == 0, stop=h == HG - 1, skip_group_check=True)
                if h == HG - 1:
                    last.then_inc(o_ready, 1)

            def group(g, next_group, hooks={}):
                for i, jobs, more_jobs, u_s, u_t, u_v, u_o in attn_schedule(next_group):
                    if u_s is not None:
                        scores(g, u_s)
                    for bp, j in jobs:
                        qkv_job(g, bp, j)
                    if u_t is not None:
                        transposes(g, u_t)
                    if u_v is not None:
                        values(g, u_v)
                    for bp, j in more_jobs:
                        qkv_job(g, bp, j)
                    if u_o is not None:
                        output(g, u_o)
                    if i in hooks:
                        hooks[i]()

            def first_turns(quad):
                if quad == 0:
                    pe.wait_ge(qkv_lo, GROUPS * PAIRS * JOBS)
                else:
                    pe.wait_ge(s_masked, GROUPS * UNITS)
                ln_turns(0, quad, FIRST_NORM_BANKS)

            last_hooks = {14: lambda: first_turns(0), 16: lambda: first_turns(1), 18: lambda: gate_logits(expert_layers[0], 0, FIRST_GATE_BANKS),
                          19: lambda: gate_logits_turn(expert_layers[0], 0, FIRST_GATE_BANKS)}

            for j in range(JOBS):
                qkv_job(0, 0, j)
            pe.wait_ge(const_ready, 4)
            group(0, True)
            with pe.Fori(1, GROUPS - 1) as g:
                group(g, True)
            group(GROUPS - 1, False, last_hooks)
            l0, l1 = expert_layers

            def second_norm(f):
                pe.wait_ge(o_added, GROUPS * 2 * PAIRS)
                gate_turns(f, 0, FIRST_TURN_BANKS)
                ln_turns(2 * f["norm"] + 1, 0, NORM_BANKS)
                pe.wait_ge(f["combT_copied"], 4 * f["layer"] + 2)
                ln_turns(2 * f["norm"] + 1, 1, NORM_BANKS)
                gate_logits(f, 1, GATE_BANKS)
                gate_logits_turn(f, 1, GATE_BANKS)

            experts_tensor(l0, {}, lambda: second_norm(l0), True)
            def turns(u, quad):
                return lambda: ln_turns(u, quad, HT_BANKS)

            hooks = {2: turns(3, 0), 4: turns(3, 1)}
            def next_turns():
                pe.wait_ge(m["out_added"], 12)
                ln_turns(4, 0, HT_BANKS)

            def next_logits():
                for i, read in enumerate(bank_read):
                    pe.wait_ge(read, (PROJECTIONS - i + 2) // 3)
                gate_logits(l1, 0, SSM_GATE_BANKS)

            hooks.update({30: next_turns, 31: turns(4, 1), 32: next_logits, 33: lambda: gate_logits_turn(l1, 0, SSM_GATE_BANKS)})
            ssm_tensor(hooks)
            experts_tensor(l1, {}, lambda: second_norm(l1), False)


def lay_out(inputs):
    import numpy as np

    a = {n: np.asarray(v) for n, v in inputs.items()}
    x = a["L0_attn_x"].reshape(T, D)
    def heads(w):
        return w.reshape(GROUPS, HG, DH, DC, P).transpose(0, 4, 1, 3, 2)
    q, k = (heads(a[f"L0_attn_W_{n}"]).reshape(GROUPS, P, -1) for n in "QK")
    v = heads(a["L0_attn_W_V"]).transpose(0, 1, 3, 2, 4).reshape(GROUPS, P, -1)
    o = a["L0_attn_W_O"].reshape(GROUPS, HG, D, DH).transpose(0, 3, 1, 2).reshape(GROUPS, P, -1)
    attn_w = np.concatenate([q, k, v, o], axis=2)

    def hidden_tiles(gate, up, down, layer):
        n = layer["tiles"]
        pad = n * P - layer["hidden"]
        gate, up = (np.pad(w, ((0, 0), (0, pad))).reshape(DC, P, n, P).transpose(2, 1, 0, 3).reshape(n, P, DC * P) for w in (gate, up))
        down = np.pad(down, ((0, pad), (0, 0))).reshape(n, P, D)
        return np.concatenate([gate, up, down], axis=2)

    def cols(w):
        return w.transpose(1, 0, 2).reshape(D, -1)

    l0_w = hidden_tiles(np.concatenate([a["L0_ffn_sg"], cols(a["L0_ffn_wg"])], 1),
                        np.concatenate([a["L0_ffn_su"], cols(a["L0_ffn_wu"])], 1),
                        np.concatenate([a["L0_ffn_sd"], a["L0_ffn_wd"].reshape(-1, D)], 0), L0)
    up = a["L1_ffn_expert_up_w"].transpose(0, 2, 1)
    sh = a["L1_ffn_shared_up_w"].T
    w, s = L1["width"], L1["shared"]
    l1_w = hidden_tiles(np.concatenate([sh[:, :s], cols(up[:, :, :w])], 1),
                        np.concatenate([sh[:, s:], cols(up[:, :, w:])], 1),
                        np.concatenate([a["L1_ffn_shared_down_w"].T, a["L1_ffn_expert_down_w"].transpose(0, 2, 1).reshape(-1, D)], 0), L1)
    rows = lambda w: w.reshape(DC, P, -1).transpose(1, 0, 2)

    pw = a["L1_attn_in_proj_w"]
    def tile(w, n):
        return np.pad(w, ((0, n * P - w.shape[0]),) + ((0, 0),) * (w.ndim - 1))
    cut = [E, 2 * E, 2 * E + NS, 2 * E + 2 * NS]
    g_, h_, b_, c_, d_ = np.split(pw, cut)
    in_w = np.concatenate([g_, h_, tile(b_, 1), tile(c_, 1), tile(d_, 1)])
    in_w = rows(np.ascontiguousarray(in_w.T))
    conv = np.concatenate([a["L1_attn_conv_w"], a["L1_attn_conv_b"][:, None]], 1)
    h_, b_, c_ = np.split(conv, [E, E + NS])
    conv = np.concatenate([h_, tile(b_, 1), tile(c_, 1)]).reshape(CJ, P, TAPS + 1).transpose(1, 0, 2).reshape(P, -1)
    per = lambda v: np.ascontiguousarray(v.reshape(EJ, P).T)
    ssm_cols = np.concatenate([conv, per(np.repeat(a["L1_attn_D"], HP)), per(a["L1_attn_norm_w"]),
                               tile(a["L1_attn_dt_bias"][:, None], 1), tile(a["L1_attn_A_log"][:, None], 1)], 1)
    out_w = a["L1_attn_out_proj_w"].T.reshape(EJ, P, D).transpose(1, 0, 2)
    out = dict(x_rows=x, x_cols=x.T, attn_w=attn_w, l0_gate=rows(a["L0_ffn_gate_w"]), l0_w=l0_w,
               l1_gate=rows(a["L1_ffn_gate_w"].T), l1_w=l1_w, in_w=in_w, ssm_cols=ssm_cols, out_w=out_w)
    return {n: np.ascontiguousarray(v) for n, v in out.items()}


def kernel(**inputs):
    import concourse.bacc as bacc
    from concourse.bass_utils import run_bass_kernel_spmd

    nc = bacc.Bacc("TRN2", target_bir_lowering=False, num_devices=1)
    arrays = lay_out(inputs)
    aps = {n: nc.dram_tensor(n, v.shape, mybir.dt.from_np(v.dtype), kind="ExternalInput").ap() for n, v in arrays.items()}
    out = nc.dram_tensor("out", (T, D), F32, kind="ExternalOutput").ap()
    program(nc, **aps, out=out)
    result = run_bass_kernel_spmd(nc, [arrays], core_ids=[0])
    return result.results[0]["out"].reshape(BATCH, SEQ, D)
```
